# Optimizing a Trainium2 kernel written in Bass

```python
import numpy as np
import jax
import jax.numpy as jnp

def _softmax(x, axis=-1):
    return jax.nn.softmax(x, axis=axis)

def _gelu(x):
    return jax.nn.gelu(x, approximate=True)

def _silu(x):
    return jax.nn.silu(x)

def _sigmoid(x):
    return jax.nn.sigmoid(x)

def _layernorm(x, axis=-1, eps=1e-05):
    m = jnp.mean(x, axis=axis, keepdims=True)
    v = jnp.var(x, axis=axis, keepdims=True)
    return (x - m) / jnp.sqrt(v + eps)

def _scatter_add(tgt, idx, src, axis=0):
    return tgt.at[idx].add(src)

def _segment_sum(src, seg, n):
    return jax.ops.segment_sum(src, seg, n)
kernel_name = 'mk_perceiver_d1_seqx_r2_d00bf1'

def setup_inputs(seed: int=0):
    np.random.seed(seed)
    _w = jnp.asarray

    def _rec_inputs():
        import jax
        import jax.numpy as jnp
        _rk = jax.random.key(seed)
        x = 7.22e-05 + 1 * jax.random.normal(jax.random.fold_in(_rk, 1), (1, 512, 512), jnp.float32)
        _lenS = 512 - jax.random.randint(jax.random.fold_in(_rk, 7), (1,), 0, max(1, 512 // 4) + 1, jnp.int32)
        _lenS2 = 8192 - jax.random.randint(jax.random.fold_in(_rk, 8), (1,), 0, max(1, 8192 // 4) + 1, jnp.int32)
        _ctx_1024P = jax.random.normal(jax.random.fold_in(_rk, 11), (1, 16, 512), jnp.float32)
        _ctx_1024c = jax.random.dirichlet(jax.random.fold_in(_rk, 511), 0.3 * jnp.ones((16,), jnp.float32), (1, 8192))
        _ctx_1024t = jnp.einsum('bsk,bkd->bsd', _ctx_1024c, _ctx_1024P)
        _ctx_1024t = _ctx_1024t * jax.lax.rsqrt(jnp.mean(jnp.square(_ctx_1024t)) + 1e-12) * 0.953939
        ctx_1024 = 4.13588e-05 + 0.999923 * (_ctx_1024t + 0.3 * jax.random.normal(jax.random.fold_in(_rk, 611), (1, 8192, 512), jnp.float32))
        return (x, ctx_1024)
    x, ctx_1024 = _rec_inputs()

    def _L0_xattn_setup():
        import jax, jax.numpy as jnp
        import numpy as np
        EMBED_DIM = 512
        NUM_HEADS = 16
        HEAD_DIM = EMBED_DIM // NUM_HEADS
        B, N, M = (4, 1024, 1024)

        def _split_heads(x):
            b, t, _ = x.shape
            return x.reshape(b, t, NUM_HEADS, HEAD_DIM).transpose(0, 2, 1, 3)
        key = jax.random.key(seed)
        ks = jax.random.split(key, 10)
        s = 1.0 / np.sqrt(EMBED_DIM)
        return {'query_modal': jax.random.normal(ks[0], (B, N, EMBED_DIM), jnp.float32), 'key_value_modal': jax.random.normal(ks[1], (B, M, EMBED_DIM), jnp.float32), 'Wq': jax.random.normal(ks[2], (EMBED_DIM, EMBED_DIM), jnp.float32) * s, 'bq': jnp.zeros((EMBED_DIM,), jnp.float32), 'Wk': jax.random.normal(ks[3], (EMBED_DIM, EMBED_DIM), jnp.float32) * s, 'bk': jnp.zeros((EMBED_DIM,), jnp.float32), 'Wv': jax.random.normal(ks[4], (EMBED_DIM, EMBED_DIM), jnp.float32) * s, 'bv': jnp.zeros((EMBED_DIM,), jnp.float32), 'Wo': jax.random.normal(ks[5], (EMBED_DIM, EMBED_DIM), jnp.float32) * s, 'bo': jnp.zeros((EMBED_DIM,), jnp.float32)}
    _L0_xattn_all = _L0_xattn_setup()
    _L0_xattn_in = {k: v for k, v in _L0_xattn_all.items() if k in ('Wq', 'bq', 'Wk', 'bk', 'Wv', 'bv', 'Wo', 'bo')}
    del _L0_xattn_all

    def _L0_attn_setup():
        import jax, jax.numpy as jnp
        import numpy as np
        NUM_HEADS = 16
        TOP_K = 128
        LN_EPS = 1e-05

        def layernorm(x, w, b):
            mu = jnp.mean(x, axis=-1, keepdims=True)
            var = jnp.mean((x - mu) ** 2, axis=-1, keepdims=True)
            return (x - mu) * jax.lax.rsqrt(var + LN_EPS) * w + b

        def top_k_activation(x, k):
            n = x.shape[-1]
            if k >= n:
                return x
            vals, idx = jax.lax.top_k(x, k)
            flat = x.reshape(-1, n)
            rows = jnp.arange(flat.shape[0])[:, None]
            out = jnp.zeros_like(flat).at[rows, idx.reshape(-1, k)].set(vals.reshape(-1, k))
            return out.reshape(x.shape)
        key = jax.random.key(seed)
        ks = jax.random.split(key, 8)
        B, S, H = (2, 1024, 512)
        hd = H // NUM_HEADS
        return {'x': jax.random.normal(ks[0], (B, S, H), dtype=jnp.float32), 'W_Q': jax.random.normal(ks[1], (H, H), dtype=jnp.float32) * 0.02, 'W_K': jax.random.normal(ks[2], (H, H), dtype=jnp.float32) * 0.02, 'W_V': jax.random.normal(ks[3], (H, H), dtype=jnp.float32) * 0.02, 'W_O': jax.random.normal(ks[4], (H, H), dtype=jnp.float32) * 0.02, 'q_ln_w': jnp.ones((hd,), dtype=jnp.float32), 'q_ln_b': jnp.zeros((hd,), dtype=jnp.float32), 'k_ln_w': jnp.ones((hd,), dtype=jnp.float32), 'k_ln_b': jnp.zeros((hd,), dtype=jnp.float32), 'sparse_W_V': jax.random.normal(ks[5], (NUM_HEADS, hd, TOP_K), dtype=jnp.float32) * 0.02, 'sparse_W_O': jax.random.normal(ks[6], (NUM_HEADS, TOP_K, hd), dtype=jnp.float32) * 0.02}
    _L0_attn_all = _L0_attn_setup()
    _L0_attn_in = {k: v for k, v in _L0_attn_all.items() if k in ('W_Q', 'W_K', 'W_V', 'W_O', 'q_ln_w', 'q_ln_b', 'k_ln_w', 'k_ln_b', 'sparse_W_V', 'sparse_W_O')}
    del _L0_attn_all

    def _L0_ffn_setup():
        import jax, jax.numpy as jnp
        import numpy as np
        E = 8
        D = 512
        H = 1024
        TOP_K = 2
        key = jax.random.key(seed)
        k_x, k_g, k_w1, k_w2 = jax.random.split(key, 4)
        B, S = (4, 1024)
        inp = {'input': jax.random.normal(k_x, (B, S, D), dtype=jnp.float32), 'Wg': jax.random.normal(k_g, (D, E), dtype=jnp.float32) * 0.02, 'W1': jax.random.normal(k_w1, (E, D, H), dtype=jnp.float32) * 0.02, 'b1': jnp.zeros((E, H), dtype=jnp.float32), 'W2': jax.random.normal(k_w2, (E, H, D), dtype=jnp.float32) * 0.02, 'b2': jnp.zeros((E, D), dtype=jnp.float32)}
        return inp
    _L0_ffn_all = _L0_ffn_setup()
    _L0_ffn_in = {k: v for k, v in _L0_ffn_all.items() if k in ('Wg', 'W1', 'b1', 'W2', 'b2')}
    del _L0_ffn_all
    return {'x': x, 'ctx_1024': ctx_1024, 'L0_xattn_Wq': _L0_xattn_in['Wq'], 'L0_xattn_bq': _L0_xattn_in['bq'], 'L0_xattn_Wk': _L0_xattn_in['Wk'], 'L0_xattn_bk': _L0_xattn_in['bk'], 'L0_xattn_Wv': _L0_xattn_in['Wv'], 'L0_xattn_bv': _L0_xattn_in['bv'], 'L0_xattn_Wo': _L0_xattn_in['Wo'], 'L0_xattn_bo': _L0_xattn_in['bo'], 'L0_attn_W_Q': _L0_attn_in['W_Q'], 'L0_attn_W_K': _L0_attn_in['W_K'], 'L0_attn_W_V': _L0_attn_in['W_V'], 'L0_attn_W_O': _L0_attn_in['W_O'], 'L0_attn_q_ln_w': _L0_attn_in['q_ln_w'], 'L0_attn_q_ln_b': _L0_attn_in['q_ln_b'], 'L0_attn_k_ln_w': _L0_attn_in['k_ln_w'], 'L0_attn_k_ln_b': _L0_attn_in['k_ln_b'], 'L0_attn_sparse_W_V': _L0_attn_in['sparse_W_V'], 'L0_attn_sparse_W_O': _L0_attn_in['sparse_W_O'], 'L0_ffn_Wg': _L0_ffn_in['Wg'], 'L0_ffn_W1': _L0_ffn_in['W1'], 'L0_ffn_b1': _L0_ffn_in['b1'], 'L0_ffn_W2': _L0_ffn_in['W2'], 'L0_ffn_b2': _L0_ffn_in['b2']}

def reference(x, ctx_1024, L0_xattn_Wq, L0_xattn_bq, L0_xattn_Wk, L0_xattn_bk, L0_xattn_Wv, L0_xattn_bv, L0_xattn_Wo, L0_xattn_bo, L0_attn_W_Q, L0_attn_W_K, L0_attn_W_V, L0_attn_W_O, L0_attn_q_ln_w, L0_attn_q_ln_b, L0_attn_k_ln_w, L0_attn_k_ln_b, L0_attn_sparse_W_V, L0_attn_sparse_W_O, L0_ffn_Wg, L0_ffn_W1, L0_ffn_b1, L0_ffn_W2, L0_ffn_b2):
    import jax
    import jax.numpy as jnp

    def _L0_xattn_ref(query_modal, key_value_modal, Wq, bq, Wk, bk, Wv, bv, Wo, bo):
        import jax, jax.numpy as jnp
        import numpy as np
        EMBED_DIM = 512
        NUM_HEADS = 16
        HEAD_DIM = EMBED_DIM // NUM_HEADS
        B, N, M = (4, 1024, 1024)

        def _split_heads(x):
            b, t, _ = x.shape
            return x.reshape(b, t, NUM_HEADS, HEAD_DIM).transpose(0, 2, 1, 3)
        q = _split_heads(query_modal @ Wq.T + bq)
        k = _split_heads(key_value_modal @ Wk.T + bk)
        v = _split_heads(key_value_modal @ Wv.T + bv)
        scale = HEAD_DIM ** (-0.5)
        scores = jnp.einsum('bhnd,bhmd->bhnm', q, k) * scale
        attn = jax.nn.softmax(scores, axis=-1)
        x = jnp.einsum('bhnm,bhmd->bhnd', attn, v)
        x = x.transpose(0, 2, 1, 3).reshape(query_modal.shape)
        return x @ Wo.T + bo

    def _L0_attn_ref(x, W_Q, W_K, W_V, W_O, q_ln_w, q_ln_b, k_ln_w, k_ln_b, sparse_W_V, sparse_W_O):
        import jax, jax.numpy as jnp
        import numpy as np
        NUM_HEADS = 16
        TOP_K = 128
        LN_EPS = 1e-05

        def layernorm(x, w, b):
            mu = jnp.mean(x, axis=-1, keepdims=True)
            var = jnp.mean((x - mu) ** 2, axis=-1, keepdims=True)
            return (x - mu) * jax.lax.rsqrt(var + LN_EPS) * w + b

        def top_k_activation(x, k):
            n = x.shape[-1]
            if k >= n:
                return x
            vals, idx = jax.lax.top_k(x, k)
            flat = x.reshape(-1, n)
            rows = jnp.arange(flat.shape[0])[:, None]
            out = jnp.zeros_like(flat).at[rows, idx.reshape(-1, k)].set(vals.reshape(-1, k))
            return out.reshape(x.shape)
        B, S, H = x.shape
        nh = sparse_W_V.shape[0]
        hd = H // nh

        def split_heads(t):
            return t.reshape(B, S, nh, hd).transpose(0, 2, 1, 3)
        Q = split_heads(jnp.einsum('bsd,od->bso', x, W_Q))
        K = split_heads(jnp.einsum('bsd,od->bso', x, W_K))
        V = split_heads(jnp.einsum('bsd,od->bso', x, W_V))
        Q = layernorm(Q, q_ln_w, q_ln_b)
        K = layernorm(K, k_ln_w, k_ln_b)
        scores = jnp.einsum('bhqd,bhkd->bhqk', Q, K) / jnp.sqrt(jnp.float32(hd))
        attn = jax.nn.softmax(scores, axis=-1)
        context = jnp.einsum('bhqk,bhkd->bhqd', attn, V)
        context_flat = context.transpose(0, 2, 1, 3).reshape(B * nh, S, hd)
        v_weights = sparse_W_V.mean(axis=2)
        z = jnp.einsum('bnd,hd->bhn', context_flat, v_weights)
        z_sparse = top_k_activation(z, TOP_K)
        o_weights = sparse_W_O.mean(axis=1)
        y_flat = jnp.einsum('bhn,hd->bnd', z_sparse, o_weights)
        y = y_flat.reshape(B, nh, S, hd).transpose(0, 2, 1, 3).reshape(B, S, H)
        y = jnp.einsum('bsd,od->bso', y, W_O)
        return y

    def _L0_ffn_ref(input, Wg, W1, b1, W2, b2):
        import jax, jax.numpy as jnp
        import numpy as np
        E = 8
        D = 512
        H = 1024
        TOP_K = 2
        logits = jnp.einsum('bsd,de->bse', input, Wg)
        probs = jax.nn.softmax(logits, axis=-1)
        top_vals, top_idx = jax.lax.top_k(probs, TOP_K)
        top_vals = top_vals / jnp.sum(top_vals, axis=-1, keepdims=True)
        onehot = jax.nn.one_hot(top_idx, E, dtype=input.dtype)
        mask = jnp.sum(onehot, axis=2)
        scores = jnp.sum(onehot * top_vals[..., None], axis=2)
        xm = input[None] * jnp.moveaxis(mask, -1, 0)[..., None]
        h = jnp.einsum('ebsd,edh->ebsh', xm, W1) + b1[:, None, None, :]
        h = jax.nn.relu(h)
        y = jnp.einsum('ebsh,ehd->ebsd', h, W2) + b2[:, None, None, :]
        out = jnp.sum(y * jnp.moveaxis(scores, -1, 0)[..., None], axis=0)
        return out
    x = x + _L0_xattn_ref(_layernorm(x, axis=-1), ctx_1024, L0_xattn_Wq, L0_xattn_bq, L0_xattn_Wk, L0_xattn_bk, L0_xattn_Wv, L0_xattn_bv, L0_xattn_Wo, L0_xattn_bo)
    x = x + _L0_attn_ref(_layernorm(x, axis=-1), L0_attn_W_Q, L0_attn_W_K, L0_attn_W_V, L0_attn_W_O, L0_attn_q_ln_w, L0_attn_q_ln_b, L0_attn_k_ln_w, L0_attn_k_ln_b, L0_attn_sparse_W_V, L0_attn_sparse_W_O)
    x = x + _L0_ffn_ref(_layernorm(x, axis=-1), L0_ffn_Wg, L0_ffn_W1, L0_ffn_b1, L0_ffn_W2, L0_ffn_b2)
    return x

_drawn_inputs = setup_inputs


def setup_inputs(seed=0):
    import zlib

    import numpy as np

    out = dict(_drawn_inputs(seed))
    spreads = {'L0_xattn_bq': (0.0, 0.344),
     'L0_xattn_bk': (0.0, 2.0),
     'L0_xattn_bv': (0.0, 0.1),
     'L0_xattn_bo': (0.0, 0.1),
     'L0_attn_q_ln_w': (1.0, 0.6),
     'L0_attn_q_ln_b': (0.0, 2.0),
     'L0_attn_k_ln_w': (1.0, 0.6),
     'L0_attn_k_ln_b': (0.0, 2.0),
     'L0_ffn_b1': (0.0, 0.29),
     'L0_ffn_b2': (0.0, 0.1)}
    factors = {'L0_attn_W_Q': 44.927,
     'L0_attn_W_K': 40.601,
     'L0_attn_W_V': 23.114,
     'L0_attn_W_O': 8.0,
     'L0_attn_sparse_W_V': 8.0,
     'L0_attn_sparse_W_O': 8.0}
    for name, (base, spread) in spreads.items():
        noise = np.random.default_rng([zlib.crc32(name.encode()), seed]).standard_normal(out[name].shape)
        drawn = base * np.exp(spread * noise) if base else spread * noise
        out[name] = jnp.asarray(drawn.astype(out[name].dtype))
    for name, factor in factors.items():
        out[name] = (out[name] * factor).astype(out[name].dtype)
    return out
```

```python
from contextlib import ExitStack

import concourse.bass as bass
from concourse import mybir

F32 = mybir.dt.float32
F32R = mybir.dt.float32r
BF16 = mybir.dt.bfloat16
U32 = mybir.dt.uint32
ALU = mybir.AluOpType
ACT = mybir.ActivationFunctionType
AX = mybir.AxisListType

P = 128
D = 512
DC = D // P
N = 512
NT = N // P
M = 8192
CH = 512
NCH = M // CH
KT = CH // P
H = 16
HD = D // H
HG = P // HD
G = H // HG
SCALE = HD ** -0.5
EPS = 1e-5
KEEP = 128
TOPM = 128
E = 8
FF = 1024
FC = FF // P
NEG = -3.0e38
STK = 3 * HD
MROW = STK


class Ctx:
    pass


def f32(ap):
    return ap.bitcast(F32)


def allocators(nc, stack, tag):
    def sb(name, shape, dt=F32):
        return stack.enter_context(nc.sbuf_tensor(f"{tag}_{name}", shape, dt))

    def pb(name, shape, dt=F32):
        return stack.enter_context(nc.psum_tensor(f"{tag}_{name}", shape, dt))

    def sem(name):
        return stack.enter_context(nc.semaphore(f"{tag}_{name}"))

    return sb, pb, sem


def split_product(pe, out, a, b, last=True, first=True):
    n = len(a)
    for i in range(n):
        (ah, al), (bh, bl) = a[i], b[i]
        pe.matmul(out, ah, bh, start=(first and i == 0), stop=False)
        pe.matmul(out, ah, bl, start=False, stop=False)
        mm = pe.matmul(out, al, bh, start=False, stop=(last and i == n - 1))
    return mm


def prepare(nc, c):
    with ExitStack() as stack:
        sb, pb, sem = allocators(nc, stack, "prep")
        w_raw = {n: sb(f"{n}_raw", [P, DC, D]) for n in ("wq", "wk", "wv")}
        stats = sb("stats", [P, NT, 6])
        mv = sb("mv", [P, NT, 2])
        std = sb("std", [P, NT])
        rstd = sb("rstd", [P, NT])
        h = sb("h", [P, NT, D])
        hT = sb("hT", [P, DC, N])
        tp = [pb(f"tp{i}", [P, N]) for i in range(DC)]
        qp = [pb(f"qp{i}", [P, N]) for i in range(G)]
        x_in, w_in, wkv_in, rest_in = sem("x_in"), sem("w_in"), sem("wkv_in"), sem("rest_in")
        s_const, s_ident = sem("const"), sem("ident")
        s_stats, s_var, s_std, s_rstd, s_h = sem("stats"), sem("var"), sem("std"), sem("rstd"), sem("h")
        s_tp, s_hT, s_q, s_qT, s_mask, s_whi, s_wlo = (
            sem(n) for n in ("tp", "hT", "q", "qT", "mask", "whi", "wlo"))
        block = stack.enter_context(nc.Block())

        @block.sync
        def _(sp):
            sp.dma_start(c.x[:, :, :], c.dram["x"].rearrange("(t p) d -> p t d", p=P)).then_inc(x_in, 16)
            sp.dma_start(w_raw["wq"][:, :, :], c.dram["WqT"].rearrange("(k p) o -> p k o", p=P)).then_inc(w_in, 16)
            sp.dma_start(w_raw["wk"][:, :, :], c.dram["WkT"].rearrange("(k p) o -> p k o", p=P)).then_inc(wkv_in, 16)
            sp.dma_start(w_raw["wv"][:, :, :], c.dram["WvT"].rearrange("(k p) o -> p k o", p=P)).then_inc(wkv_in, 16)
            sp.dma_start(c.woT[:, :, :], c.dram["WoT"].rearrange("(k p) o -> p k o", p=P)).then_inc(rest_in, 16)
            sp.wait_ge(rest_in, 64)

        @block.gpsimd
        def _(pool):
            pool.memset(c.ident[:, :], 0.0).then_inc(s_ident, 1)
            pool.memset(f32(c.qmask[:, :, :]), 0.0).then_inc(s_const, 1)
            pool.wait_ge(s_ident, 1)
            pool.affine_select(out=c.ident[:, :], in_=c.ident[:, :], compare_op=ALU.not_equal, fill=1.0,
                               base=0, pattern=[[-1, P]], channel_multiplier=1).then_inc(s_ident, 1)
            pool.wait_ge(wkv_in, 32)
            for n, (raw, hi, lo) in enumerate(((w_raw["wk"], c.wk_hi, c.wk_lo), (w_raw["wv"], c.wv_hi, c.wv_lo))):
                pool.wait_ge(s_whi, n + 1)
                pool.tensor_tensor(lo[:, :, :], raw[:, :, :], f32(hi[:, :, :]), ALU.subtract).then_inc(s_wlo, 1)

        @block.scalar
        def _(act):
            act.dma_start(c.bq[:, :], c.dram["bq"]).then_inc(rest_in, 16)
            act.dma_start(c.bk[:, :], c.dram["bk"]).then_inc(rest_in, 16)
            act.dma_start(c.bv[:, :], c.dram["bv"]).then_inc(rest_in, 16)
            act.wait_ge(s_var, 1)
            act.activation(std[:, :], std[:, :], ACT.Sqrt).then_inc(s_std, 1)
            act.wait_ge(wkv_in, 32)
            act.activation(c.wk_hi[:, :, :], w_raw["wk"][:, :, :], ACT.Copy).then_inc(s_whi, 1)
            act.activation(c.wv_hi[:, :, :], w_raw["wv"][:, :, :], ACT.Copy).then_inc(s_whi, 1)
            for k in range(DC):
                act.wait_ge(s_tp, k + 1)
                act.activation(hT[:, k, :], tp[k][:, :], ACT.Copy).then_inc(s_hT, 1)
            act.wait_ge(rest_in, 64)
            for g in range(G):
                act.wait_ge(s_q, g + 1)
                act.activation(c.qT[:, g, :], qp[g][:, :], ACT.Identity, bias=c.bq[:, g:g + 1]).then_inc(s_qT, 1)

        @block.vector
        def _(dve):
            dve.wait_ge(x_in, 16)
            layer_norm(dve, c.x, h, stats, mv, std, rstd, s_stats, s_var, s_std, s_rstd, s_h)
            dve.wait_ge(s_const, 1)
            dve.wait_ge(s_qT, G)
            for j in range(HG):
                rows = slice(HD * j, HD * j + HD)
                dve.tensor_copy(c.qmask[rows, j::HG, :], c.qT[rows, :, :]).then_inc(s_mask, 1)

        @block.tensor
        def _(pe):
            pe.wait_ge(s_ident, 2)
            pe.wait_ge(s_h, NT)
            for k in range(DC):
                for t in range(NT):
                    mm = pe.transpose(tp[k][:, t * P:(t + 1) * P], h[:, t, k * P:(k + 1) * P], c.ident[:, :])
                mm.then_inc(s_tp, 1)
            pe.wait_ge(w_in, 16)
            pe.wait_ge(s_hT, DC)
            for g in range(G):
                for k in range(DC):
                    mm = pe.matmul(qp[g][:, :], w_raw["wq"][:, k, g * P:(g + 1) * P], hT[:, k, :],
                                   start=(k == 0), stop=(k == DC - 1))
                mm.then_inc(s_q, 1)


def layer_norm(dve, x, h, stats, mv, std, rstd, s_stats, s_var, s_std, s_rstd, s_h):
    for t in range(NT):
        dve.bn_stats(stats[:, t, :], x[:, t, :]).then_inc(s_stats, 1)
    for t in range(NT):
        dve.wait_ge(s_stats, t + 1)
        dve.bn_aggr(mv[:, t, :], stats[:, t, :]).then_inc(s_stats, 1)
    dve.wait_ge(s_stats, 2 * NT)
    dve.tensor_scalar(std[:, :], mv[:, :, 1], EPS, None, ALU.add).then_inc(s_var, 1)
    dve.wait_ge(s_std, 1)
    dve.reciprocal(rstd[:, :], std[:, :]).then_inc(s_rstd, 1)
    dve.wait_ge(s_rstd, 1)
    for t in range(NT):
        dve.tensor_scalar(h[:, t, :], x[:, t, :], mv[:, t, 0:1], rstd[:, t:t + 1],
                          ALU.subtract, ALU.mult).then_inc(s_h, 1)


def project_context(nc, c):
    PRIME_LO, PRIME_V, PRIME_EV, PRIME_OUT, PRIME_ST, PRIME_CP, PRIME_R, PRIME_M = 1, 8, 4, 16, 1, 1, 18, 1
    PAIRS = 2
    with ExitStack() as stack:
        sb, pb, sem = allocators(nc, stack, "ctx")
        raw = sb("raw", [P, DC, CH])
        hi = [sb(f"hi{b}", [P, DC, CH], F32R) for b in range(2)]
        lo = [sb(f"lo{b}", [P, DC, CH], F32R) for b in range(2)]
        k_hi = [sb(f"k_hi{b}", [P, G, CH], F32R) for b in range(2)]
        k_lo = sb("k_lo", [P, G, CH], F32R)
        v = sb("v", [P, G, KT, P])
        run = sb("run", [P, H, 2 * CH], BF16)
        half = sb("half", [P, 2, 2 * CH], BF16)
        st = sb("st", [P, H, 2])
        best = sb("best", [P, H, 2])
        proj = [pb(f"proj{i}", [P, CH]) for i in range(4)]
        sc = [pb(f"sc{i}", [P, 2 * CH]) for i in range(2)]
        ctx_in, s_turn, s_hi, s_lo = sem("ctx_in"), sem("turn"), sem("hi"), sem("lo")
        k_proj, v_proj, k_hi_done, k_lo_done, v_done = (
            sem(n) for n in ("k_proj", "v_proj", "k_hi_done", "k_lo_done", "v_done"))
        k_hi_out = [sem(f"k_hi_out{b}") for b in range(2)]
        k_lo_out, v_out = sem("k_lo_out"), sem("v_out")
        sc_ready = [sem(f"sc_ready{i}") for i in range(2)]
        s_st, s_copied, s_run, s_best = sem("st"), sem("copied"), sem("run"), sem("best")
        s_tree, s_neg, s_neg_hi = sem("tree"), sem("neg"), sem("neg_hi")
        block = stack.enter_context(nc.Block())

        @block.sync
        def _(sp):
            sp.sem_inc(k_hi_out[0], PRIME_OUT)
            sp.sem_inc(k_hi_out[1], PRIME_OUT)
            sp.sem_inc(k_lo_out, PRIME_OUT)
            sp.sem_inc(v_out, PRIME_OUT)

            def load(n):
                sp.wait_ge(s_lo, n + PRIME_LO)
                sp.dma_start(raw[:, :, :], c.dram["ctx"][n]).then_inc(ctx_in, 16)

            def store(n, b):
                sp.wait_ge(k_hi_done, G * n + G)
                sp.dma_start(c.k_dram[n, :, 0].rearrange("g p k -> p g k"), f32(k_hi[b][:, :, :])).then_inc(k_hi_out[b], 16)
                sp.wait_ge(k_lo_done, G * n + G)
                sp.dma_start(c.k_dram[n, :, 1].rearrange("g p k -> p g k"), f32(k_lo[:, :, :])).then_inc(k_lo_out, 16)
                sp.wait_ge(v_done, KT * n + KT + PRIME_EV)
                sp.dma_start(c.v_dram[n].rearrange("g p t d -> p g t d"), v[:, :, :, :]).then_inc(v_out, 16)

            load(0)
            with sp.Fori(0, NCH // 2 - 1) as i:
                for b in range(2):
                    load(2 * i + b + 1)
                    store(2 * i + b, b)
            load(NCH - 1)
            store(NCH - 2, 0)
            store(NCH - 1, 1)
            sp.wait_ge(k_hi_out[0], 16 * (NCH // 2) + PRIME_OUT)
            sp.wait_ge(k_hi_out[1], 16 * (NCH // 2) + PRIME_OUT)
            sp.wait_ge(k_lo_out, 16 * NCH + PRIME_OUT)
            sp.wait_ge(v_out, 16 * NCH + PRIME_OUT)

        @block.gpsimd
        def _(pool):
            pool.sem_inc(s_lo, PRIME_LO)
            with pool.Fori(0, NCH // 2) as i:
                for b in range(2):
                    n = 2 * i + b
                    pool.wait_ge(ctx_in, 16 * n + 16)
                    pool.wait_ge(v_proj, KT * (n - 1) + PRIME_V)
                    pool.sem_inc(s_turn, 1)
                    pool.tensor_copy(hi[b][:, :, :], raw[:, :, :]).then_inc(s_hi, 1)
                    pool.wait_ge(s_hi, n + 1)
                    pool.tensor_tensor(lo[b][:, :, :], raw[:, :, :], f32(hi[b][:, :, :]), ALU.subtract).then_inc(s_lo, 1)

        @block.tensor
        def _(pe):
            pe.sem_inc(v_proj, PRIME_V)
            with pe.Fori(0, NCH // 2) as i:
                for b in range(2):
                    n = 2 * i + b
                    pe.wait_ge(s_lo, n + 1 + PRIME_LO)
                    for g in range(G):
                        pe.wait_ge(v_done, KT * (n - 1) + g + 1 + PRIME_EV)
                        split_product(pe, proj[g][:, :],
                                      [(c.wk_hi[:, k, g * P:(g + 1) * P], c.wk_lo[:, k, g * P:(g + 1) * P]) for k in range(DC)],
                                      [(hi[b][:, k, :], lo[b][:, k, :]) for k in range(DC)]).then_inc(k_proj, 1)
                    for t in range(KT):
                        pe.wait_ge(k_lo_done, G * n + t + 1)
                        split_product(pe, proj[t][:, :],
                                      [(hi[b][:, k, t * P:(t + 1) * P], lo[b][:, k, t * P:(t + 1) * P]) for k in range(DC)],
                                      [(c.wv_hi[:, k, :], c.wv_lo[:, k, :]) for k in range(DC)]).then_inc(v_proj, 1)
                        for h in range(HG * t, HG * t + HG):
                            for s in range(PAIRS):
                                if s == 0:
                                    pe.wait_ge(s_st, H * n + h - 1 + 1 + PRIME_ST)
                                else:
                                    pe.wait_ge(s_copied, H * n + h - 1 + 1 + PRIME_CP)
                                for q in range(2):
                                    at = (2 * s + q) * P
                                    mm = pe.matmul(sc[s][:, q * CH:(q + 1) * CH], c.qmask[:, h, at:at + P],
                                                   k_hi[b][:, t, :], start=True, stop=True)
                                mm.then_inc(sc_ready[s], 1)

        @block.scalar
        def _(act):
            act.sem_inc(v_done, PRIME_EV)
            act.sem_inc(s_copied, PRIME_CP)
            with act.Fori(0, NCH // 2) as i:
                for b in range(2):
                    n = 2 * i + b
                    act.wait_ge(k_hi_out[b], 16 * i + PRIME_OUT)
                    for g in range(G):
                        act.wait_ge(k_proj, G * n + g + 1)
                        act.activation(k_hi[b][:, g, :], proj[g][:, :], ACT.Identity, bias=c.bk[:, g:g + 1]).then_inc(k_hi_done, 1)
                    act.wait_ge(v_out, 16 * n + PRIME_OUT)
                    for t in range(KT):
                        act.wait_ge(v_proj, KT * n + t + 1 + PRIME_V)
                        act.activation(v[:, :, t, :], proj[t][:, :].rearrange("p (g d) -> p g d", g=G), ACT.Copy).then_inc(v_done, 1)
                        for h in range(HG * t, HG * t + HG):
                            act.wait_ge(sc_ready[1], H * n + h + 1)
                            act.wait_ge(s_run, H * n + h - 2 + 1 + PRIME_R)
                            act.activation(half[:, h % 2, :], sc[1][:, :], ACT.Copy).then_inc(s_copied, 1)

        @block.vector
        def _(dve):
            dve.memset(run[:, :, :], NEG).then_inc(s_run, 1)
            dve.memset(best[:, :, :], NEG).then_inc(s_best, PRIME_M)
            dve.wait_ge(s_run, 1)
            dve.sem_inc(s_run, PRIME_R - 1)
            dve.sem_inc(s_st, PRIME_ST)

            def merge(n, h):
                dve.wait_ge(s_copied, H * n + h + 1 + PRIME_CP)
                dve.wait_ge(s_run, H * (n - 1) + h + 1 + PRIME_R)
                dve.tensor_tensor(run[:, h, :], run[:, h, :], half[:, h % 2, :], ALU.max).then_inc(s_run, 1)

            with dve.Fori(0, NCH // 2) as i:
                for b in range(2):
                    n = 2 * i + b
                    dve.wait_ge(k_lo_out, 16 * n + PRIME_OUT)
                    for g in range(G):
                        dve.wait_ge(k_hi_done, G * n + g + 1)
                        dve.scalar_tensor_tensor(out=k_lo[:, g, :], in0=proj[g][:, :], scalar=c.bk[:, g:g + 1],
                                                 in1=f32(k_hi[b][:, g, :]), op0=ALU.add, op1=ALU.subtract).then_inc(k_lo_done, 1)
                    for h in range(H):
                        dve.wait_ge(sc_ready[0], H * n + h + 1)
                        dve.tensor_reduce(st[:, h, :], sc[0][:, :].rearrange("p (q k) -> p q k", q=2), AX.X, ALU.max).then_inc(s_st, 1)
                        if h >= 1:
                            merge(n, h - 1)
                    merge(n, H - 1)
                    dve.wait_ge(s_st, H * n + H + PRIME_ST)
                    dve.wait_ge(s_best, n + PRIME_M)
                    dve.tensor_tensor(best[:, :, :], best[:, :, :], st[:, :, :], ALU.max).then_inc(s_best, 1)

            dve.wait_ge(s_run, H * NCH + PRIME_R)
            view = run[:, :, :].rearrange("p h (q k) -> p (h q) k", q=2)
            width, steps = CH // 2, 0
            while width >= 32:
                if steps:
                    dve.wait_ge(s_tree, steps)
                dve.tensor_tensor(view[:, :, 0:width], view[:, :, 0:width], view[:, :, width:2 * width], ALU.max).then_inc(s_tree, 1)
                steps += 1
                width //= 2
            dve.wait_ge(s_tree, steps)
            dve.tensor_reduce(c.neg[:, :, 2:4], view[:, :, 0:2 * width].rearrange("p (h q) k -> p h q k", q=2), AX.X, ALU.max).then_inc(s_tree, 1)
            dve.wait_ge(s_best, NCH + PRIME_M)
            dve.tensor_copy(c.neg[:, :, 0:2], best[:, :, :]).then_inc(s_tree, 1)
            dve.wait_ge(s_tree, steps + 2)


def stack_queries(nc, c):
    with ExitStack() as stack:
        sb, pb, sem = allocators(nc, stack, "stq")
        q_hi = sb("q_hi", [P, G, N], F32R)
        q_lo = sb("q_lo", [P, G, N], F32R)
        shift = sb("shift", [P, MROW + 2 * H * NT])
        shift_hi = sb("shift_hi", [P, H * NT], F32R)
        rows = [pb(f"rows{i}", [P, N]) for i in range(4)]
        block = stack.enter_context(nc.Block())
        maximum_rows(nc, block, c, sem, c.neg, shift, shift_hi, rows, c.qst)
        s_hi, s_lo, s_copy_act, s_copy_dve = sem("hi"), sem("lo"), sem("copy_act"), sem("copy_dve")

        @block.gpsimd
        def _(pool):
            pool.wait_ge(s_hi, 1)
            pool.tensor_tensor(q_lo[:, :, :], c.qT[:, :, :], f32(q_hi[:, :, :]), ALU.subtract).then_inc(s_lo, 1)

        @block.scalar
        def _(act):
            act.activation(q_hi[:, :, :], c.qT[:, :, :], ACT.Copy).then_inc(s_hi, 1)
            act.wait_ge(s_hi, 1)
            stack_copies(act, c.qst, f32(q_hi[:, :, :]), 0, s_copy_act)
            act.wait_ge(s_lo, 1)
            stack_copies(act, c.qst, f32(q_lo[:, :, :]), 2, s_copy_act)
            act.wait_ge(s_copy_act, 2 * HG)

        @block.vector
        def _(dve):
            dve.wait_ge(s_hi, 1)
            stack_copies(dve, c.qst, f32(q_hi[:, :, :]), 1, s_copy_dve)
            dve.wait_ge(s_copy_dve, HG)


def stack_copies(engine, stacks, part, place, s_copy):
    for j in range(HG):
        src, dst = part[HD * j:HD * j + HD, :, :], stacks[HD * place:HD * place + HD, j::HG, :]
        if engine.engine == mybir.EngineType.Activation:
            engine.activation(dst, src, ACT.Copy).then_inc(s_copy, 1)
        else:
            engine.tensor_copy(dst, src).then_inc(s_copy, 1)


def maximum_rows(nc, block, c, sem, best, shift, shift_hi, rows, stacks):
    s_set, s_t, s_row = sem("set"), sem("turned"), sem("row")
    COUNT = H * NT

    @block.vector
    def _(dve):
        flat = best[:, :, :].rearrange("p h t -> p (h t)")
        parts = shift[:, MROW:].rearrange("p (i two) -> p i two", two=2)
        dve.memset(shift[:, 0:MROW], 0.0).then_inc(s_set, 1)
        dve.tensor_scalar(shift_hi[:, :], flat, -1.0, None, ALU.mult).then_inc(s_set, 1)
        dve.wait_ge(s_set, 2)
        dve.tensor_copy(parts[:, :, 0], f32(shift_hi[:, :])).then_inc(s_set, 1)
        dve.scalar_tensor_tensor(out=parts[:, :, 1], in0=flat, scalar=-1.0, in1=f32(shift_hi[:, :]),
                                 op0=ALU.mult, op1=ALU.subtract).then_inc(s_set, 1)
        for h in range(H):
            dve.wait_ge(s_t, h + 1)
            dve.tensor_copy(stacks[MROW:MROW + 2, h, :], rows[h % 4][MROW:MROW + 2, :]).then_inc(s_row, 1)
        dve.wait_ge(s_row, H)

    @block.tensor
    def _(pe):
        pe.wait_ge(s_set, 4)
        for h in range(H):
            if h >= 4:
                pe.wait_ge(s_row, h - 3)
            for t in range(NT):
                i = h * NT + t
                mm = pe.transpose(rows[h % 4][0:MROW + 2, t * P:(t + 1) * P], shift[:, 2 * i:2 * i + MROW + 2], c.ident[:, :])
            mm.then_inc(s_t, 1)


def attend_context(nc, c):
    PRIME_EXP, PRIME_PV, PRIME_ADD, PRIME_SUM = 2, 8, 6, 1
    RING = 2 * KT
    with ExitStack() as stack:
        sb, pb, sem = allocators(nc, stack, "att")
        kst = [sb(f"kst{b}", [STK + 2, HG, CH], F32R) for b in range(2)]
        val = [sb(f"val{b}", [P, KT, P]) for b in range(2)]
        pr = sb("pr", [P, RING, HG, N])
        tot = [sb(f"tot{b}", [P, HG, N]) for b in range(2)]
        rs = sb("rs", [P, N])
        zero = sb("zero", [P, N], BF16)
        sc = [pb(f"sc{s}", [P, 2 * N]) for s in range(2)]
        o = [pb(f"o{i}", [P, N]) for i in range(2)]
        den = [pb(f"den{i}", [P, N]) for i in range(2)]
        kv_in = [sem(f"kv_in{b}") for b in range(2)]
        s_ones, s_zero, s_sc, s_exp, s_pv, s_add, s_sum, s_clear = (
            sem(n) for n in ("ones", "zero", "sc", "exp", "pv", "add", "sum", "clear"))
        s_rs, s_norm, s_out = sem("rs"), sem("norm"), sem("out")
        SUMS = NCH + 1
        block = stack.enter_context(nc.Block())

        @block.gpsimd
        def _(pool):
            for b in range(2):
                pool.memset(f32(kst[b][MROW:MROW + 2, :, :]), 1.0).then_inc(s_ones, 1)

        @block.sync
        def _(sp):
            for g in range(G):
                with sp.Fori(0, NCH // 2) as i:
                    for b in range(2):
                        chunk = 2 * i + b
                        sp.wait_ge(s_pv, KT * (NCH * g + chunk - 1) + PRIME_PV)
                        for row, part in ((0, 0), (1, 1), (2, 0)):
                            sp.dma_start(f32(kst[b][HD * row:HD * row + HD, :, :]),
                                         c.k_dram[chunk, g, part].rearrange("(j d) k -> d j k", j=HG)).then_inc(kv_in[b], 16)
                        sp.dma_start(val[b][:, :, :], c.v_dram[chunk, g]).then_inc(kv_in[b], 16)

        @block.tensor
        def _(pe):
            pe.sem_inc(s_pv, PRIME_PV)
            pe.sem_inc(s_sum, PRIME_SUM)
            pe.wait_ge(s_ones, 2)
            pe.wait_ge(s_zero, 1)

            def scores(g, b, i, u):
                T = KT * (NCH * g + 2 * i + b) + u
                if u == 0:
                    pe.wait_ge(kv_in[b], 64 * (NCH // 2 * g + i + 1))
                for s in range(2):
                    pe.wait_ge(s_exp, 2 * (T - 1) + s + 1 + PRIME_EXP)
                    for r in range(2):
                        j = 2 * s + r
                        mm = pe.matmul(sc[s][:, r * N:(r + 1) * N], kst[b][:, j, u * P:(u + 1) * P],
                                       c.qst[:, HG * g + j, :], start=True, stop=True)
                    mm.then_inc(s_sc, 1)

            def weighted(g, b, i, u):
                T = KT * (NCH * g + 2 * i + b) + u
                pe.wait_ge(s_exp, 2 * T + 2 + PRIME_EXP)
                for j in range(HG):
                    at = slice(HD * j, HD * j + HD)
                    mm = pe.matmul(o[g % 2][at, :], val[b][:, u, at], pr[:, KT * b + u, j, :],
                                   start=False, stop=False, skip_group_check=True)
                mm.then_inc(s_pv, 1)

            def sums(g, b, count):
                pe.wait_ge(s_add, 3 * count + PRIME_ADD)
                for j in range(HG):
                    mm = pe.matmul(den[g % 2][HD * j:HD * j + HD, :], c.ones[:, :], tot[b][:, j, :],
                                   start=False, stop=False, skip_group_check=True)
                mm.then_inc(s_sum, 1)

            def body(g, i, last):
                for b in range(2):
                    for u in range(KT):
                        if u + 1 < KT:
                            scores(g, b, i, u + 1)
                        elif b == 0:
                            scores(g, 1, i, 0)
                        elif not last:
                            scores(g, 0, i + 1, 0)
                        elif g + 1 < G:
                            scores(g + 1, 0, 0, 0)
                        weighted(g, b, i, u)
                        if u == 1:
                            sums(g, 1 - b, NCH * g + 2 * i + b)

            scores(0, 0, 0, 0)
            for g in range(G):
                if g >= 2:
                    pe.wait_ge(s_out, g - 1)
                for bank in (o[g % 2], den[g % 2]):
                    pe.matmul(bank[:, :], zero[:, 0:P], zero[:, :], start=True, stop=False, skip_group_check=True)
                pe.wait_ge(s_clear, g + 1)
                with pe.Fori(0, NCH // 2 - 1) as i:
                    body(g, i, False)
                body(g, NCH // 2 - 1, True)
                sums(g, 1, NCH * (g + 1))

        @block.scalar
        def _(act):
            act.sem_inc(s_exp, PRIME_EXP)
            for g in range(G):
                with act.Fori(0, NCH // 2) as i:
                    for b in range(2):
                        for u in range(KT):
                            T = KT * (NCH * g + 2 * i + b) + u
                            act.wait_ge(s_pv, T - RING + 1 + PRIME_PV)
                            act.wait_ge(s_add, 3 * (NCH * g + 2 * i + b - 2) + max(u, 1) + PRIME_ADD)
                            for s in range(2):
                                act.wait_ge(s_sc, 2 * T + s + 1)
                                act.activation(pr[:, KT * b + u, 2 * s:2 * s + 2, :],
                                               sc[s][:, :].rearrange("p (j q) -> p j q", j=2), ACT.Exp,
                                               scale=SCALE).then_inc(s_exp, 1)

        def normalise(dve, c, g):
            dve.wait_ge(s_sum, SUMS * (g + 1) + PRIME_SUM)
            dve.wait_ge(s_pv, KT * NCH * (g + 1) + PRIME_PV)
            dve.reciprocal(rs[:, :], den[g % 2][:, :]).then_inc(s_rs, 1)
            dve.wait_ge(s_rs, g + 1)
            dve.tensor_tensor(c.aoT[:, g, :], o[g % 2][:, :], rs[:, :], ALU.mult).then_inc(s_norm, 1)
            dve.wait_ge(s_norm, g + 1)
            dve.tensor_scalar(c.aoT[:, g, :], c.aoT[:, g, :], c.bv[:, g:g + 1], None, ALU.add).then_inc(s_out, 1)
            dve.wait_ge(s_out, g + 1)

        @block.vector
        def _(dve):
            dve.sem_inc(s_add, PRIME_ADD)
            dve.memset(zero[:, :], 0.0).then_inc(s_zero, 1)
            for g in range(G):
                if g >= 1:
                    dve.wait_ge(s_sum, SUMS * g + PRIME_SUM)
                dve.memset(tot[1][:, :, :], 0.0).then_inc(s_clear, 1)
                if g >= 1:
                    normalise(dve, c, g - 1)
                with dve.Fori(0, NCH // 2) as i:
                    for b in range(2):
                        chunk = NCH * g + 2 * i + b
                        dve.wait_ge(s_sum, SUMS * g + 2 * i + b + PRIME_SUM)
                        for u in range(1, KT):
                            dve.wait_ge(s_exp, 2 * (KT * chunk + u) + 2 + PRIME_EXP)
                            if u == 1:
                                one = pr[:, KT * b, :, :]
                            else:
                                dve.wait_ge(s_add, 3 * chunk + u - 1 + PRIME_ADD)
                                one = tot[b][:, :, :]
                            dve.tensor_tensor(tot[b][:, :, :], one, pr[:, KT * b + u, :, :], ALU.add).then_inc(s_add, 1)
            normalise(dve, c, G - 1)



def rows_out(nc, c, name, srcT, w, add, out, bias=None):
    with ExitStack() as stack:
        sb, pb, sem = allocators(nc, stack, name)
        acc = [pb(f"acc{t}", [P, D]) for t in range(NT)]
        s_mm, s_out = sem("mm"), sem("out")
        block = stack.enter_context(nc.Block())

        @block.tensor
        def _(pe):
            for t in range(NT):
                if bias is not None:
                    pe.matmul(acc[t][:, :], c.one_row[:, :], bias, start=True, stop=False)
                for k in range(DC):
                    mm = pe.matmul(acc[t][:, :], srcT[:, k, t * P:(t + 1) * P], w[:, k, :],
                                   start=(bias is None and k == 0), stop=(k == DC - 1))
                mm.then_inc(s_mm, 1)

        @block.vector
        def _(dve):
            for t in range(NT):
                dve.wait_ge(s_mm, t + 1)
                dve.tensor_tensor(out[:, t, :], acc[t][:, :], add[:, t, :], ALU.add).then_inc(s_out, 1)
            dve.wait_ge(s_out, NT)


def normalised_transposed(nc, c, name, x, hT):
    with ExitStack() as stack:
        sb, pb, sem = allocators(nc, stack, name)
        stats = sb("stats", [P, NT, 6])
        mv = sb("mv", [P, NT, 2])
        std = sb("std", [P, NT])
        rstd = sb("rstd", [P, NT])
        h = sb("h", [P, NT, D])
        tp = [pb(f"tp{i}", [P, N]) for i in range(DC)]
        s_stats, s_var, s_std, s_rstd, s_h, s_tp, s_hT = (
            sem(n) for n in ("stats", "var", "std", "rstd", "h", "tp", "hT"))
        block = stack.enter_context(nc.Block())

        @block.vector
        def _(dve):
            layer_norm(dve, x, h, stats, mv, std, rstd, s_stats, s_var, s_std, s_rstd, s_h)

        @block.tensor
        def _(pe):
            pe.wait_ge(s_h, NT)
            for k in range(DC):
                for t in range(NT):
                    mm = pe.transpose(tp[k][:, t * P:(t + 1) * P], h[:, t, k * P:(k + 1) * P], c.ident[:, :])
                mm.then_inc(s_tp, 1)

        @block.scalar
        def _(act):
            act.wait_ge(s_var, 1)
            act.activation(std[:, :], std[:, :], ACT.Sqrt).then_inc(s_std, 1)
            for k in range(DC):
                act.wait_ge(s_tp, k + 1)
                act.activation(hT[:, k, :], tp[k][:, :], ACT.Copy).then_inc(s_hT, 1)
            act.wait_ge(s_hT, DC)


def self_projections(nc, c):
    with ExitStack() as stack:
        sb, pb, sem = allocators(nc, stack, "sp")
        w = {n: sb(n, [P, DC, D]) for n in ("wq", "wk")}
        aff = sb("aff", [P, 4])
        total = sb("total", [P, NT * H])
        mean = sb("mean", [P, NT * H])
        spread = sb("spread", [P, NT * H])
        std = sb("std", [P, NT * H])
        rstd = sb("rstd", [P, NT * H])
        cen = sb("cen", [P, NT, D])
        sq = sb("sq", [P, NT, D])
        nrm = sb("nrm", [P, NT, D])
        full = sb("full", [P, G, N])
        hi = sb("hi", [P, G, N], F32R)
        lo = sb("lo", [P, G, N], F32R)
        raw = pb("raw", [P, NT, D])
        tp = [pb(f"tp{i}", [P, N]) for i in range(G)]
        w_in, aff_in, rest_in = sem("w_in"), sem("aff_in"), sem("rest_in")
        s_raw, s_cen, s_sq, s_var, s_std, s_nrm, s_tp, s_full, s_hi, s_lo, s_copy_act, s_copy_dve, s_v = (
            sem(n) for n in ("raw", "cen", "sq", "var", "std", "nrm", "tp", "full", "hi", "lo", "copy_act", "copy_dve", "v"))
        s_step = sem("step")
        block = stack.enter_context(nc.Block())
        KINDS = (("wq", c.sqst, 1, 0), ("wk", c.skst, 2, 2))

        def heads(ap):
            return ap.rearrange("p t (h d) -> p (t h) d", d=HD)

        def wide(ap):
            return ap[:, :].unsqueeze(2).broadcast_to([P, NT * H, HD])

        @block.sync
        def _(sp):
            sp.dma_start(w["wq"][:, :, :], c.dram["sWqT"].rearrange("(k p) o -> p k o", p=P)).then_inc(w_in, 16)
            sp.dma_start(w["wk"][:, :, :], c.dram["sWkT"].rearrange("(k p) o -> p k o", p=P)).then_inc(w_in, 16)
            for j in range(HG):
                sp.dma_start(aff[HD * j:HD * j + HD, :], c.dram["affine"]).then_inc(aff_in, 16)

        @block.tensor
        def _(pe):
            pe.wait_ge(w_in, 32)
            for n, (name, *_) in enumerate(KINDS):
                if n:
                    pe.wait_ge(s_cen, n)
                for t in range(NT):
                    for k in range(DC):
                        mm = pe.matmul(raw[:, t, :], c.hT[:, k, t * P:(t + 1) * P], w[name][:, k, :],
                                       start=(k == 0), stop=(k == DC - 1))
                mm.then_inc(s_raw, 1)
                pe.wait_ge(s_nrm, n + 1)
                for g in range(G):
                    if n:
                        pe.wait_ge(s_full, G * (n - 1) + g + 1)
                    for t in range(NT):
                        mm = pe.transpose(tp[g][:, t * P:(t + 1) * P], nrm[:, t, g * P:(g + 1) * P], c.ident[:, :])
                    mm.then_inc(s_tp, 1)
            pe.wait_ge(c.sv_in, 16)
            for t in range(NT):
                for k in range(DC):
                    mm = pe.matmul(raw[:, t, :], c.hT[:, k, t * P:(t + 1) * P], c.swvT[:, k, :],
                                   start=(k == 0), stop=(k == DC - 1))
            mm.then_inc(s_v, 1)

        @block.vector
        def _(dve):
            steps = 0

            def step(instruction):
                nonlocal steps
                steps += 1
                instruction.then_inc(s_step, 1)
                dve.wait_ge(s_step, steps)

            for n, (name, stacks, second_hi, col) in enumerate(KINDS):
                dve.wait_ge(s_raw, n + 1)
                step(dve.tensor_reduce(total[:, :], heads(raw[:, :, :]), AX.X, ALU.add))
                step(dve.tensor_scalar(mean[:, :], total[:, :], 1.0 / HD, None, ALU.mult))
                dve.tensor_tensor(heads(cen[:, :, :]), heads(raw[:, :, :]), wide(mean), ALU.subtract).then_inc(s_cen, 1)
                dve.wait_ge(s_sq, n + 1)
                step(dve.tensor_reduce(spread[:, :], heads(sq[:, :, :]), AX.X, ALU.add))
                dve.tensor_scalar(std[:, :], spread[:, :], 1.0 / HD, EPS, ALU.mult, ALU.add).then_inc(s_var, 1)
                dve.wait_ge(s_std, n + 1)
                step(dve.reciprocal(rstd[:, :], std[:, :]))
                if n:
                    dve.wait_ge(s_tp, G * n)
                dve.tensor_tensor(heads(nrm[:, :, :]), heads(cen[:, :, :]), wide(rstd), ALU.mult).then_inc(s_nrm, 1)
                dve.wait_ge(s_full, G * (n + 1))
                if n:
                    dve.wait_ge(s_copy_act, 2 * HG * n)
                    dve.wait_ge(s_copy_dve, HG * n)
                dve.tensor_copy(hi[:, :, :], full[:, :, :]).then_inc(s_hi, 1)
                dve.wait_ge(s_hi, n + 1)
                dve.tensor_tensor(lo[:, :, :], full[:, :, :], f32(hi[:, :, :]), ALU.subtract).then_inc(s_lo, 1)
                dve.wait_ge(s_lo, n + 1)
                stack_copies(dve, stacks, f32(hi[:, :, :]), 0, s_copy_dve)
            dve.wait_ge(s_v, 1)
            step(dve.tensor_copy(c.sval[:, :, :], raw[:, :, :]))
            dve.wait_ge(s_copy_dve, 2 * HG)

        @block.scalar
        def _(act):
            for n, (name, stacks, second_hi, col) in enumerate(KINDS):
                act.wait_ge(s_cen, n + 1)
                act.activation(sq[:, :, :], cen[:, :, :], ACT.Square).then_inc(s_sq, 1)
                act.wait_ge(s_var, n + 1)
                act.activation(std[:, :], std[:, :], ACT.Sqrt).then_inc(s_std, 1)
                act.wait_ge(aff_in, 16 * HG)
                if n:
                    act.wait_ge(s_lo, n)
                for g in range(G):
                    act.wait_ge(s_tp, G * n + g + 1)
                    act.activation(full[:, g, :], tp[g][:, :], ACT.Identity, scale=aff[:, col:col + 1],
                                   bias=aff[:, col + 1:col + 2]).then_inc(s_full, 1)
                act.wait_ge(s_lo, n + 1)
                for place in (1, 2):
                    part = hi if place == second_hi else lo
                    stack_copies(act, stacks, f32(part[:, :, :]), place, s_copy_act)

        @block.gpsimd
        def _(pool):
            pool.memset(f32(c.skst[MROW:MROW + 2, :, :]), 1.0).then_inc(rest_in, 1)
            pool.wait_ge(rest_in, 1)


def self_maximum(nc, c):
    with ExitStack() as stack:
        sb, pb, sem = allocators(nc, stack, "sm")
        shift = sb("shift", [P, MROW + 2 * H * NT])
        shift_hi = sb("shift_hi", [P, H * NT], F32R)
        sc = [pb(f"sc{i}", [P, 2, N]) for i in range(2)]
        rows = [pb(f"rows{i}", [P, N]) for i in range(4)]
        s_sc, s_max = sem("sc"), sem("max")
        block = stack.enter_context(nc.Block())

        @block.tensor
        def _(pe):
            for i in range(2 * H):
                if i >= 2:
                    pe.wait_ge(s_max, i - 1)
                h = i // 2
                for q in range(2):
                    at = (2 * (i % 2) + q) * P
                    mm = pe.matmul(sc[i % 2][:, q, :], c.sqst[0:STK, h, at:at + P], c.skst[0:STK, h, :], start=True, stop=True)
                mm.then_inc(s_sc, 1)

        @block.vector
        def _(dve):
            for i in range(2 * H):
                dve.wait_ge(s_sc, i + 1)
                at = 2 * (i % 2)
                dve.tensor_reduce(c.neg[:, i // 2, at:at + 2], sc[i % 2][:, :, :], AX.X, ALU.max).then_inc(s_max, 1)
            dve.wait_ge(s_max, 2 * H)

        maximum_rows(nc, block, c, sem, c.neg, shift, shift_hi, rows, c.sqst)


def self_attend(nc, c):
    with ExitStack() as stack:
        sb, pb, sem = allocators(nc, stack, "sa")
        pr = sb("pr", [P, 4, HG, N])
        rs = sb("rs", [P, N])
        sc = [pb(f"sc{s}", [P, 2 * N]) for s in range(2)]
        o = [pb(f"o{i}", [P, N]) for i in range(2)]
        den = [pb(f"den{i}", [P, N]) for i in range(2)]
        s_sc, s_exp, s_pv, s_rs, s_out = (sem(n) for n in ("sc", "exp", "pv", "rs", "out"))
        block = stack.enter_context(nc.Block())

        @block.tensor
        def _(pe):
            def scores(T):
                g, u = divmod(T, NT)
                for s in range(2):
                    if T >= 1:
                        pe.wait_ge(s_exp, 2 * (T - 1) + s + 1)
                    for r in range(2):
                        j = 2 * s + r
                        mm = pe.matmul(sc[s][:, r * N:(r + 1) * N], c.skst[:, HG * g + j, u * P:(u + 1) * P],
                                       c.sqst[:, HG * g + j, :], start=True, stop=True)
                    mm.then_inc(s_sc, 1)

            scores(0)
            for T in range(G * NT):
                g, u = divmod(T, NT)
                if T + 1 < G * NT:
                    scores(T + 1)
                pe.wait_ge(s_exp, 2 * T + 2)
                if u == 0 and g >= 2:
                    pe.wait_ge(s_out, g - 1)
                for j in range(HG):
                    at = slice(HD * j, HD * j + HD)
                    pe.matmul(o[g % 2][at, :], c.sval[:, u, P * g + HD * j:P * g + HD * j + HD], pr[:, T % 4, j, :],
                              start=(u == 0), stop=(u == NT - 1))
                for j in range(HG):
                    at = slice(HD * j, HD * j + HD)
                    mm = pe.matmul(den[g % 2][at, :], c.ones[:, :], pr[:, T % 4, j, :], start=(u == 0), stop=(u == NT - 1))
                mm.then_inc(s_pv, 1)

        @block.scalar
        def _(act):
            for T in range(G * NT):
                if T >= 4:
                    act.wait_ge(s_pv, T - 3)
                for s in range(2):
                    act.wait_ge(s_sc, 2 * T + s + 1)
                    act.activation(pr[:, T % 4, 2 * s:2 * s + 2, :], sc[s][:, :].rearrange("p (j q) -> p j q", j=2),
                                   ACT.Exp, scale=SCALE).then_inc(s_exp, 1)

        @block.vector
        def _(dve):
            for g in range(G):
                dve.wait_ge(s_pv, NT * (g + 1))
                if g >= 1:
                    dve.wait_ge(s_out, g)
                dve.reciprocal(rs[:, :], den[g % 2][:, :]).then_inc(s_rs, 1)
                dve.wait_ge(s_rs, g + 1)
                dve.tensor_tensor(c.aoT[:, g, :], o[g % 2][:, :], rs[:, :], ALU.mult).then_inc(s_out, 1)
            dve.wait_ge(s_out, G)


def sparse_mix(nc, c):
    with ExitStack() as stack:
        sb, pb, sem = allocators(nc, stack, "mix")
        wv = sb("wv", [P, H, TOPM])
        wo = sb("wo", [P, HD, TOPM])
        vm = sb("vm", [P, H])
        om = sb("om", [P, HD])
        bv = sb("bv", [P, HG * H])
        bo = sb("bo", [P, HG, HD])
        flat = sb("flat", [P, G, N])
        z = sb("z", [P, 2, N])
        left = sb("left", [P, 2, N])
        top = sb("top", [P, 2, 8])
        zs = sb("zs", [P, 2, N])
        zp = [pb(f"zp{i}", [P, N]) for i in range(2)]
        yp = [pb(f"yp{g}", [P, N]) for g in range(G)]
        w_in, s_zero, s_vm, s_om, s_bv, s_bo, s_zp, s_z, s_zs, s_y, s_yT = (
            sem(n) for n in ("w_in", "zero", "vm", "om", "bv", "bo", "zp", "z", "zs", "y", "yT"))
        s_top, s_left, s_flat_act, s_flat_dve = sem("top"), sem("left"), sem("flat_act"), sem("flat_dve")
        block = stack.enter_context(nc.Block())

        def regroup(j, i):
            rows_per_block = N // H
            dst = flat[HD * i:HD * i + HD, :, :].rearrange("d b (t g j) -> d b t g j", g=G, j=HG)[:, :, :, :, j]
            src = c.aoT[HD * j:HD * j + HD, :, :].rearrange("d g (b i t) -> d b i t g", i=HG, t=rows_per_block)[:, :, i, :, :]
            return dst, src

        @block.sync
        def _(sp):
            for j in range(HG):
                sp.dma_start(wv[HD * j:HD * j + HD, :, :], c.dram["spVT"]).then_inc(w_in, 16)
            for j in range(2 * HG):
                sp.dma_start(wo[H * j:H * j + H, :, :], c.dram["spOT"]).then_inc(w_in, 16)

        @block.gpsimd
        def _(pool):
            pool.memset(bv[:, :], 0.0).then_inc(s_zero, 1)
            pool.wait_ge(s_om, 2)
            for half in range(2):
                rows = slice(64 * half, 64 * half + 64)
                pool.tensor_copy(bo[rows, :, :], om[rows, :].unsqueeze(1).broadcast_to([64, HG, HD])).then_inc(s_bo, 1)
                pool.wait_ge(s_bo, 3 * half + 1)
                pool.affine_select(out=bo[rows, :, :], in_=bo[rows, :, :], compare_op=ALU.is_ge, fill=0.0, base=0,
                                   pattern=[[-H, HG], [0, HD]], channel_multiplier=1).then_inc(s_bo, 1)
                pool.wait_ge(s_bo, 3 * half + 2)
                pool.affine_select(out=bo[rows, :, :], in_=bo[rows, :, :], compare_op=ALU.is_ge, fill=0.0, base=H - 1,
                                   pattern=[[H, HG], [0, HD]], channel_multiplier=-1).then_inc(s_bo, 1)

        @block.vector
        def _(dve):
            dve.wait_ge(w_in, 16 * 3 * HG)
            dve.tensor_reduce(vm[:, :], wv[:, :, :], AX.X, ALU.add).then_inc(s_vm, 1)
            dve.tensor_reduce(om[:, :], wo[:, :, :], AX.X, ALU.add).then_inc(s_om, 1)
            dve.wait_ge(s_om, 1)
            dve.tensor_scalar(om[:, :], om[:, :], 1.0 / TOPM, None, ALU.mult).then_inc(s_om, 1)
            dve.wait_ge(s_vm, 1)
            dve.wait_ge(s_zero, 1)
            for j in range(HG):
                rows = slice(HD * j, HD * j + HD)
                dve.tensor_scalar(bv[rows, H * j:H * j + H], vm[rows, :], 1.0 / TOPM, None, ALU.mult).then_inc(s_bv, 1)
            for j in range(HG // 2, HG):
                for i in range(HG):
                    dve.tensor_copy(*regroup(j, i)).then_inc(s_flat_dve, 1)
            for i in range(2):
                dve.wait_ge(s_zp, i + 1)
                dve.tensor_copy(z[:, i, :], zp[i][:, :]).then_inc(s_z, 1)
            for i in range(2):
                dve.wait_ge(s_z, i + 1)
            for r in range(KEEP // 8):
                for i in range(2):
                    rest = z if r == 0 else left
                    if r:
                        dve.wait_ge(s_left, 2 * (r - 1) + i + 1)
                    dve.max(out=top[:, i, :], in_=rest[:, i, :]).then_inc(s_top, 1)
                for i in range(2):
                    rest = z if r == 0 else left
                    dve.wait_ge(s_top, 2 * r + i + 1)
                    dve.match_replace(out=left[:, i, :], in_to_replace=top[:, i, :], in_values=rest[:, i, :],
                                      imm_value=NEG).then_inc(s_left, 1)
            for i in range(2):
                dve.wait_ge(s_left, 2 * (KEEP // 8 - 1) + i + 1)
                dve.scalar_tensor_tensor(out=zs[:, i, :], in0=left[:, i, :], scalar=NEG, in1=z[:, i, :],
                                         op0=ALU.is_equal, op1=ALU.mult).then_inc(s_zs, 1)

        @block.tensor
        def _(pe):
            pe.wait_ge(s_bv, HG)
            pe.wait_ge(s_flat_act, HG * HG // 2)
            pe.wait_ge(s_flat_dve, HG * HG // 2)
            for g in range(G):
                mm = pe.matmul(zp[g // 2][64 * (g % 2):64 * (g % 2) + 64, :], bv[:, :], flat[:, g, :], start=True, stop=True)
                if g % 2:
                    mm.then_inc(s_zp, 1)
            pe.wait_ge(s_bo, 6)
            for g in range(G):
                pe.wait_ge(s_zs, g // 2 + 1)
                rows = slice(64 * (g % 2), 64 * (g % 2) + 64)
                pe.matmul(yp[g][:, :], bo[rows, :, :].rearrange("p j d -> p (j d)"), zs[rows, g // 2, :],
                          start=True, stop=True).then_inc(s_y, 1)

        @block.scalar
        def _(act):
            for j in range(HG // 2):
                for i in range(HG):
                    dst, src = regroup(j, i)
                    act.activation(dst, src, ACT.Copy).then_inc(s_flat_act, 1)
            for g in range(G):
                act.wait_ge(s_y, g + 1)
                act.activation(c.yT[:, g, :], yp[g][:, :], ACT.Copy).then_inc(s_yT, 1)
            act.wait_ge(s_yT, G)


def route(nc, c):
    with ExitStack() as stack:
        sb, pb, sem = allocators(nc, stack, "rt")
        wg = sb("wg", [P, DC, E])
        b2 = sb("b2", [E, D])
        iota = sb("iota", [P, E])
        big = sb("big", [P, NT])
        ex = sb("ex", [P, NT, E])
        su = sb("su", [P, NT])
        ri = sb("ri", [P, NT])
        prob = sb("prob", [P, NT, E])
        top = sb("top", [P, NT, 8])
        idx = sb("idx", [P, NT, 8], U32)
        idf = sb("idf", [P, NT, 8])
        m1 = sb("m1", [P, NT, E])
        m2 = sb("m2", [P, NT, E])
        two = sb("two", [P, NT])
        rt = sb("rt", [P, NT])
        scT = sb("scT", [E, N])
        lg = pb("lg", [P, NT, E])
        tp = pb("tp", [P, N])
        ac = [pb(f"ac{t}", [P, D]) for t in range(NT)]
        w_in, s_lg, s_step, s_exp, s_iota, s_score, s_tp, s_scT, s_ac, s_hi = (
            sem(n) for n in ("w_in", "lg", "step", "exp", "iota", "score", "tp", "scT", "ac", "hi"))
        s_sub = sem("sub")
        block = stack.enter_context(nc.Block())

        @block.sync
        def _(sp):
            sp.dma_start(wg[:, :, :], c.dram["Wg"].rearrange("(k p) e -> p k e", p=P)).then_inc(w_in, 16)
            sp.dma_start(b2[:, :], c.dram["b2"]).then_inc(w_in, 16)
            sp.dma_start(c.b1[:, :, :], c.dram["b1"]).then_inc(w_in, 16)
            sp.wait_ge(w_in, 48)

        @block.gpsimd
        def _(pool):
            pool.iota(iota[:, :], pattern=[[1, E]], base=0, channel_multiplier=0,
                      allow_small_or_imprecise_dtypes=True).then_inc(s_iota, 1)

        @block.tensor
        def _(pe):
            pe.wait_ge(w_in, 48)
            for t in range(NT):
                for k in range(DC):
                    mm = pe.matmul(lg[:, t, :], c.hT[:, k, t * P:(t + 1) * P], wg[:, k, :], start=(k == 0), stop=(k == DC - 1))
            mm.then_inc(s_lg, 1)
            pe.wait_ge(s_score, 1)
            for t in range(NT):
                mm = pe.transpose(tp[0:E, t * P:(t + 1) * P], c.score[:, t, :], c.ident[:, :])
            mm.then_inc(s_tp, 1)
            pe.wait_ge(s_scT, 1)
            for t in range(NT):
                pe.matmul(ac[t][:, :], scT[:, t * P:(t + 1) * P], b2[:, :], start=True, stop=True).then_inc(s_ac, 1)

        @block.scalar
        def _(act):
            act.activation(c.hT_hi[:, :, :], c.hT[:, :, :], ACT.Copy).then_inc(s_hi, 1)
            act.wait_ge(s_sub, 1)
            act.activation(ex[:, :, :], ex[:, :, :], ACT.Exp).then_inc(s_exp, 1)
            act.wait_ge(s_tp, 1)
            act.activation(scT[:, :], tp[0:E, :], ACT.Copy).then_inc(s_scT, 1)

        @block.vector
        def _(dve):
            steps = 0

            def step(instruction):
                nonlocal steps
                steps += 1
                instruction.then_inc(s_step, 1)
                dve.wait_ge(s_step, steps)

            def wide(ap, n=E):
                return ap.unsqueeze(2).broadcast_to([P, NT, n])

            dve.wait_ge(s_hi, 1)
            step(dve.tensor_tensor(c.hT_lo[:, :, :], c.hT[:, :, :], f32(c.hT_hi[:, :, :]), ALU.subtract))
            dve.wait_ge(s_lg, 1)
            step(dve.tensor_reduce(big[:, :], lg[:, :, :], AX.X, ALU.max))
            dve.tensor_tensor(ex[:, :, :], lg[:, :, :], wide(big[:, :]), ALU.subtract).then_inc(s_sub, 1)
            dve.wait_ge(s_exp, 1)
            step(dve.tensor_reduce(su[:, :], ex[:, :, :], AX.X, ALU.add))
            step(dve.reciprocal(ri[:, :], su[:, :]))
            step(dve.tensor_tensor(prob[:, :, :], ex[:, :, :], wide(ri[:, :]), ALU.mult))
            for t in range(NT):
                step(dve.max(out=top[:, t, :], in_=prob[:, t, :]))
                step(dve.max_index(out=idx[:, t, :], in_max=top[:, t, :], in_values=prob[:, t, :]))
            step(dve.tensor_copy(idf[:, :, :], idx[:, :, :]))
            dve.wait_ge(s_iota, 1)
            number = iota[:, :].unsqueeze(1).broadcast_to([P, NT, E])
            step(dve.tensor_tensor(m1[:, :, :], number, wide(idf[:, :, 0]), ALU.is_equal))
            step(dve.tensor_tensor(m2[:, :, :], number, wide(idf[:, :, 1]), ALU.is_equal))
            step(dve.tensor_tensor(m1[:, :, :], m1[:, :, :], m2[:, :, :], ALU.add))
            step(dve.tensor_tensor(two[:, :], top[:, :, 0], top[:, :, 1], ALU.add))
            step(dve.reciprocal(rt[:, :], two[:, :]))
            step(dve.tensor_tensor(m2[:, :, :], prob[:, :, :], m1[:, :, :], ALU.mult))
            dve.tensor_tensor(c.score[:, :, :], m2[:, :, :], wide(rt[:, :]), ALU.mult).then_inc(s_score, 1)
            for t in range(NT):
                dve.wait_ge(s_ac, t + 1)
                step(dve.tensor_tensor(c.x[:, t, :], ac[t][:, :], c.x[:, t, :], ALU.add))


def experts(nc, c):
    PRIME = 8
    HALF = 4
    with ExitStack() as stack:
        sb, pb, sem = allocators(nc, stack, "ex")
        raw1 = sb("raw1", [P, DC, FF])
        raw2 = sb("raw2", [P, FC, D])
        w1_hi, w1_lo = sb("w1_hi", [P, DC, FF], F32R), sb("w1_lo", [P, DC, FF], F32R)
        w2_hi, w2_lo = sb("w2_hi", [P, FC, D], F32R), sb("w2_lo", [P, FC, D], F32R)
        hid = sb("hid", [P, 2, N])
        hid_hi, hid_lo = sb("hid_hi", [P, FC, N], F32R), sb("hid_lo", [P, FC, N], F32R)
        hp = [pb(f"hp{i}", [P, N]) for i in range(HALF)]
        yp = [pb(f"yp{t}", [P, D]) for t in range(NT)]
        in1, in2, s_hi1, s_lo1, s_hi2, s_lo2, s_hp, s_hid, s_hh, s_hl, s_yp, s_acc = (
            sem(n) for n in ("in1", "in2", "hi1", "lo1", "hi2", "lo2", "hp", "hid", "hh", "hl", "yp", "acc"))
        s_done = sem("done")
        block = stack.enter_context(nc.Block())

        @block.sync
        def _(sp):
            with sp.Fori(0, E) as e:
                sp.wait_ge(s_lo1, e + PRIME)
                sp.dma_start(raw1[:, :, :], c.dram["W1"][e].rearrange("(k p) f -> p k f", p=P)).then_inc(in1, 16)
                sp.wait_ge(s_lo2, e + PRIME)
                sp.dma_start(raw2[:, :, :], c.dram["W2"][e].rearrange("(k p) d -> p k d", p=P)).then_inc(in2, 16)
            sp.wait_ge(s_acc, NT * E + PRIME)
            sp.dma_start(c.dram["out"].rearrange("(t p) d -> p t d", p=P), c.x[:, :, :]).then_inc(s_done, 16)
            sp.wait_ge(s_done, 16)

        @block.gpsimd
        def _(pool):
            pool.sem_inc(s_lo1, PRIME)
            pool.sem_inc(s_lo2, PRIME)
            with pool.Fori(0, E) as e:
                pool.wait_ge(s_hi1, e + 1)
                pool.tensor_tensor(w1_lo[:, :, :], raw1[:, :, :], f32(w1_hi[:, :, :]), ALU.subtract).then_inc(s_lo1, 1)
                pool.wait_ge(s_hi2, e + 1)
                pool.tensor_tensor(w2_lo[:, :, :], raw2[:, :, :], f32(w2_hi[:, :, :]), ALU.subtract).then_inc(s_lo2, 1)

        @block.tensor
        def _(pe):
            pe.sem_inc(s_hp, PRIME)
            pe.sem_inc(s_yp, PRIME)
            with pe.Fori(0, E) as e:
                pe.wait_ge(s_lo1, e + 1 + PRIME)
                for f in range(FC):
                    pe.wait_ge(s_hid, FC * e + f - HALF + 1 + PRIME)
                    split_product(pe, hp[f % HALF][:, :],
                                  [(w1_hi[:, k, f * P:(f + 1) * P], w1_lo[:, k, f * P:(f + 1) * P]) for k in range(DC)],
                                  [(c.hT_hi[:, k, :], c.hT_lo[:, k, :]) for k in range(DC)]).then_inc(s_hp, 1)
                pe.wait_ge(s_lo2, e + 1 + PRIME)
                pe.wait_ge(s_hl, FC * e + FC + PRIME)
                for t in range(NT):
                    pe.wait_ge(s_acc, NT * (e - 1) + t + 1 + PRIME)
                    split_product(pe, yp[t][:, :],
                                  [(hid_hi[:, f, t * P:(t + 1) * P], hid_lo[:, f, t * P:(t + 1) * P]) for f in range(FC)],
                                  [(w2_hi[:, f, :], w2_lo[:, f, :]) for f in range(FC)]).then_inc(s_yp, 1)

        @block.scalar
        def _(act):
            act.sem_inc(s_hid, PRIME)
            with act.Fori(0, E) as e:
                act.wait_ge(in1, 16 * e + 16)
                act.wait_ge(s_hp, FC * e + PRIME)
                act.activation(w1_hi[:, :, :], raw1[:, :, :], ACT.Copy).then_inc(s_hi1, 1)
                act.wait_ge(in2, 16 * e + 16)
                act.wait_ge(s_yp, NT * e + PRIME)
                act.activation(w2_hi[:, :, :], raw2[:, :, :], ACT.Copy).then_inc(s_hi2, 1)
                for f in range(FC):
                    act.wait_ge(s_hp, FC * e + f + 1 + PRIME)
                    act.wait_ge(s_hl, FC * e + f - 2 + 1 + PRIME)
                    act.activation(hid[:, f % 2, :], hp[f % HALF][:, :], ACT.Relu,
                                   bias=c.b1[:, f, bass.ds(e, 1)]).then_inc(s_hid, 1)

        @block.vector
        def _(dve):
            dve.sem_inc(s_hl, PRIME)
            dve.sem_inc(s_acc, PRIME)
            with dve.Fori(0, E) as e:
                dve.wait_ge(s_yp, NT * e + PRIME)
                for f in range(FC):
                    dve.wait_ge(s_hid, FC * e + f + 1 + PRIME)
                    dve.tensor_copy(hid_hi[:, f, :], hid[:, f % 2, :]).then_inc(s_hh, 1)
                    dve.wait_ge(s_hh, FC * e + f + 1)
                    dve.tensor_tensor(hid_lo[:, f, :], hid[:, f % 2, :], f32(hid_hi[:, f, :]), ALU.subtract).then_inc(s_hl, 1)
                for t in range(NT):
                    dve.wait_ge(s_yp, NT * e + t + 1 + PRIME)
                    dve.wait_ge(s_acc, NT * (e - 1) + t + 1 + PRIME)
                    dve.scalar_tensor_tensor(out=c.x[:, t, :], in0=yp[t][:, :], scalar=c.score[:, t, bass.ds(e, 1)],
                                             in1=c.x[:, t, :], op0=ALU.mult, op1=ALU.add).then_inc(s_acc, 1)


def load_small(nc, c):
    with ExitStack() as stack:
        sb, pb, sem = allocators(nc, stack, "sml")
        s_in, s_set = sem("in"), sem("set")
        block = stack.enter_context(nc.Block())

        @block.sync
        def _(sp):
            sp.dma_start(c.bo[:, :], c.dram["bo"]).then_inc(s_in, 16)
            sp.wait_ge(s_in, 16)

        @block.gpsimd
        def _(pool):
            pool.memset(c.ones[:, :], 1.0).then_inc(s_set, 1)
            pool.memset(c.one_row[:, :], 1.0).then_inc(s_set, 1)
            pool.wait_ge(s_set, 2)


def perceiver_layer(nc, dram):
    c = Ctx()
    c.dram = dram
    c.k_dram = nc.dram_tensor("keys_scratch", [NCH, G, 2, P, CH], F32).ap()
    c.v_dram = nc.dram_tensor("values_scratch", [NCH, G, P, KT, P], F32).ap()
    with ExitStack() as whole:
        sb, pb, sem = allocators(nc, whole, "g")
        c.ident = sb("ident", [P, P])
        c.ones = sb("ones", [P, HD])
        c.one_row = sb("one_row", [1, P])
        c.x = sb("x", [P, NT, D])
        c.bq, c.bk, c.bv = sb("bq", [P, DC]), sb("bk", [P, DC]), sb("bv", [P, DC])
        c.bo = sb("bo", [1, D])
        c.neg = sb("neg", [P, H, NT])
        load_small(nc, c)
        with ExitStack() as cross:
            sb, pb, sem = allocators(nc, cross, "x")
            c.woT = sb("woT", [P, DC, D])
            c.qT = sb("qT", [P, G, N])
            with ExitStack() as first:
                sb, pb, sem = allocators(nc, first, "f")
                c.qmask = sb("qmask", [P, H, N], F32R)
                c.wk_hi, c.wk_lo = sb("wk_hi", [P, DC, D], F32R), sb("wk_lo", [P, DC, D], F32R)
                c.wv_hi, c.wv_lo = sb("wv_hi", [P, DC, D], F32R), sb("wv_lo", [P, DC, D], F32R)
                prepare(nc, c)
                project_context(nc, c)
            with ExitStack() as second:
                sb, pb, sem = allocators(nc, second, "s")
                c.qst = sb("qst", [STK + 2, H, N], F32R)
                c.aoT = sb("aoT", [P, G, N])
                stack_queries(nc, c)
                attend_context(nc, c)
                rows_out(nc, c, "xo", c.aoT, c.woT, c.x, c.x, bias=c.bo[:, :])
        with ExitStack() as own:
            sb, pb, sem = allocators(nc, own, "o")
            c.hT = sb("hT", [P, DC, N])
            c.sqst = sb("sqst", [STK + 2, H, N], F32R)
            c.skst = sb("skst", [STK + 2, H, N], F32R)
            c.sval = sb("sval", [P, NT, D])
            c.swvT = sb("swvT", [P, DC, D])
            c.swoT = sb("swoT", [P, DC, D])
            c.aoT = sb("aoT", [P, G, N])
            c.yT = sb("yT", [P, G, N])
            c.sv_in, c.so_in = sem("sv_in"), sem("so_in")
            with nc.Block() as block:
                @block.sync
                def _(sp):
                    sp.dma_start(c.swvT[:, :, :], dram["sWvT"].rearrange("(k p) o -> p k o", p=P)).then_inc(c.sv_in, 16)
                    sp.dma_start(c.swoT[:, :, :], dram["sWoT"].rearrange("(k p) o -> p k o", p=P)).then_inc(c.so_in, 16)
            normalised_transposed(nc, c, "n2", c.x, c.hT)
            self_projections(nc, c)
            self_maximum(nc, c)
            self_attend(nc, c)
            sparse_mix(nc, c)
            with nc.Block() as block:
                @block.tensor
                def _(pe):
                    pe.wait_ge(c.so_in, 16)
            rows_out(nc, c, "so", c.yT, c.swoT, c.x, c.x)
        with ExitStack() as ffn:
            sb, pb, sem = allocators(nc, ffn, "m")
            c.hT_hi, c.hT_lo = sb("hT_hi", [P, DC, N], F32R), sb("hT_lo", [P, DC, N], F32R)
            c.score = sb("score", [P, NT, E])
            c.b1 = sb("b1", [P, FC, E])
            with ExitStack() as routing:
                sb, pb, sem = allocators(nc, routing, "r")
                c.hT = sb("hT", [P, DC, N])
                normalised_transposed(nc, c, "n3", c.x, c.hT)
                route(nc, c)
            experts(nc, c)


def kernel(**inputs):
    import numpy as _np
    import concourse.bacc as _bacc
    from concourse import mybir as _mybir
    from concourse.bass_utils import run_bass_kernel_spmd as _run

    a = {k: _np.asarray(v) for k, v in inputs.items()}
    keep = _np.ascontiguousarray
    column = lambda b: keep(b.reshape(DC, P).T)
    arrays = {
        "x": keep(a["x"][0]),
        "ctx": keep(a["ctx_1024"][0].reshape(NCH, CH, DC, P).transpose(0, 3, 2, 1)),
        "WqT": keep(a["L0_xattn_Wq"].T), "WkT": keep(a["L0_xattn_Wk"].T),
        "WvT": keep(a["L0_xattn_Wv"].T), "WoT": keep(a["L0_xattn_Wo"].T),
        "bq": column(a["L0_xattn_bq"]), "bk": column(a["L0_xattn_bk"]), "bv": column(a["L0_xattn_bv"]),
        "bo": keep(a["L0_xattn_bo"].reshape(1, D)),
        "sWqT": keep(a["L0_attn_W_Q"].T), "sWkT": keep(a["L0_attn_W_K"].T),
        "sWvT": keep(a["L0_attn_W_V"].T), "sWoT": keep(a["L0_attn_W_O"].T),
        "affine": keep(_np.stack([a["L0_attn_q_ln_w"], a["L0_attn_q_ln_b"], a["L0_attn_k_ln_w"], a["L0_attn_k_ln_b"]], 1)),
        "spVT": keep(a["L0_attn_sparse_W_V"].transpose(1, 0, 2)),
        "spOT": keep(a["L0_attn_sparse_W_O"].transpose(0, 2, 1)),
        "Wg": keep(a["L0_ffn_Wg"]), "W1": keep(a["L0_ffn_W1"]), "W2": keep(a["L0_ffn_W2"]),
        "b1": keep(a["L0_ffn_b1"].reshape(E, FC, P).transpose(2, 1, 0)), "b2": keep(a["L0_ffn_b2"]),
    }
    nc = _bacc.Bacc("TRN2", target_bir_lowering=False, num_devices=1)
    dram = {n: nc.dram_tensor(f"in_{n}", v.shape, _mybir.dt.from_np(v.dtype), kind="ExternalInput").ap()
            for n, v in arrays.items()}
    dram["out"] = nc.dram_tensor("out_0", (N, D), F32, kind="ExternalOutput").ap()
    perceiver_layer(nc, dram)
    r = _run(nc, [{f"in_{n}": v for n, v in arrays.items()}], core_ids=[0])
    return r.results[0]["out_0"].reshape(1, N, D)
```

```python
from contextlib import ExitStack

import concourse.bass as bass
from concourse import mybir

F32 = mybir.dt.float32
F32R = mybir.dt.float32r
BF16 = mybir.dt.bfloat16
U32 = mybir.dt.uint32
ALU = mybir.AluOpType
ACT = mybir.ActivationFunctionType
AX = mybir.AxisListType

P = 128
D = 512
DC = D // P
N = 512
NT = N // P
M = 8192
CH = 512
NCH = M // CH
KT = CH // P
H = 16
HD = D // H
HG = P // HD
G = H // HG
SCALE = HD ** -0.5
EPS = 1e-5
KEEP = 128
TOPM = 128
E = 8
FF = 1024
FC = FF // P
NEG = -3.0e38
STK = 3 * HD
MROW = STK


class Ctx:
    pass


def f32(ap):
    return ap.bitcast(F32)


def allocators(nc, stack, tag):
    def sb(name, shape, dt=F32):
        return stack.enter_context(nc.sbuf_tensor(f"{tag}_{name}", shape, dt))

    def pb(name, shape, dt=F32):
        return stack.enter_context(nc.psum_tensor(f"{tag}_{name}", shape, dt))

    def sem(name):
        return stack.enter_context(nc.semaphore(f"{tag}_{name}"))

    return sb, pb, sem


def split_product(pe, out, a, b, last=True, first=True):
    n = len(a)
    for i in range(n):
        (ah, al), (bh, bl) = a[i], b[i]
        pe.matmul(out, ah, bh, start=(first and i == 0), stop=False)
        pe.matmul(out, ah, bl, start=False, stop=False)
        mm = pe.matmul(out, al, bh, start=False, stop=(last and i == n - 1))
    return mm


def prepare(nc, c):
    with ExitStack() as stack:
        sb, pb, sem = allocators(nc, stack, "prep")
        w_raw = {n: sb(f"{n}_raw", [P, DC, D]) for n in ("wq", "wk", "wv")}
        stats = sb("stats", [P, NT, 6])
        mv = sb("mv", [P, NT, 2])
        std = sb("std", [P, NT])
        rstd = sb("rstd", [P, NT])
        h = sb("h", [P, NT, D])
        hT = sb("hT", [P, DC, N])
        tp = [pb(f"tp{i}", [P, N]) for i in range(DC)]
        qp = [pb(f"qp{i}", [P, N]) for i in range(G)]
        x_in, w_in, wkv_in, rest_in = sem("x_in"), sem("w_in"), sem("wkv_in"), sem("rest_in")
        s_const, s_ident = sem("const"), sem("ident")
        s_stats, s_var, s_std, s_rstd, s_h = sem("stats"), sem("var"), sem("std"), sem("rstd"), sem("h")
        s_tp, s_hT, s_q, s_qT, s_mask, s_whi, s_wlo = (
            sem(n) for n in ("tp", "hT", "q", "qT", "mask", "whi", "wlo"))
        block = stack.enter_context(nc.Block())

        @block.sync
        def _(sp):
            sp.dma_start(c.x[:, :, :], c.dram["x"].rearrange("(t p) d -> p t d", p=P)).then_inc(x_in, 16)
            sp.dma_start(w_raw["wq"][:, :, :], c.dram["WqT"].rearrange("(k p) o -> p k o", p=P)).then_inc(w_in, 16)
            sp.dma_start(w_raw["wk"][:, :, :], c.dram["WkT"].rearrange("(k p) o -> p k o", p=P)).then_inc(wkv_in, 16)
            sp.dma_start(w_raw["wv"][:, :, :], c.dram["WvT"].rearrange("(k p) o -> p k o", p=P)).then_inc(wkv_in, 16)
            sp.wait_ge(rest_in, 48)

        @block.gpsimd
        def _(pool):
            pool.memset(c.ident[:, :], 0.0).then_inc(s_ident, 1)
            pool.memset(f32(c.qmask[:, :, :]), 0.0).then_inc(s_const, 1)
            pool.wait_ge(s_ident, 1)
            pool.affine_select(out=c.ident[:, :], in_=c.ident[:, :], compare_op=ALU.not_equal, fill=1.0,
                               base=0, pattern=[[-1, P]], channel_multiplier=1).then_inc(s_ident, 1)
            pool.wait_ge(wkv_in, 32)
            for n, (raw, hi, lo) in enumerate(((w_raw["wk"], c.wk_hi, c.wk_lo), (w_raw["wv"], c.wv_hi, c.wv_lo))):
                pool.wait_ge(s_whi, n + 1)
                pool.tensor_tensor(lo[:, :, :], raw[:, :, :], f32(hi[:, :, :]), ALU.subtract).then_inc(s_wlo, 1)

        @block.scalar
        def _(act):
            act.dma_start(c.bq[:, :], c.dram["bq"]).then_inc(rest_in, 16)
            act.dma_start(c.bk[:, :], c.dram["bk"]).then_inc(rest_in, 16)
            act.dma_start(c.bv[:, :], c.dram["bv"]).then_inc(rest_in, 16)
            act.wait_ge(s_var, 1)
            act.activation(std[:, :], std[:, :], ACT.Sqrt).then_inc(s_std, 1)
            act.wait_ge(wkv_in, 32)
            act.activation(c.wk_hi[:, :, :], w_raw["wk"][:, :, :], ACT.Copy).then_inc(s_whi, 1)
            act.activation(c.wv_hi[:, :, :], w_raw["wv"][:, :, :], ACT.Copy).then_inc(s_whi, 1)
            for k in range(DC):
                act.wait_ge(s_tp, k + 1)
                act.activation(hT[:, k, :], tp[k][:, :], ACT.Copy).then_inc(s_hT, 1)
            act.wait_ge(rest_in, 48)
            for g in range(G):
                act.wait_ge(s_q, g + 1)
                act.activation(c.qT[:, g, :], qp[g][:, :], ACT.Identity, bias=c.bq[:, g:g + 1]).then_inc(s_qT, 1)

        @block.vector
        def _(dve):
            dve.wait_ge(x_in, 16)
            layer_norm(dve, c.x, h, stats, mv, std, rstd, s_stats, s_var, s_std, s_rstd, s_h)
            dve.wait_ge(s_const, 1)
            dve.wait_ge(s_qT, G)
            for j in range(HG):
                rows = slice(HD * j, HD * j + HD)
                dve.tensor_copy(c.qmask[rows, j::HG, :], c.qT[rows, :, :]).then_inc(s_mask, 1)

        @block.tensor
        def _(pe):
            pe.wait_ge(s_ident, 2)
            pe.wait_ge(s_h, NT)
            for k in range(DC):
                for t in range(NT):
                    mm = pe.transpose(tp[k][:, t * P:(t + 1) * P], h[:, t, k * P:(k + 1) * P], c.ident[:, :])
                mm.then_inc(s_tp, 1)
            pe.wait_ge(w_in, 16)
            pe.wait_ge(s_hT, DC)
            for g in range(G):
                for k in range(DC):
                    mm = pe.matmul(qp[g][:, :], w_raw["wq"][:, k, g * P:(g + 1) * P], hT[:, k, :],
                                   start=(k == 0), stop=(k == DC - 1))
                mm.then_inc(s_q, 1)


def layer_norm(dve, x, h, stats, mv, std, rstd, s_stats, s_var, s_std, s_rstd, s_h):
    for t in range(NT):
        dve.bn_stats(stats[:, t, :], x[:, t, :]).then_inc(s_stats, 1)
    for t in range(NT):
        dve.wait_ge(s_stats, t + 1)
        dve.bn_aggr(mv[:, t, :], stats[:, t, :]).then_inc(s_stats, 1)
    dve.wait_ge(s_stats, 2 * NT)
    dve.tensor_scalar(std[:, :], mv[:, :, 1], EPS, None, ALU.add).then_inc(s_var, 1)
    dve.wait_ge(s_std, 1)
    dve.reciprocal(rstd[:, :], std[:, :]).then_inc(s_rstd, 1)
    dve.wait_ge(s_rstd, 1)
    for t in range(NT):
        dve.tensor_scalar(h[:, t, :], x[:, t, :], mv[:, t, 0:1], rstd[:, t:t + 1],
                          ALU.subtract, ALU.mult).then_inc(s_h, 1)


def project_context(nc, c):
    PRIME_LO, PRIME_V, PRIME_EV, PRIME_OUT, PRIME_ST, PRIME_CP, PRIME_R, PRIME_M = 1, 8, 4, 16, 1, 1, 18, 1
    PAIRS = 2
    with ExitStack() as stack:
        sb, pb, sem = allocators(nc, stack, "ctx")
        raw = sb("raw", [P, DC, CH])
        hi = [sb(f"hi{b}", [P, DC, CH], F32R) for b in range(2)]
        lo = [sb(f"lo{b}", [P, DC, CH], F32R) for b in range(2)]
        k_hi = [sb(f"k_hi{b}", [P, G, CH], F32R) for b in range(2)]
        k_lo = sb("k_lo", [P, G, CH], F32R)
        v = sb("v", [P, G, KT, P])
        run = sb("run", [P, H, 2 * CH], BF16)
        half = sb("half", [P, 2, 2 * CH], BF16)
        st = sb("st", [P, H, 2])
        best = sb("best", [P, H, 2])
        proj = [pb(f"proj{i}", [P, CH]) for i in range(4)]
        sc = [pb(f"sc{i}", [P, 2 * CH]) for i in range(2)]
        ctx_in, s_turn, s_hi, s_lo = sem("ctx_in"), sem("turn"), sem("hi"), sem("lo")
        k_proj, v_proj, k_hi_done, k_lo_done, v_done = (
            sem(n) for n in ("k_proj", "v_proj", "k_hi_done", "k_lo_done", "v_done"))
        k_hi_out = [sem(f"k_hi_out{b}") for b in range(2)]
        k_lo_out, v_out = sem("k_lo_out"), sem("v_out")
        sc_ready = [sem(f"sc_ready{i}") for i in range(2)]
        s_st, s_copied, s_run, s_best = sem("st"), sem("copied"), sem("run"), sem("best")
        s_tree, s_neg, s_neg_hi = sem("tree"), sem("neg"), sem("neg_hi")
        block = stack.enter_context(nc.Block())

        @block.sync
        def _(sp):
            sp.sem_inc(k_hi_out[0], PRIME_OUT)
            sp.sem_inc(k_hi_out[1], PRIME_OUT)
            sp.sem_inc(k_lo_out, PRIME_OUT)
            sp.sem_inc(v_out, PRIME_OUT)

            def load(n):
                sp.wait_ge(s_lo, n + PRIME_LO)
                sp.dma_start(raw[:, :, :], c.dram["ctx"][n]).then_inc(ctx_in, 16)

            def store(n, b):
                sp.wait_ge(k_hi_done, G * n + G)
                sp.dma_start(c.k_dram[n, :, 0].rearrange("g p k -> p g k"), f32(k_hi[b][:, :, :])).then_inc(k_hi_out[b], 16)
                sp.wait_ge(k_lo_done, G * n + G)
                sp.dma_start(c.k_dram[n, :, 1].rearrange("g p k -> p g k"), f32(k_lo[:, :, :])).then_inc(k_lo_out, 16)
                sp.wait_ge(v_done, KT * n + KT + PRIME_EV)
                sp.dma_start(c.v_dram[n].rearrange("g p t d -> p g t d"), v[:, :, :, :]).then_inc(v_out, 16)

            load(0)
            with sp.Fori(0, NCH // 2 - 1) as i:
                for b in range(2):
                    load(2 * i + b + 1)
                    store(2 * i + b, b)
            load(NCH - 1)
            store(NCH - 2, 0)
            store(NCH - 1, 1)
            sp.wait_ge(k_hi_out[0], 16 * (NCH // 2) + PRIME_OUT)
            sp.wait_ge(k_hi_out[1], 16 * (NCH // 2) + PRIME_OUT)
            sp.wait_ge(k_lo_out, 16 * NCH + PRIME_OUT)
            sp.wait_ge(v_out, 16 * NCH + PRIME_OUT)

        @block.gpsimd
        def _(pool):
            pool.sem_inc(s_lo, PRIME_LO)
            with pool.Fori(0, NCH // 2) as i:
                for b in range(2):
                    n = 2 * i + b
                    pool.wait_ge(ctx_in, 16 * n + 16)
                    pool.wait_ge(v_proj, KT * (n - 1) + PRIME_V)
                    pool.sem_inc(s_turn, 1)
                    pool.tensor_copy(hi[b][:, :, :], raw[:, :, :]).then_inc(s_hi, 1)
                    pool.wait_ge(s_hi, n + 1)
                    pool.tensor_tensor(lo[b][:, :, :], raw[:, :, :], f32(hi[b][:, :, :]), ALU.subtract).then_inc(s_lo, 1)

        @block.tensor
        def _(pe):
            pe.sem_inc(v_proj, PRIME_V)

            def keys(n, b, g, part):
                if part == 0:
                    if g == 0:
                        pe.wait_ge(s_lo, n + 1 + PRIME_LO)
                    pe.wait_ge(v_done, KT * (n - 1) + g + 1 + PRIME_EV)
                ks = range(DC // 2 * part, DC // 2 * part + DC // 2)
                mm = split_product(pe, proj[g][:, :],
                                   [(c.wk_hi[:, k, g * P:(g + 1) * P], c.wk_lo[:, k, g * P:(g + 1) * P]) for k in ks],
                                   [(hi[b][:, k, :], lo[b][:, k, :]) for k in ks], first=(part == 0), last=(part == 1))
                if part == 1:
                    mm.then_inc(k_proj, 1)

            def values(n, b, t, part):
                if part == 0:
                    pe.wait_ge(k_lo_done, G * n + t + 1)
                ks = range(DC // 2 * part, DC // 2 * part + DC // 2)
                mm = split_product(pe, proj[t][:, :],
                                   [(hi[b][:, k, t * P:(t + 1) * P], lo[b][:, k, t * P:(t + 1) * P]) for k in ks],
                                   [(c.wv_hi[:, k, :], c.wv_lo[:, k, :]) for k in ks], first=(part == 0), last=(part == 1))
                if part == 1:
                    mm.then_inc(v_proj, 1)

            def scores(n, b, h):
                if h % HG == 0:
                    pe.wait_ge(k_hi_done, G * n + h // HG + 1)
                for s in range(PAIRS):
                    if s == 0:
                        pe.wait_ge(s_st, H * n + h - 1 + 1 + PRIME_ST)
                    else:
                        pe.wait_ge(s_copied, H * n + h - 1 + 1 + PRIME_CP)
                    for q in range(2):
                        at = (2 * s + q) * P
                        mm = pe.matmul(sc[s][:, q * CH:(q + 1) * CH], c.qmask[:, h, at:at + P],
                                       k_hi[b][:, h // HG, :], start=True, stop=True)
                    mm.then_inc(sc_ready[s], 1)

            def chunk(n, b, last=False):
                for h in range(H):
                    scores(n, b, h)
                    if h < 2 * KT:
                        values(n, b, h // 2, h % 2)
                    elif not last:
                        keys(n + 1, 1 - b, h // 2 - KT, h % 2)

            for g in range(G):
                for part in range(2):
                    keys(0, 0, g, part)
            with pe.Fori(0, NCH // 2 - 1) as i:
                for b in range(2):
                    chunk(2 * i + b, b)
            chunk(NCH - 2, 0)
            chunk(NCH - 1, 1, last=True)

        @block.scalar
        def _(act):
            act.sem_inc(v_done, PRIME_EV)
            act.sem_inc(s_copied, PRIME_CP)

            def keys(n, b, g):
                if g == 0:
                    act.wait_ge(k_hi_out[b], 8 * (n - b) + PRIME_OUT)
                act.wait_ge(k_proj, G * n + g + 1)
                act.activation(k_hi[b][:, g, :], proj[g][:, :], ACT.Identity, bias=c.bk[:, g:g + 1]).then_inc(k_hi_done, 1)

            def values(n, t):
                if t == 0:
                    act.wait_ge(v_out, 16 * n + PRIME_OUT)
                act.wait_ge(v_proj, KT * n + t + 1 + PRIME_V)
                act.activation(v[:, :, t, :], proj[t][:, :].rearrange("p (g d) -> p g d", g=G), ACT.Copy).then_inc(v_done, 1)

            def copy(n, h):
                act.wait_ge(sc_ready[1], H * n + h + 1)
                act.wait_ge(s_run, H * n + h - 2 + 1 + PRIME_R)
                act.activation(half[:, h % 2, :], sc[1][:, :], ACT.Copy).then_inc(s_copied, 1)

            def chunk(n, b, last=False):
                for h in range(H):
                    copy(n, h)
                    if h % 2 and h < 2 * KT:
                        values(n, h // 2)
                    elif h % 2 and not last:
                        keys(n + 1, 1 - b, h // 2 - KT)

            for g in range(G):
                keys(0, 0, g)
            with act.Fori(0, NCH // 2 - 1) as i:
                for b in range(2):
                    chunk(2 * i + b, b)
            chunk(NCH - 2, 0)
            chunk(NCH - 1, 1, last=True)

        @block.vector
        def _(dve):
            dve.memset(run[:, :, :], NEG).then_inc(s_run, 1)
            dve.memset(best[:, :, :], NEG).then_inc(s_best, PRIME_M)
            dve.wait_ge(s_run, 1)
            dve.sem_inc(s_run, PRIME_R - 1)
            dve.sem_inc(s_st, PRIME_ST)

            def merge(n, h):
                dve.wait_ge(s_copied, H * n + h + 1 + PRIME_CP)
                dve.wait_ge(s_run, H * (n - 1) + h + 1 + PRIME_R)
                dve.tensor_tensor(run[:, h, :], run[:, h, :], half[:, h % 2, :], ALU.max).then_inc(s_run, 1)

            def keys(n, b, g):
                if g == 0:
                    dve.wait_ge(k_lo_out, 16 * n + PRIME_OUT)
                dve.wait_ge(k_hi_done, G * n + g + 1)
                dve.scalar_tensor_tensor(out=k_lo[:, g, :], in0=proj[g][:, :], scalar=c.bk[:, g:g + 1],
                                         in1=f32(k_hi[b][:, g, :]), op0=ALU.add, op1=ALU.subtract).then_inc(k_lo_done, 1)

            def chunk(n, b, last=False):
                dve.wait_ge(s_best, n + PRIME_M)
                for h in range(H):
                    dve.wait_ge(sc_ready[0], H * n + h + 1)
                    dve.tensor_reduce(st[:, h, :], sc[0][:, :].rearrange("p (q k) -> p q k", q=2), AX.X, ALU.max).then_inc(s_st, 1)
                    if h >= 1:
                        merge(n, h - 1)
                    if h >= 2 * KT + 2 and h % 2 == 0 and not last:
                        keys(n + 1, 1 - b, h // 2 - KT - 1)
                merge(n, H - 1)
                if not last:
                    keys(n + 1, 1 - b, G - 1)
                dve.wait_ge(s_st, H * n + H + PRIME_ST)
                dve.tensor_tensor(best[:, :, :], best[:, :, :], st[:, :, :], ALU.max).then_inc(s_best, 1)

            for g in range(G):
                keys(0, 0, g)
            with dve.Fori(0, NCH // 2 - 1) as i:
                for b in range(2):
                    chunk(2 * i + b, b)
            chunk(NCH - 2, 0)
            chunk(NCH - 1, 1, last=True)

            dve.wait_ge(s_run, H * NCH + PRIME_R)
            view = run[:, :, :].rearrange("p h (q k) -> p (h q) k", q=2)
            width, steps = CH // 2, 0
            while width >= 32:
                if steps:
                    dve.wait_ge(s_tree, steps)
                dve.tensor_tensor(view[:, :, 0:width], view[:, :, 0:width], view[:, :, width:2 * width], ALU.max).then_inc(s_tree, 1)
                steps += 1
                width //= 2
            dve.wait_ge(s_tree, steps)
            dve.tensor_reduce(c.neg[:, :, 2:4], view[:, :, 0:2 * width].rearrange("p (h q) k -> p h q k", q=2), AX.X, ALU.max).then_inc(s_tree, 1)
            dve.wait_ge(s_best, NCH + PRIME_M)
            dve.tensor_copy(c.neg[:, :, 0:2], best[:, :, :]).then_inc(s_tree, 1)
            dve.wait_ge(s_tree, steps + 2)


def stack_queries(nc, c):
    with ExitStack() as stack:
        sb, pb, sem = allocators(nc, stack, "stq")
        q_hi = sb("q_hi", [P, G, N], F32R)
        q_lo = sb("q_lo", [P, G, N], F32R)
        shift = sb("shift", [P, MROW + 2 * H * NT])
        shift_hi = sb("shift_hi", [P, H * NT], F32R)
        rows = [pb(f"rows{i}", [P, N]) for i in range(4)]
        block = stack.enter_context(nc.Block())
        maximum_rows(nc, block, c, sem, c.neg, shift, shift_hi, rows, c.qst)
        s_hi, s_lo, s_copy_act, s_copy_dve = sem("hi"), sem("lo"), sem("copy_act"), sem("copy_dve")
        w_in = sem("w_in")

        @block.sync
        def _(sp):
            sp.dma_start(c.woT[:, :, :], c.dram["WoT"].rearrange("(k p) o -> p k o", p=P)).then_inc(w_in, 16)
            sp.wait_ge(w_in, 16)

        @block.gpsimd
        def _(pool):
            pool.wait_ge(s_hi, 1)
            pool.tensor_tensor(q_lo[:, :, :], c.qT[:, :, :], f32(q_hi[:, :, :]), ALU.subtract).then_inc(s_lo, 1)

        @block.scalar
        def _(act):
            act.activation(q_hi[:, :, :], c.qT[:, :, :], ACT.Copy).then_inc(s_hi, 1)
            act.wait_ge(s_hi, 1)
            stack_copies(act, c.qst, f32(q_hi[:, :, :]), 0, s_copy_act)
            act.wait_ge(s_lo, 1)
            stack_copies(act, c.qst, f32(q_lo[:, :, :]), 2, s_copy_act)
            act.wait_ge(s_copy_act, 2 * HG)

        @block.vector
        def _(dve):
            dve.wait_ge(s_hi, 1)
            stack_copies(dve, c.qst, f32(q_hi[:, :, :]), 1, s_copy_dve)
            dve.wait_ge(s_copy_dve, HG)


def stack_copies(engine, stacks, part, place, s_copy):
    for j in range(HG):
        src, dst = part[HD * j:HD * j + HD, :, :], stacks[HD * place:HD * place + HD, j::HG, :]
        if engine.engine == mybir.EngineType.Activation:
            engine.activation(dst, src, ACT.Copy).then_inc(s_copy, 1)
        else:
            engine.tensor_copy(dst, src).then_inc(s_copy, 1)


def maximum_rows(nc, block, c, sem, best, shift, shift_hi, rows, stacks):
    s_set, s_t, s_row = sem("set"), sem("turned"), sem("row")
    COUNT = H * NT

    @block.vector
    def _(dve):
        flat = best[:, :, :].rearrange("p h t -> p (h t)")
        parts = shift[:, MROW:].rearrange("p (i two) -> p i two", two=2)
        dve.memset(shift[:, 0:MROW], 0.0).then_inc(s_set, 1)
        dve.tensor_scalar(shift_hi[:, :], flat, -1.0, None, ALU.mult).then_inc(s_set, 1)
        dve.wait_ge(s_set, 2)
        dve.tensor_copy(parts[:, :, 0], f32(shift_hi[:, :])).then_inc(s_set, 1)
        dve.scalar_tensor_tensor(out=parts[:, :, 1], in0=flat, scalar=-1.0, in1=f32(shift_hi[:, :]),
                                 op0=ALU.mult, op1=ALU.subtract).then_inc(s_set, 1)
        for h in range(H):
            dve.wait_ge(s_t, h + 1)
            dve.tensor_copy(stacks[MROW:MROW + 2, h, :], rows[h % 4][MROW:MROW + 2, :]).then_inc(s_row, 1)
        dve.wait_ge(s_row, H)

    @block.tensor
    def _(pe):
        pe.wait_ge(s_set, 4)
        for h in range(H):
            if h >= 4:
                pe.wait_ge(s_row, h - 3)
            for t in range(NT):
                i = h * NT + t
                mm = pe.transpose(rows[h % 4][0:MROW + 2, t * P:(t + 1) * P], shift[:, 2 * i:2 * i + MROW + 2], c.ident[:, :])
            mm.then_inc(s_t, 1)


def attend_context(nc, c):
    CHUNKS = 3
    BODY = CHUNKS * KT
    TILES = NCH * KT
    LOOPS = NCH // CHUNKS
    REST = TILES - LOOPS * BODY
    RING = UNIT = BODY // 2
    PAIRS = 3
    UNITS = 2 * LOOPS + 1

    def added(u):
        return (UNIT - 1) * (u // UNIT) + max(u % UNIT, 1)

    ADDS = added(TILES - 1)
    with ExitStack() as stack:
        sb, pb, sem = allocators(nc, stack, "att")
        kst = [sb(f"kst{b}", [STK + 2, HG, CH], F32R) for b in range(CHUNKS)]
        val = [sb(f"val{b}", [P, KT, P]) for b in range(CHUNKS)]
        pr = sb("pr", [P, RING, HG, N])
        tot = [sb(f"tot{b}", [P, HG, N]) for b in range(2)]
        rs = sb("rs", [P, N])
        whole = sb("whole", [P, N])
        sc = [pb(f"sc{s}", [P, 2 * N]) for s in range(PAIRS)]
        o, den = pb("o", [P, N]), pb("den", [P, N])
        k_in = [sem(f"k_in{b}") for b in range(CHUNKS)]
        v_in = [sem(f"v_in{b}") for b in range(CHUNKS)]
        s_ones, s_sc, s_exp, s_pv, s_add, s_sum, s_whole = (
            sem(n) for n in ("ones", "sc", "exp", "pv", "add", "sum", "whole"))
        s_rs, s_norm, s_out = sem("rs"), sem("norm"), sem("out")
        block = stack.enter_context(nc.Block())

        @block.gpsimd
        def _(pool):
            for b in range(CHUNKS):
                pool.memset(f32(kst[b][MROW:MROW + 2, :, :]), 1.0).then_inc(s_ones, 1)

        @block.sync
        def _(sp):
            def load(g, i, m):
                chunk = CHUNKS * i + m
                b = (NCH * g + m) % CHUNKS
                if NCH * g + m >= CHUNKS or not isinstance(i, int):
                    sp.wait_ge(s_sc, 2 * KT * (NCH * g + chunk - CHUNKS + 1))
                for row, part in ((0, 0), (1, 1), (2, 0)):
                    sp.dma_start(f32(kst[b][HD * row:HD * row + HD, :, :]),
                                 c.k_dram[chunk, g, part].rearrange("(j d) k -> d j k", j=HG)).then_inc(k_in[b], 16)
                if NCH * g + m >= CHUNKS or not isinstance(i, int):
                    sp.wait_ge(s_pv, KT * (NCH * g + chunk - CHUNKS + 1))
                sp.dma_start(val[b][:, :, :], c.v_dram[chunk, g]).then_inc(v_in[b], 16)

            for g in range(G):
                for m in range(CHUNKS):
                    load(g, 0, m)
                with sp.Fori(1, LOOPS) as i:
                    for m in range(CHUNKS):
                        load(g, i, m)
                for m in range(CHUNKS * LOOPS, NCH):
                    load(g, 0, m)

        @block.tensor
        def _(pe):
            pe.wait_ge(s_ones, CHUNKS)

            def scores(g, i, pair):
                u, s = divmod(pair, 2)
                m = NCH * g + u // KT
                if u % KT == 0 and s == 0:
                    pe.wait_ge(k_in[m % CHUNKS], 48 * (m // CHUNKS + i + 1))
                place = 2 * TILES * g + pair
                if place >= PAIRS or not isinstance(i, int):
                    pe.wait_ge(s_exp, place + 2 * BODY * i - PAIRS + 1)
                for r in range(2):
                    j = 2 * s + r
                    at = u % KT * P
                    mm = pe.matmul(sc[place % PAIRS][:, r * N:(r + 1) * N], kst[m % CHUNKS][:, j, at:at + P],
                                   c.qst[:, HG * (g + u // TILES) + j, :], start=True, stop=True)
                mm.then_inc(s_sc, 1)

            def weighted(g, i, u, first=False):
                m, T = NCH * g + u // KT, TILES * g + u
                if u % KT == 0:
                    pe.wait_ge(v_in[m % CHUNKS], 16 * (m // CHUNKS + i + 1))
                pe.wait_ge(s_exp, 2 * (T + BODY * i) + 2)
                for j in range(HG):
                    at = slice(HD * j, HD * j + HD)
                    mm = pe.matmul(o[at, :], val[m % CHUNKS][:, u % KT, at], pr[:, T % RING, j, :],
                                   start=first, stop=False, skip_group_check=True)
                mm.then_inc(s_pv, 1)

            def sums(g, i, k):
                pe.wait_ge(s_add, ADDS * g + added(UNIT * k + (REST if k == UNITS - 1 else UNIT) - 1)
                           + 2 * (UNIT - 1) * i)
                for j in range(HG):
                    mm = pe.matmul(den[HD * j:HD * j + HD, :], c.ones[:, :], tot[(UNITS * g + k) % 2][:, j, :],
                                   start=(k == 0 and isinstance(i, int)), stop=False, skip_group_check=True)
                mm.then_inc(s_sum, 1)

            def step(g, i, us, before):
                for u in us:
                    for s in range(2):
                        pair = 2 * u + PAIRS + s
                        if not (g == G - 1 and pair >= 2 * TILES):
                            scores(g, i, pair)
                    first = isinstance(i, int) and u == 0
                    if first and g:
                        pe.wait_ge(s_whole, g)
                    weighted(g, i, u, first)
                    if u % UNIT == 1 and (u > 1 or before):
                        if u > 1:
                            if isinstance(i, int) and u < BODY and g:
                                pe.wait_ge(s_rs, g)
                            sums(g, i, u // UNIT - 1)
                        else:
                            sums(*before)

            for pair in range(PAIRS):
                scores(0, 0, pair)
            for g in range(G):
                step(g, 0, range(BODY), before=(g - 1, 0, UNITS - 1) if g else None)
                with pe.Fori(1, LOOPS) as i:
                    step(g, i, range(BODY), before=(g, i, -1))
                step(g, 0, range(TILES - REST, TILES), before=None)
            sums(G - 1, 0, UNITS - 1)

        @block.scalar
        def _(act):
            def exponentials(g, i, u):
                T = TILES * g + u
                if not isinstance(i, int) or u >= RING:
                    act.wait_ge(s_pv, T + BODY * i - RING + 1)
                    act.wait_ge(s_add, ADDS * g + 2 * (UNIT - 1) * i + added(u) - (UNIT - 1))
                elif g:
                    act.wait_ge(s_pv, T - RING + 1)
                    act.wait_ge(s_add, ADDS * (g - 1) + added(TILES + u - RING))
                for s in range(2):
                    act.wait_ge(s_sc, 2 * (T + BODY * i) + s + 1)
                    act.activation(pr[:, T % RING, 2 * s:2 * s + 2, :],
                                   sc[(2 * T + s) % PAIRS][:, :].rearrange("p (j q) -> p j q", j=2), ACT.Exp,
                                   scale=SCALE).then_inc(s_exp, 1)

            for g in range(G):
                for u in range(BODY):
                    exponentials(g, 0, u)
                with act.Fori(1, LOOPS) as i:
                    for u in range(BODY):
                        exponentials(g, i, u)
                for u in range(TILES - REST, TILES):
                    exponentials(g, 0, u)

        @block.vector
        def _(dve):
            def add(g, i, u):
                v, unit = u % UNIT, UNITS * g + u // UNIT
                if v == 0:
                    return
                total = tot[unit % 2]
                dve.wait_ge(s_exp, 2 * (TILES * g + u + BODY * i) + 2)
                if v == 1:
                    if unit >= 2 or not isinstance(i, int):
                        dve.wait_ge(s_sum, unit + 2 * i - 1)
                    so_far = pr[:, (TILES * g + u - 1) % RING, :, :]
                else:
                    dve.wait_ge(s_add, ADDS * g + 2 * (UNIT - 1) * i + added(u) - 1)
                    so_far = total[:, :, :]
                dve.tensor_tensor(total[:, :, :], so_far, pr[:, (TILES * g + u) % RING, :, :], ALU.add).then_inc(s_add, 1)

            def normalise(g):
                dve.wait_ge(s_sum, UNITS * (g + 1))
                dve.reciprocal(rs[:, :], den[:, :]).then_inc(s_rs, 1)
                dve.wait_ge(s_rs, g + 1)
                dve.wait_ge(s_whole, g + 1)
                dve.tensor_tensor(c.aoT[:, g, :], whole[:, :], rs[:, :], ALU.mult).then_inc(s_norm, 1)
                dve.wait_ge(s_norm, g + 1)
                dve.tensor_scalar(c.aoT[:, g, :], c.aoT[:, g, :], c.bv[:, g:g + 1], None, ALU.add).then_inc(s_out, 1)

            for g in range(G):
                for u in range(BODY):
                    add(g, 0, u)
                    if u == UNIT // 2 and g:
                        normalise(g - 1)
                with dve.Fori(1, LOOPS) as i:
                    for u in range(BODY):
                        add(g, i, u)
                for u in range(TILES - REST, TILES):
                    add(g, 0, u)
                dve.wait_ge(s_pv, TILES * (g + 1))
                if g:
                    dve.wait_ge(s_norm, g)
                dve.tensor_copy(whole[:, :], o[:, :]).then_inc(s_whole, 1)
            normalise(G - 1)
            dve.wait_ge(s_out, G)


def add_and_normalise(nc, c, name, srcT, w, hT, bias=None):
    with ExitStack() as stack:
        sb, pb, sem = allocators(nc, stack, name)
        stats = sb("stats", [P, NT, 6])
        mv = sb("mv", [P, NT, 2])
        std = sb("std", [P, NT])
        rstd = sb("rstd", [P, NT])
        h = sb("h", [P, NT, D])
        acc = [pb(f"acc{t}", [P, D]) for t in range(NT)]
        tp = pb("tp", [P, DC, N])
        s_mm, s_x, s_stats, s_mv, s_var, s_std, s_rstd, s_h, s_tp, s_hT = (
            sem(n) for n in ("mm", "x", "stats", "mv", "var", "std", "rstd", "h", "tp", "hT"))
        block = stack.enter_context(nc.Block())

        @block.tensor
        def _(pe):
            for t in range(NT):
                if bias is not None:
                    pe.matmul(acc[t][:, :], c.one_row[:, :], bias, start=True, stop=False)
                for k in range(DC):
                    mm = pe.matmul(acc[t][:, :], srcT[:, k, t * P:(t + 1) * P], w[:, k, :],
                                   start=(bias is None and k == 0), stop=(k == DC - 1))
                mm.then_inc(s_mm, 1)
            for t in range(NT):
                pe.wait_ge(s_h, t + 1)
                for k in range(DC):
                    mm = pe.transpose(tp[:, k, t * P:(t + 1) * P], h[:, t, k * P:(k + 1) * P], c.ident[:, :])
            mm.then_inc(s_tp, 1)

        @block.vector
        def _(dve):
            for t in range(NT):
                dve.wait_ge(s_mm, t + 1)
                dve.tensor_tensor(c.x[:, t, :], acc[t][:, :], c.x[:, t, :], ALU.add).then_inc(s_x, 1)
                dve.wait_ge(s_x, t + 1)
                dve.bn_stats(stats[:, t, :], c.x[:, t, :]).then_inc(s_stats, 1)
                dve.wait_ge(s_stats, t + 1)
                dve.bn_aggr(mv[:, t, :], stats[:, t, :]).then_inc(s_mv, 1)
                dve.wait_ge(s_mv, t + 1)
                dve.tensor_scalar(std[:, t:t + 1], mv[:, t, 1:2], EPS, None, ALU.add).then_inc(s_var, 1)
            for t in range(NT):
                dve.wait_ge(s_std, t + 1)
                dve.reciprocal(rstd[:, t:t + 1], std[:, t:t + 1]).then_inc(s_rstd, 1)
                dve.wait_ge(s_rstd, t + 1)
                dve.tensor_scalar(h[:, t, :], c.x[:, t, :], mv[:, t, 0:1], rstd[:, t:t + 1],
                                  ALU.subtract, ALU.mult).then_inc(s_h, 1)
            for k in range(DC // 2):
                dve.wait_ge(s_tp, 1)
                dve.tensor_copy(hT[:, k, :], tp[:, k, :]).then_inc(s_h, 1)
            dve.wait_ge(s_h, NT + DC // 2)

        @block.scalar
        def _(act):
            for t in range(NT):
                act.wait_ge(s_var, t + 1)
                act.activation(std[:, t:t + 1], std[:, t:t + 1], ACT.Sqrt).then_inc(s_std, 1)
            act.wait_ge(s_tp, 1)
            for k in range(DC // 2, DC):
                act.activation(hT[:, k, :], tp[:, k, :], ACT.Copy).then_inc(s_hT, 1)
            act.wait_ge(s_hT, DC // 2)


def self_projections(nc, c):
    with ExitStack() as stack:
        sb, pb, sem = allocators(nc, stack, "sp")
        w = {n: sb(n, [P, DC, D]) for n in ("wq", "wk")}
        aff = sb("aff", [P, 4])
        total = sb("total", [P, NT * H])
        mean = sb("mean", [P, NT * H])
        spread = sb("spread", [P, NT * H])
        std = sb("std", [P, NT * H])
        rstd = sb("rstd", [P, NT * H])
        cen = sb("cen", [P, NT, D])
        sq = sb("sq", [P, NT, D])
        nrm = sb("nrm", [P, NT, D])
        full = sb("full", [P, G, N])
        hi = sb("hi", [P, G, N], F32R)
        lo = sb("lo", [P, G, N], F32R)
        raw = pb("raw", [P, NT, D])
        tp = [pb(f"tp{i}", [P, N]) for i in range(G)]
        w_in, aff_in, rest_in = sem("w_in"), sem("aff_in"), sem("rest_in")
        s_raw, s_cen, s_sq, s_var, s_std, s_nrm, s_tp, s_full, s_hi, s_lo, s_copy_act, s_copy_dve, s_v = (
            sem(n) for n in ("raw", "cen", "sq", "var", "std", "nrm", "tp", "full", "hi", "lo", "copy_act", "copy_dve", "v"))
        s_step = sem("step")
        block = stack.enter_context(nc.Block())
        KINDS = (("wq", c.sqst, 1, 0), ("wk", c.skst, 2, 2))

        def heads(ap):
            return ap.rearrange("p t (h d) -> p (t h) d", d=HD)

        def wide(ap):
            return ap[:, :].unsqueeze(2).broadcast_to([P, NT * H, HD])

        @block.sync
        def _(sp):
            sp.dma_start(w["wq"][:, :, :], c.dram["sWqT"].rearrange("(k p) o -> p k o", p=P)).then_inc(w_in, 16)
            sp.dma_start(w["wk"][:, :, :], c.dram["sWkT"].rearrange("(k p) o -> p k o", p=P)).then_inc(w_in, 16)
            for j in range(HG):
                sp.dma_start(aff[HD * j:HD * j + HD, :], c.dram["affine"]).then_inc(aff_in, 16)
            sp.dma_start(c.swvT[:, :, :], c.dram["sWvT"].rearrange("(k p) o -> p k o", p=P)).then_inc(c.sv_in, 16)
            sp.dma_start(c.swoT[:, :, :], c.dram["sWoT"].rearrange("(k p) o -> p k o", p=P)).then_inc(c.so_in, 16)
            sp.wait_ge(c.so_in, 16)

        @block.tensor
        def _(pe):
            pe.wait_ge(w_in, 32)
            for n, (name, *_) in enumerate(KINDS):
                if n:
                    pe.wait_ge(s_cen, n)
                for t in range(NT):
                    for k in range(DC):
                        mm = pe.matmul(raw[:, t, :], c.hT[:, k, t * P:(t + 1) * P], w[name][:, k, :],
                                       start=(k == 0), stop=(k == DC - 1))
                mm.then_inc(s_raw, 1)
                pe.wait_ge(s_nrm, n + 1)
                for g in range(G):
                    if n:
                        pe.wait_ge(s_full, G * (n - 1) + g + 1)
                    for t in range(NT):
                        mm = pe.transpose(tp[g][:, t * P:(t + 1) * P], nrm[:, t, g * P:(g + 1) * P], c.ident[:, :])
                    mm.then_inc(s_tp, 1)
            pe.wait_ge(c.sv_in, 16)
            for t in range(NT):
                for k in range(DC):
                    mm = pe.matmul(raw[:, t, :], c.hT[:, k, t * P:(t + 1) * P], c.swvT[:, k, :],
                                   start=(k == 0), stop=(k == DC - 1))
            mm.then_inc(s_v, 1)

        @block.vector
        def _(dve):
            steps = 0

            def step(instruction):
                nonlocal steps
                steps += 1
                instruction.then_inc(s_step, 1)
                dve.wait_ge(s_step, steps)

            for n, (name, stacks, second_hi, col) in enumerate(KINDS):
                dve.wait_ge(s_raw, n + 1)
                step(dve.tensor_reduce(total[:, :], heads(raw[:, :, :]), AX.X, ALU.add))
                step(dve.tensor_scalar(mean[:, :], total[:, :], 1.0 / HD, None, ALU.mult))
                dve.tensor_tensor(heads(cen[:, :, :]), heads(raw[:, :, :]), wide(mean), ALU.subtract).then_inc(s_cen, 1)
                dve.wait_ge(s_sq, n + 1)
                step(dve.tensor_reduce(spread[:, :], heads(sq[:, :, :]), AX.X, ALU.add))
                dve.tensor_scalar(std[:, :], spread[:, :], 1.0 / HD, EPS, ALU.mult, ALU.add).then_inc(s_var, 1)
                dve.wait_ge(s_std, n + 1)
                step(dve.reciprocal(rstd[:, :], std[:, :]))
                if n:
                    dve.wait_ge(s_tp, G * n)
                dve.tensor_tensor(heads(nrm[:, :, :]), heads(cen[:, :, :]), wide(rstd), ALU.mult).then_inc(s_nrm, 1)
                dve.wait_ge(s_full, G * (n + 1))
                if n:
                    dve.wait_ge(s_copy_act, 2 * HG * n)
                    dve.wait_ge(s_copy_dve, HG * n)
                dve.tensor_copy(hi[:, :, :], full[:, :, :]).then_inc(s_hi, 1)
                dve.wait_ge(s_hi, n + 1)
                dve.tensor_tensor(lo[:, :, :], full[:, :, :], f32(hi[:, :, :]), ALU.subtract).then_inc(s_lo, 1)
                dve.wait_ge(s_lo, n + 1)
                stack_copies(dve, stacks, f32(hi[:, :, :]), 0, s_copy_dve)
            dve.wait_ge(s_v, 1)
            step(dve.tensor_copy(c.sval[:, :, :], raw[:, :, :]))
            dve.wait_ge(s_copy_dve, 2 * HG)

        @block.scalar
        def _(act):
            for n, (name, stacks, second_hi, col) in enumerate(KINDS):
                act.wait_ge(s_cen, n + 1)
                act.activation(sq[:, :, :], cen[:, :, :], ACT.Square).then_inc(s_sq, 1)
                act.wait_ge(s_var, n + 1)
                act.activation(std[:, :], std[:, :], ACT.Sqrt).then_inc(s_std, 1)
                act.wait_ge(aff_in, 16 * HG)
                if n:
                    act.wait_ge(s_lo, n)
                for g in range(G):
                    act.wait_ge(s_tp, G * n + g + 1)
                    act.activation(full[:, g, :], tp[g][:, :], ACT.Identity, scale=aff[:, col:col + 1],
                                   bias=aff[:, col + 1:col + 2]).then_inc(s_full, 1)
                act.wait_ge(s_lo, n + 1)
                for place in (1, 2):
                    part = hi if place == second_hi else lo
                    stack_copies(act, stacks, f32(part[:, :, :]), place, s_copy_act)

        @block.gpsimd
        def _(pool):
            pool.memset(f32(c.skst[MROW:MROW + 2, :, :]), 1.0).then_inc(rest_in, 1)
            pool.wait_ge(rest_in, 1)


def self_attend(nc, c):
    STEPS = HG * NT
    with ExitStack() as stack:
        sb, pb, sem = allocators(nc, stack, "sa")
        shift = sb("shift", [P, MROW + 2 * H * NT])
        shift_hi = sb("shift_hi", [P, H * NT], F32R)
        pr = sb("pr", [P, 2, HG, N])
        rs = sb("rs", [P, N])
        full = [pb(f"full{i}", [P, N]) for i in range(2)]
        rows = pb("rows", [P, N])
        sc = [pb(f"sc{i}", [P, N]) for i in range(3)]
        o = pb("o", [P, N])
        den = pb("den", [P, N])
        s_full, s_max, s_set, s_hi, s_parts, s_t, s_row, s_sc, s_exp, s_pv, s_rs, s_out = (
            sem(n) for n in ("full", "max", "set", "hi", "parts", "t", "row", "sc", "exp", "pv", "rs", "out"))
        block = stack.enter_context(nc.Block())

        @block.tensor
        def _(pe):
            def whole(i):
                if i >= 2:
                    pe.wait_ge(s_max, i - 1)
                h, t = divmod(i, NT)
                pe.matmul(full[i % 2][:, :], c.sqst[0:STK, h, t * P:(t + 1) * P], c.skst[0:STK, h, :],
                          start=True, stop=True).then_inc(s_full, 1)

            def turn(h):
                if h % HG == 0:
                    pe.wait_ge(s_parts, 2 * (h // HG) + 2)
                if h >= 1:
                    pe.wait_ge(s_row, h)
                for t in range(NT):
                    i = h * NT + t
                    mm = pe.transpose(rows[0:MROW + 2, t * P:(t + 1) * P], shift[:, 2 * i:2 * i + MROW + 2], c.ident[:, :])
                mm.then_inc(s_t, 1)

            def scores(i):
                g, u, j = i // STEPS, i // HG % NT, i % HG
                if i >= 3:
                    pe.wait_ge(s_exp, i - 2)
                pe.matmul(sc[i % 3][:, :], c.skst[:, HG * g + j, u * P:(u + 1) * P],
                          c.sqst[:, HG * g + j, :], start=True, stop=True).then_inc(s_sc, 1)

            def weighted(T):
                g, u = divmod(T, NT)
                pe.wait_ge(s_exp, HG * T + HG)
                if u == 0 and g >= 1:
                    pe.wait_ge(s_out, g)
                for j in range(HG):
                    at = slice(HD * j, HD * j + HD)
                    pe.matmul(o[at, :], c.sval[:, u, P * g + HD * j:P * g + HD * j + HD], pr[:, T % 2, j, :],
                              start=(u == 0), stop=(u == NT - 1))
                for j in range(HG):
                    at = slice(HD * j, HD * j + HD)
                    mm = pe.matmul(den[at, :], c.ones[:, :], pr[:, T % 2, j, :], start=(u == 0), stop=(u == NT - 1))
                mm.then_inc(s_pv, 1)

            pe.wait_ge(s_set, 1)
            for i in range(STEPS):
                whole(i)
            for h in range(HG):
                turn(h)
            for g in range(G):
                pe.wait_ge(s_row, HG * (g + 1))
                for i in range(STEPS * g, STEPS * (g + 1)):
                    if g + 1 < G:
                        whole(i + STEPS)
                    scores(i)
                    if i % HG == HG - 1 and i >= 2 * HG - 1:
                        weighted(i // HG - 1)
                if g + 1 < G:
                    for h in range(HG * (g + 1), HG * (g + 2)):
                        turn(h)
            weighted(G * NT - 1)

        @block.scalar
        def _(act):
            def to_rows(g):
                for h in range(HG * g, HG * g + HG):
                    act.wait_ge(s_t, h + 1)
                    act.activation(c.sqst[MROW:MROW + 2, h, :], rows[MROW:MROW + 2, :], ACT.Copy).then_inc(s_row, 1)

            to_rows(0)
            for i in range(STEPS * G):
                T = i // HG
                if i % HG == 0 and T >= 2:
                    act.wait_ge(s_pv, T - 1)
                act.wait_ge(s_sc, i + 1)
                act.activation(pr[:, T % 2, i % HG, :], sc[i % 3][:, :], ACT.Exp, scale=SCALE).then_inc(s_exp, 1)
                if i % STEPS == STEPS - 1 and i + 1 < STEPS * G:
                    to_rows(i // STEPS + 1)

        @block.vector
        def _(dve):
            parts = shift[:, MROW:].rearrange("p (i two) -> p i two", two=2)
            dve.memset(shift[:, 0:MROW], 0.0).then_inc(s_set, 1)

            def normalise(g):
                dve.wait_ge(s_pv, NT * (g + 1))
                if g >= 1:
                    dve.wait_ge(s_out, g)
                dve.reciprocal(rs[:, :], den[:, :]).then_inc(s_rs, 1)
                dve.wait_ge(s_rs, g + 1)
                dve.tensor_tensor(c.aoT[:, g, :], o[:, :], rs[:, :], ALU.mult).then_inc(s_out, 1)

            for g in range(G):
                for i in range(STEPS * g, STEPS * g + STEPS):
                    dve.wait_ge(s_full, i + 1)
                    dve.tensor_reduce(c.neg[:, i // NT, i % NT:i % NT + 1], full[i % 2][:, :], AX.X, ALU.max).then_inc(s_max, 1)
                    if i == STEPS * g + HG + 2 and g >= 2:
                        normalise(g - 2)
                at = slice(STEPS * g, STEPS * g + STEPS)
                best = c.neg[:, HG * g:HG * g + HG, :].rearrange("p h t -> p (h t)")
                dve.wait_ge(s_max, STEPS * (g + 1))
                dve.tensor_scalar(shift_hi[:, at], best, -1.0, None, ALU.mult).then_inc(s_hi, 1)
                dve.wait_ge(s_hi, g + 1)
                dve.tensor_copy(parts[:, at, 0], f32(shift_hi[:, at])).then_inc(s_parts, 1)
                dve.scalar_tensor_tensor(out=parts[:, at, 1], in0=best, scalar=-1.0, in1=f32(shift_hi[:, at]),
                                         op0=ALU.mult, op1=ALU.subtract).then_inc(s_parts, 1)
            for g in (G - 2, G - 1):
                normalise(g)
            dve.wait_ge(s_out, G)


def sparse_mix(nc, c):
    with ExitStack() as stack:
        sb, pb, sem = allocators(nc, stack, "mix")
        wv = sb("wv", [P, H, TOPM])
        wo = sb("wo", [P, HD, TOPM])
        vm = sb("vm", [P, H])
        om = sb("om", [P, HD])
        bv = sb("bv", [P, HG * H])
        bo = sb("bo", [P, HG, HD])
        flat = sb("flat", [P, G, N])
        z = sb("z", [P, 2, N])
        left = sb("left", [P, 2, N])
        top = sb("top", [P, 2, 8])
        zs = sb("zs", [P, 2, N])
        zp = [pb(f"zp{i}", [P, N]) for i in range(2)]
        yp = [pb(f"yp{g}", [P, N]) for g in range(G)]
        w_in, s_zero, s_vm, s_om, s_bv, s_bo, s_zp, s_z, s_zs, s_y, s_yT = (
            sem(n) for n in ("w_in", "zero", "vm", "om", "bv", "bo", "zp", "z", "zs", "y", "yT"))
        s_top, s_left, s_flat_act, s_flat_dve = sem("top"), sem("left"), sem("flat_act"), sem("flat_dve")
        block = stack.enter_context(nc.Block())

        def regroup(j, i):
            rows_per_block = N // H
            dst = flat[HD * i:HD * i + HD, :, :].rearrange("d b (t g j) -> d b t g j", g=G, j=HG)[:, :, :, :, j]
            src = c.aoT[HD * j:HD * j + HD, :, :].rearrange("d g (b i t) -> d b i t g", i=HG, t=rows_per_block)[:, :, i, :, :]
            return dst, src

        @block.sync
        def _(sp):
            for j in range(HG):
                sp.dma_start(wv[HD * j:HD * j + HD, :, :], c.dram["spVT"]).then_inc(w_in, 16)
            for j in range(2 * HG):
                sp.dma_start(wo[H * j:H * j + H, :, :], c.dram["spOT"]).then_inc(w_in, 16)

        @block.gpsimd
        def _(pool):
            pool.memset(bv[:, :], 0.0).then_inc(s_zero, 1)
            pool.wait_ge(s_om, 2)
            for half in range(2):
                rows = slice(64 * half, 64 * half + 64)
                pool.tensor_copy(bo[rows, :, :], om[rows, :].unsqueeze(1).broadcast_to([64, HG, HD])).then_inc(s_bo, 1)
                pool.wait_ge(s_bo, 3 * half + 1)
                pool.affine_select(out=bo[rows, :, :], in_=bo[rows, :, :], compare_op=ALU.is_ge, fill=0.0, base=0,
                                   pattern=[[-H, HG], [0, HD]], channel_multiplier=1).then_inc(s_bo, 1)
                pool.wait_ge(s_bo, 3 * half + 2)
                pool.affine_select(out=bo[rows, :, :], in_=bo[rows, :, :], compare_op=ALU.is_ge, fill=0.0, base=H - 1,
                                   pattern=[[H, HG], [0, HD]], channel_multiplier=-1).then_inc(s_bo, 1)
            pool.wait_ge(s_bo, 6)

        @block.vector
        def _(dve):
            dve.wait_ge(w_in, 16 * 3 * HG)
            dve.tensor_reduce(vm[:, :], wv[:, :, :], AX.X, ALU.add).then_inc(s_vm, 1)
            dve.tensor_reduce(om[:, :], wo[:, :, :], AX.X, ALU.add).then_inc(s_om, 1)
            dve.wait_ge(s_om, 1)
            dve.tensor_scalar(om[:, :], om[:, :], 1.0 / TOPM, None, ALU.mult).then_inc(s_om, 1)
            dve.wait_ge(s_vm, 1)
            dve.wait_ge(s_zero, 1)
            for j in range(HG):
                rows = slice(HD * j, HD * j + HD)
                dve.tensor_scalar(bv[rows, H * j:H * j + H], vm[rows, :], 1.0 / TOPM, None, ALU.mult).then_inc(s_bv, 1)
            for j in range(HG // 2, HG):
                for i in range(HG):
                    dve.tensor_copy(*regroup(j, i)).then_inc(s_flat_dve, 1)
            for i in range(2):
                dve.wait_ge(s_zp, i + 1)
                dve.tensor_copy(z[:, i, :], zp[i][:, :]).then_inc(s_z, 1)
            for i in range(2):
                dve.wait_ge(s_z, i + 1)
            for r in range(KEEP // 8):
                for i in range(2):
                    rest = z if r == 0 else left
                    if r:
                        dve.wait_ge(s_left, 2 * (r - 1) + i + 1)
                    dve.max(out=top[:, i, :], in_=rest[:, i, :]).then_inc(s_top, 1)
                for i in range(2):
                    rest = z if r == 0 else left
                    dve.wait_ge(s_top, 2 * r + i + 1)
                    dve.match_replace(out=left[:, i, :], in_to_replace=top[:, i, :], in_values=rest[:, i, :],
                                      imm_value=NEG).then_inc(s_left, 1)
            for i in range(2):
                dve.wait_ge(s_left, 2 * (KEEP // 8 - 1) + i + 1)
                dve.scalar_tensor_tensor(out=zs[:, i, :], in0=left[:, i, :], scalar=NEG, in1=z[:, i, :],
                                         op0=ALU.is_equal, op1=ALU.mult).then_inc(s_zs, 1)

        @block.tensor
        def _(pe):
            pe.wait_ge(s_bv, HG)
            pe.wait_ge(s_flat_act, HG * HG // 2)
            pe.wait_ge(s_flat_dve, HG * HG // 2)
            for g in range(G):
                mm = pe.matmul(zp[g // 2][64 * (g % 2):64 * (g % 2) + 64, :], bv[:, :], flat[:, g, :], start=True, stop=True)
                if g % 2:
                    mm.then_inc(s_zp, 1)
            pe.wait_ge(s_bo, 6)
            for g in range(G):
                pe.wait_ge(s_zs, g // 2 + 1)
                rows = slice(64 * (g % 2), 64 * (g % 2) + 64)
                pe.matmul(yp[g][:, :], bo[rows, :, :].rearrange("p j d -> p (j d)"), zs[rows, g // 2, :],
                          start=True, stop=True).then_inc(s_y, 1)

        @block.scalar
        def _(act):
            for j in range(HG // 2):
                for i in range(HG):
                    dst, src = regroup(j, i)
                    act.activation(dst, src, ACT.Copy).then_inc(s_flat_act, 1)

        first_expert(nc, c, block)

        @block.scalar
        def _(act):
            for g in range(G):
                act.wait_ge(s_y, g + 1)
                act.activation(c.yT[:, g, :], yp[g][:, :], ACT.Copy).then_inc(s_yT, 1)
            act.wait_ge(s_yT, G)


def route(nc, c):
    with ExitStack() as stack:
        sb, pb, sem = allocators(nc, stack, "rt")
        wg = sb("wg", [P, DC, E])
        b2 = sb("b2", [E, D])
        iota = sb("iota", [P, E])
        big = sb("big", [P, NT])
        ex = sb("ex", [P, NT, E])
        su = sb("su", [P, NT])
        ri = sb("ri", [P, NT])
        prob = sb("prob", [P, NT, E])
        top = sb("top", [P, NT, 8])
        idx = sb("idx", [P, NT, 8], U32)
        idf = sb("idf", [P, NT, 8])
        m1 = sb("m1", [P, NT, E])
        m2 = sb("m2", [P, NT, E])
        two = sb("two", [P, NT])
        rt = sb("rt", [P, NT])
        scT = sb("scT", [E, N])
        lg = pb("lg", [P, NT, E])
        tp = pb("tp", [P, N])
        ac = [pb(f"ac{t}", [P, D]) for t in range(NT)]
        w_in, s_lg, s_step, s_exp, s_iota, s_score, s_tp, s_scT, s_ac, s_hi = (
            sem(n) for n in ("w_in", "lg", "step", "exp", "iota", "score", "tp", "scT", "ac", "hi"))
        s_sub = sem("sub")
        block = stack.enter_context(nc.Block())

        @block.sync
        def _(sp):
            sp.dma_start(wg[:, :, :], c.dram["Wg"].rearrange("(k p) e -> p k e", p=P)).then_inc(w_in, 16)
            sp.dma_start(b2[:, :], c.dram["b2"]).then_inc(w_in, 16)
            sp.dma_start(c.b1[:, :, :], c.dram["b1"]).then_inc(w_in, 16)
            sp.wait_ge(w_in, 48)

        @block.gpsimd
        def _(pool):
            pool.iota(iota[:, :], pattern=[[1, E]], base=0, channel_multiplier=0,
                      allow_small_or_imprecise_dtypes=True).then_inc(s_iota, 1)

        @block.tensor
        def _(pe):
            pe.wait_ge(w_in, 48)
            for t in range(NT):
                for k in range(DC):
                    mm = pe.matmul(lg[:, t, :], c.hT[:, k, t * P:(t + 1) * P], wg[:, k, :], start=(k == 0), stop=(k == DC - 1))
            mm.then_inc(s_lg, 1)
            pe.wait_ge(s_score, 1)
            for t in range(NT):
                mm = pe.transpose(tp[0:E, t * P:(t + 1) * P], c.score[:, t, :], c.ident[:, :])
            mm.then_inc(s_tp, 1)
            pe.wait_ge(s_scT, 1)
            for t in range(NT):
                pe.matmul(ac[t][:, :], scT[:, t * P:(t + 1) * P], b2[:, :], start=True, stop=True).then_inc(s_ac, 1)

        @block.scalar
        def _(act):
            act.activation(c.hT_hi[:, :, :], c.hT[:, :, :], ACT.Copy).then_inc(s_hi, 1)
            act.wait_ge(s_sub, 1)
            act.activation(ex[:, :, :], ex[:, :, :], ACT.Exp).then_inc(s_exp, 1)
            act.wait_ge(s_tp, 1)
            act.activation(scT[:, :], tp[0:E, :], ACT.Copy).then_inc(s_scT, 1)

        @block.vector
        def _(dve):
            steps = 0

            def step(instruction):
                nonlocal steps
                steps += 1
                instruction.then_inc(s_step, 1)
                dve.wait_ge(s_step, steps)

            def wide(ap, n=E):
                return ap.unsqueeze(2).broadcast_to([P, NT, n])

            dve.wait_ge(s_hi, 1)
            step(dve.tensor_tensor(c.hT_lo[:, :, :], c.hT[:, :, :], f32(c.hT_hi[:, :, :]), ALU.subtract))
            dve.wait_ge(s_lg, 1)
            step(dve.tensor_reduce(big[:, :], lg[:, :, :], AX.X, ALU.max))
            dve.tensor_tensor(ex[:, :, :], lg[:, :, :], wide(big[:, :]), ALU.subtract).then_inc(s_sub, 1)
            dve.wait_ge(s_exp, 1)
            step(dve.tensor_reduce(su[:, :], ex[:, :, :], AX.X, ALU.add))
            step(dve.reciprocal(ri[:, :], su[:, :]))
            step(dve.tensor_tensor(prob[:, :, :], ex[:, :, :], wide(ri[:, :]), ALU.mult))
            for t in range(NT):
                step(dve.max(out=top[:, t, :], in_=prob[:, t, :]))
                step(dve.max_index(out=idx[:, t, :], in_max=top[:, t, :], in_values=prob[:, t, :]))
            step(dve.tensor_copy(idf[:, :, :], idx[:, :, :]))
            dve.wait_ge(s_iota, 1)
            number = iota[:, :].unsqueeze(1).broadcast_to([P, NT, E])
            step(dve.tensor_tensor(m1[:, :, :], number, wide(idf[:, :, 0]), ALU.is_equal))
            step(dve.tensor_tensor(m2[:, :, :], number, wide(idf[:, :, 1]), ALU.is_equal))
            step(dve.tensor_tensor(m1[:, :, :], m1[:, :, :], m2[:, :, :], ALU.add))
            step(dve.tensor_tensor(two[:, :], top[:, :, 0], top[:, :, 1], ALU.add))
            step(dve.reciprocal(rt[:, :], two[:, :]))
            step(dve.tensor_tensor(m2[:, :, :], prob[:, :, :], m1[:, :, :], ALU.mult))
            dve.tensor_tensor(c.score[:, :, :], m2[:, :, :], wide(rt[:, :]), ALU.mult).then_inc(s_score, 1)
            for t in range(NT):
                dve.wait_ge(s_ac, t + 1)
                step(dve.tensor_tensor(c.x[:, t, :], ac[t][:, :], c.x[:, t, :], ALU.add))


def first_expert(nc, c, block):
    @block.sync
    def _(sp):
        sp.dma_start(c.raw1[:, :, :], c.dram["W1"][0].rearrange("(k p) f -> p k f", p=P)).then_inc(c.in1, 16)
        sp.dma_start(c.raw2[:, :, :], c.dram["W2"][0].rearrange("(k p) d -> p k d", p=P)).then_inc(c.in2, 16)

    @block.scalar
    def _(act):
        act.wait_ge(c.in1, 16)
        act.activation(c.w1_hi[:, :, :], c.raw1[:, :, :], ACT.Copy).then_inc(c.s_hi1, 1)
        act.wait_ge(c.in2, 16)
        act.activation(c.w2_hi[:, :, :], c.raw2[:, :, :], ACT.Copy).then_inc(c.s_hi2, 1)

    @block.gpsimd
    def _(pool):
        pool.wait_ge(c.s_hi1, 1)
        pool.tensor_tensor(c.w1_lo[:, :, :], c.raw1[:, :, :], f32(c.w1_hi[:, :, :]), ALU.subtract).then_inc(c.s_lo1, 1)
        pool.wait_ge(c.s_hi2, 1)
        pool.tensor_tensor(c.w2_lo[:, :, :], c.raw2[:, :, :], f32(c.w2_hi[:, :, :]), ALU.subtract).then_inc(c.s_lo2, 1)


def experts(nc, c):
    PRIME = 8
    HALF = 4
    with ExitStack() as stack:
        sb, pb, sem = allocators(nc, stack, "ex")
        raw1, raw2, w1_hi, w1_lo, w2_hi, w2_lo = c.raw1, c.raw2, c.w1_hi, c.w1_lo, c.w2_hi, c.w2_lo
        in1, in2, s_hi1, s_lo1, s_hi2, s_lo2 = c.in1, c.in2, c.s_hi1, c.s_lo1, c.s_hi2, c.s_lo2
        hid = sb("hid", [P, 2, N])
        hid_hi, hid_lo = sb("hid_hi", [P, FC, N], F32R), sb("hid_lo", [P, FC, N], F32R)
        hp = [pb(f"hp{i}", [P, N]) for i in range(HALF)]
        yp = [pb(f"yp{t}", [P, D]) for t in range(NT)]
        s_hp, s_hid, s_hh, s_hl, s_yp, s_acc = (sem(n) for n in ("hp", "hid", "hh", "hl", "yp", "acc"))
        s_done = sem("done")
        block = stack.enter_context(nc.Block())

        @block.sync
        def _(sp):
            with sp.Fori(1, E) as e:
                sp.wait_ge(s_lo1, e)
                sp.dma_start(raw1[:, :, :], c.dram["W1"][e].rearrange("(k p) f -> p k f", p=P)).then_inc(in1, 16)
                sp.wait_ge(s_lo2, e)
                sp.dma_start(raw2[:, :, :], c.dram["W2"][e].rearrange("(k p) d -> p k d", p=P)).then_inc(in2, 16)
            sp.wait_ge(s_acc, NT * E + PRIME)
            sp.dma_start(c.dram["out"].rearrange("(t p) d -> p t d", p=P), c.x[:, :, :]).then_inc(s_done, 16)
            sp.wait_ge(s_done, 16)

        @block.gpsimd
        def _(pool):
            with pool.Fori(1, E) as e:
                pool.wait_ge(s_hi1, e + 1)
                pool.tensor_tensor(w1_lo[:, :, :], raw1[:, :, :], f32(w1_hi[:, :, :]), ALU.subtract).then_inc(s_lo1, 1)
                pool.wait_ge(s_hi2, e + 1)
                pool.tensor_tensor(w2_lo[:, :, :], raw2[:, :, :], f32(w2_hi[:, :, :]), ALU.subtract).then_inc(s_lo2, 1)

        @block.tensor
        def _(pe):
            pe.sem_inc(s_hp, PRIME)
            pe.sem_inc(s_yp, PRIME)
            with pe.Fori(0, E) as e:
                pe.wait_ge(s_lo1, e + 1)
                for f in range(FC):
                    pe.wait_ge(s_hid, FC * e + f - HALF + 1 + PRIME)
                    split_product(pe, hp[f % HALF][:, :],
                                  [(w1_hi[:, k, f * P:(f + 1) * P], w1_lo[:, k, f * P:(f + 1) * P]) for k in range(DC)],
                                  [(c.hT_hi[:, k, :], c.hT_lo[:, k, :]) for k in range(DC)]).then_inc(s_hp, 1)
                pe.wait_ge(s_lo2, e + 1)
                pe.wait_ge(s_hl, FC * e + FC + PRIME)
                for t in range(NT):
                    pe.wait_ge(s_acc, NT * (e - 1) + t + 1 + PRIME)
                    split_product(pe, yp[t][:, :],
                                  [(hid_hi[:, f, t * P:(t + 1) * P], hid_lo[:, f, t * P:(t + 1) * P]) for f in range(FC)],
                                  [(w2_hi[:, f, :], w2_lo[:, f, :]) for f in range(FC)]).then_inc(s_yp, 1)

        @block.scalar
        def _(act):
            act.sem_inc(s_hid, PRIME)

            def hidden(e, b1):
                for f in range(FC):
                    act.wait_ge(s_hp, FC * e + f + 1 + PRIME)
                    act.wait_ge(s_hl, FC * e + f - 2 + 1 + PRIME)
                    act.activation(hid[:, f % 2, :], hp[f % HALF][:, :], ACT.Relu, bias=b1[:, f, :]).then_inc(s_hid, 1)

            hidden(0, c.b1[:, :, 0:1])
            with act.Fori(1, E) as e:
                act.wait_ge(in1, 16 * e + 16)
                act.wait_ge(s_hp, FC * e + PRIME)
                act.activation(w1_hi[:, :, :], raw1[:, :, :], ACT.Copy).then_inc(s_hi1, 1)
                act.wait_ge(in2, 16 * e + 16)
                act.wait_ge(s_yp, NT * e + PRIME)
                act.activation(w2_hi[:, :, :], raw2[:, :, :], ACT.Copy).then_inc(s_hi2, 1)
                hidden(e, c.b1[:, :, bass.ds(e, 1)])

        @block.vector
        def _(dve):
            dve.sem_inc(s_hl, PRIME)
            dve.sem_inc(s_acc, PRIME)
            with dve.Fori(0, E) as e:
                dve.wait_ge(s_yp, NT * e + PRIME)
                for f in range(FC):
                    dve.wait_ge(s_hid, FC * e + f + 1 + PRIME)
                    dve.tensor_copy(hid_hi[:, f, :], hid[:, f % 2, :]).then_inc(s_hh, 1)
                    dve.wait_ge(s_hh, FC * e + f + 1)
                    dve.tensor_tensor(hid_lo[:, f, :], hid[:, f % 2, :], f32(hid_hi[:, f, :]), ALU.subtract).then_inc(s_hl, 1)
                for t in range(NT):
                    dve.wait_ge(s_yp, NT * e + t + 1 + PRIME)
                    dve.wait_ge(s_acc, NT * (e - 1) + t + 1 + PRIME)
                    dve.scalar_tensor_tensor(out=c.x[:, t, :], in0=yp[t][:, :], scalar=c.score[:, t, bass.ds(e, 1)],
                                             in1=c.x[:, t, :], op0=ALU.mult, op1=ALU.add).then_inc(s_acc, 1)


def load_small(nc, c):
    with ExitStack() as stack:
        sb, pb, sem = allocators(nc, stack, "sml")
        s_in, s_set = sem("in"), sem("set")
        block = stack.enter_context(nc.Block())

        @block.sync
        def _(sp):
            sp.dma_start(c.bo[:, :], c.dram["bo"]).then_inc(s_in, 16)
            sp.wait_ge(s_in, 16)

        @block.gpsimd
        def _(pool):
            pool.memset(c.ones[:, :], 1.0).then_inc(s_set, 1)
            pool.memset(c.one_row[:, :], 1.0).then_inc(s_set, 1)
            pool.wait_ge(s_set, 2)


def perceiver_layer(nc, dram):
    c = Ctx()
    c.dram = dram
    c.k_dram = nc.dram_tensor("keys_scratch", [NCH, G, 2, P, CH], F32).ap()
    c.v_dram = nc.dram_tensor("values_scratch", [NCH, G, P, KT, P], F32).ap()
    with ExitStack() as whole:
        sb, pb, sem = allocators(nc, whole, "g")
        c.ident = sb("ident", [P, P])
        c.ones = sb("ones", [P, HD])
        c.one_row = sb("one_row", [1, P])
        c.x = sb("x", [P, NT, D])
        c.hT = sb("hT", [P, DC, N])
        c.bq, c.bk, c.bv = sb("bq", [P, DC]), sb("bk", [P, DC]), sb("bv", [P, DC])
        c.bo = sb("bo", [1, D])
        c.neg = sb("neg", [P, H, NT])
        load_small(nc, c)
        with ExitStack() as cross:
            sb, pb, sem = allocators(nc, cross, "x")
            c.qT = c.hT
            with ExitStack() as first:
                sb, pb, sem = allocators(nc, first, "f")
                c.qmask = sb("qmask", [P, H, N], F32R)
                c.wk_hi, c.wk_lo = sb("wk_hi", [P, DC, D], F32R), sb("wk_lo", [P, DC, D], F32R)
                c.wv_hi, c.wv_lo = sb("wv_hi", [P, DC, D], F32R), sb("wv_lo", [P, DC, D], F32R)
                prepare(nc, c)
                project_context(nc, c)
            with ExitStack() as second:
                sb, pb, sem = allocators(nc, second, "s")
                c.qst = sb("qst", [STK + 2, H, N], F32R)
                c.woT = sb("woT", [P, DC, D])
                c.aoT = sb("aoT", [P, G, N])
                stack_queries(nc, c)
                attend_context(nc, c)
                add_and_normalise(nc, c, "xo", c.aoT, c.woT, c.hT, bias=c.bo[:, :])
        with ExitStack() as own:
            sb, pb, sem = allocators(nc, own, "o")
            c.swoT = sb("swoT", [P, DC, D])
            c.aoT = sb("aoT", [P, G, N])
            c.yT = sb("yT", [P, G, N])
            c.sv_in, c.so_in = sem("sv_in"), sem("so_in")
            with ExitStack() as attention:
                sb, pb, sem = allocators(nc, attention, "a")
                c.sqst = sb("sqst", [STK + 2, H, N], F32R)
                c.skst = sb("skst", [STK + 2, H, N], F32R)
                c.sval = sb("sval", [P, NT, D])
                c.swvT = sb("swvT", [P, DC, D])
                self_projections(nc, c)
                self_attend(nc, c)
            with ExitStack() as ffn:
                sb, pb, sem = allocators(nc, ffn, "m")
                c.raw1, c.raw2 = sb("raw1", [P, DC, FF]), sb("raw2", [P, FC, D])
                c.w1_hi, c.w1_lo = sb("w1_hi", [P, DC, FF], F32R), sb("w1_lo", [P, DC, FF], F32R)
                c.w2_hi, c.w2_lo = sb("w2_hi", [P, FC, D], F32R), sb("w2_lo", [P, FC, D], F32R)
                c.in1, c.in2, c.s_hi1, c.s_lo1, c.s_hi2, c.s_lo2 = (
                    sem(n) for n in ("in1", "in2", "hi1", "lo1", "hi2", "lo2"))
                sparse_mix(nc, c)
                add_and_normalise(nc, c, "so", c.yT, c.swoT, c.hT)
                c.hT_hi, c.hT_lo = sb("hT_hi", [P, DC, N], F32R), sb("hT_lo", [P, DC, N], F32R)
                c.score = sb("score", [P, NT, E])
                c.b1 = sb("b1", [P, FC, E])
                route(nc, c)
                experts(nc, c)


def kernel(**inputs):
    import numpy as _np
    import concourse.bacc as _bacc
    from concourse import mybir as _mybir
    from concourse.bass_utils import run_bass_kernel_spmd as _run

    a = {k: _np.asarray(v) for k, v in inputs.items()}
    keep = _np.ascontiguousarray
    column = lambda b: keep(b.reshape(DC, P).T)
    arrays = {
        "x": keep(a["x"][0]),
        "ctx": keep(a["ctx_1024"][0].reshape(NCH, CH, DC, P).transpose(0, 3, 2, 1)),
        "WqT": keep(a["L0_xattn_Wq"].T), "WkT": keep(a["L0_xattn_Wk"].T),
        "WvT": keep(a["L0_xattn_Wv"].T), "WoT": keep(a["L0_xattn_Wo"].T),
        "bq": column(a["L0_xattn_bq"]), "bk": column(a["L0_xattn_bk"]), "bv": column(a["L0_xattn_bv"]),
        "bo": keep(a["L0_xattn_bo"].reshape(1, D)),
        "sWqT": keep(a["L0_attn_W_Q"].T), "sWkT": keep(a["L0_attn_W_K"].T),
        "sWvT": keep(a["L0_attn_W_V"].T), "sWoT": keep(a["L0_attn_W_O"].T),
        "affine": keep(_np.stack([a["L0_attn_q_ln_w"], a["L0_attn_q_ln_b"], a["L0_attn_k_ln_w"], a["L0_attn_k_ln_b"]], 1)),
        "spVT": keep(a["L0_attn_sparse_W_V"].transpose(1, 0, 2)),
        "spOT": keep(a["L0_attn_sparse_W_O"].transpose(0, 2, 1)),
        "Wg": keep(a["L0_ffn_Wg"]), "W1": keep(a["L0_ffn_W1"]), "W2": keep(a["L0_ffn_W2"]),
        "b1": keep(a["L0_ffn_b1"].reshape(E, FC, P).transpose(2, 1, 0)), "b2": keep(a["L0_ffn_b2"]),
    }
    nc = _bacc.Bacc("TRN2", target_bir_lowering=False, num_devices=1)
    dram = {n: nc.dram_tensor(f"in_{n}", v.shape, _mybir.dt.from_np(v.dtype), kind="ExternalInput").ap()
            for n, v in arrays.items()}
    dram["out"] = nc.dram_tensor("out_0", (N, D), F32, kind="ExternalOutput").ap()
    perceiver_layer(nc, dram)
    r = _run(nc, [{f"in_{n}": v for n, v in arrays.items()}], core_ids=[0])
    return r.results[0]["out_0"].reshape(1, N, D)
```

```python
from contextlib import ExitStack

import concourse.bass as bass
from concourse import mybir

F32 = mybir.dt.float32
F32R = mybir.dt.float32r
BF16 = mybir.dt.bfloat16
U32 = mybir.dt.uint32
ALU = mybir.AluOpType
ACT = mybir.ActivationFunctionType
AX = mybir.AxisListType

P = 128
D = 512
DC = D // P
N = 512
NT = N // P
M = 8192
CH = 512
NCH = M // CH
KT = CH // P
H = 16
HD = D // H
HG = P // HD
G = H // HG
SCALE = HD ** -0.5
EPS = 1e-5
KEEP = 128
TOPM = 128
E = 8
FF = 1024
FC = FF // P
NEG = -3.0e38
STK = 3 * HD
PRIME_LO = 1
MROW = STK


class Ctx:
    pass


def f32(ap):
    return ap.bitcast(F32)


def allocators(nc, stack, tag):
    def sb(name, shape, dt=F32):
        return stack.enter_context(nc.sbuf_tensor(f"{tag}_{name}", shape, dt))

    def pb(name, shape, dt=F32):
        return stack.enter_context(nc.psum_tensor(f"{tag}_{name}", shape, dt))

    def sem(name):
        return stack.enter_context(nc.semaphore(f"{tag}_{name}"))

    return sb, pb, sem


def split_product(pe, out, a, b, last=True, first=True):
    n = len(a)
    for i in range(n):
        (ah, al), (bh, bl) = a[i], b[i]
        pe.matmul(out, ah, bh, start=(first and i == 0), stop=False)
        pe.matmul(out, ah, bl, start=False, stop=False)
        mm = pe.matmul(out, al, bh, start=False, stop=(last and i == n - 1))
    return mm


def prepare(nc, c):
    with ExitStack() as stack:
        sb, pb, sem = allocators(nc, stack, "prep")
        w_raw = {n: sb(f"{n}_raw", [P, DC, D]) for n in ("wq", "wk", "wv")}
        stats = sb("stats", [P, NT, 6])
        mv = sb("mv", [P, NT, 2])
        std = sb("std", [P, NT])
        rstd = sb("rstd", [P, NT])
        h = sb("h", [P, NT, D])
        hT = sb("hT", [P, DC, N])
        tp = [pb(f"tp{i}", [P, N]) for i in range(2)]
        qp = [pb(f"qp{i}", [P, N]) for i in range(2)]
        x_in, wq_in, wk_in, wv_in, small_in = (sem(n) for n in ("x_in", "wq_in", "wk_in", "wv_in", "small_in"))
        s_const, s_ident = sem("const"), sem("ident")
        s_stats, s_var, s_std, s_rstd, s_h = sem("stats"), sem("var"), sem("std"), sem("rstd"), sem("h")
        s_tp, s_hT, s_q, s_qT, s_qhi, s_qlo, s_whi, s_wlo = (
            sem(n) for n in ("tp", "hT", "q", "qT", "qhi", "qlo", "whi", "wlo"))
        block = stack.enter_context(nc.Block())

        @block.sync
        def _(sp):
            def weights(name):
                return c.dram[name].rearrange("(k p) o -> p k o", p=P)

            sp.dma_start(c.x[:, :, :], c.dram["x"].rearrange("(t p) d -> p t d", p=P)).then_inc(x_in, 16)
            sp.dma_start(w_raw["wq"][:, :, :], weights("WqT")).then_inc(wq_in, 16)
            sp.dma_start(c.raw[:, :, :], c.dram["ctx"][0]).then_inc(c.ctx_in, 16)
            sp.dma_start(w_raw["wk"][:, :, :], weights("WkT")).then_inc(wk_in, 16)
            sp.dma_start(w_raw["wv"][:, :, :], weights("WvT")).then_inc(wv_in, 16)
            sp.wait_ge(small_in, 64)

        @block.gpsimd
        def _(pool):
            pool.sem_inc(c.s_lo, PRIME_LO)
            pool.memset(c.ident[:, :], 0.0).then_inc(s_ident, 1)
            pool.wait_ge(s_ident, 1)
            pool.affine_select(out=c.ident[:, :], in_=c.ident[:, :], compare_op=ALU.not_equal, fill=1.0,
                               base=0, pattern=[[-1, P]], channel_multiplier=1).then_inc(s_ident, 1)
            pool.memset(f32(c.stacks[:, :, :]), 0.0).then_inc(s_const, 1)
            pool.memset(c.ones[:, :], 1.0).then_inc(s_const, 1)
            pool.memset(c.one_row[:, :], 1.0).then_inc(s_const, 1)
            pool.wait_ge(s_const, 3)
            pool.wait_ge(c.ctx_in, 16)
            pool.tensor_copy(c.hi[0][:, :, :], c.raw[:, :, :]).then_inc(c.s_hi, 1)
            pool.wait_ge(c.s_hi, 1)
            pool.tensor_tensor(c.lo[0][:, :, :], c.raw[:, :, :], f32(c.hi[0][:, :, :]), ALU.subtract).then_inc(c.s_lo, 1)
            pool.wait_ge(s_whi, 2)
            pool.tensor_tensor(c.wv_lo[:, :, :], w_raw["wv"][:, :, :], f32(c.wv_hi[:, :, :]), ALU.subtract).then_inc(s_const, 1)

        @block.scalar
        def _(act):
            for name, tile in (("bq", c.bq), ("bk", c.bk), ("bv", c.bv), ("bo", c.bo)):
                act.dma_start(tile[:, :], c.dram[name]).then_inc(small_in, 16)
            act.wait_ge(s_var, 1)
            act.activation(std[:, :], std[:, :], ACT.Sqrt).then_inc(s_std, 1)
            for k in range(DC):
                act.wait_ge(s_tp, k + 1)
                act.activation(hT[:, k, :], tp[k % 2][:, :], ACT.Copy).then_inc(s_hT, 1)
            act.wait_ge(wk_in, 16)
            act.activation(c.wk_hi[:, :, :], w_raw["wk"][:, :, :], ACT.Copy).then_inc(s_whi, 1)
            act.wait_ge(small_in, 64)
            for g in range(G):
                act.wait_ge(s_q, g + 1)
                act.activation(h[:, g, :], qp[g % 2][:, :], ACT.Identity, bias=c.bq[:, g:g + 1]).then_inc(s_qT, 1)
                if g == 0:
                    act.wait_ge(wv_in, 16)
                    act.activation(c.wv_hi[:, :, :], w_raw["wv"][:, :, :], ACT.Copy).then_inc(s_whi, 1)
            for g in range(G):
                act.wait_ge(c.k_proj, g + 1)
                act.activation(c.k_hi[0][:, g, :], c.proj[g][:, :], ACT.Identity, bias=c.bk[:, g:g + 1]).then_inc(c.k_hi_done, 1)

        @block.vector
        def _(dve):
            dve.wait_ge(x_in, 16)
            layer_norm(dve, c.x, h, stats, mv, std, rstd, s_stats, s_var, s_std, s_rstd, s_h)
            dve.wait_ge(s_whi, 1)
            dve.tensor_tensor(c.wk_lo[:, :, :], w_raw["wk"][:, :, :], f32(c.wk_hi[:, :, :]), ALU.subtract).then_inc(s_wlo, 1)
            dve.wait_ge(s_const, 1)
            for g in range(G):
                dve.wait_ge(s_qT, g + 1)
                dve.tensor_copy(c.q_hi[:, g, :], h[:, g, :]).then_inc(s_qhi, 1)
                dve.wait_ge(s_qhi, g + 1)
                dve.tensor_tensor(c.q_lo[:, g, :], h[:, g, :], f32(c.q_hi[:, g, :]), ALU.subtract).then_inc(s_qlo, 1)
                for j in range(HG):
                    rows = slice(HD * j, HD * j + HD)
                    dve.tensor_copy(c.stacks[rows, HG * g + j, :], f32(c.q_hi[rows, g, :])).then_inc(s_qlo, 1)
            for g in range(G):
                dve.wait_ge(c.k_hi_done, g + 1)
                dve.scalar_tensor_tensor(out=c.k_lo[:, g, :], in0=c.proj[g][:, :], scalar=c.bk[:, g:g + 1],
                                         in1=f32(c.k_hi[0][:, g, :]), op0=ALU.add, op1=ALU.subtract).then_inc(c.k_lo_done, 1)

        @block.tensor
        def _(pe):
            pe.wait_ge(s_ident, 2)
            pe.wait_ge(s_h, NT)
            for k in range(DC):
                if k >= 2:
                    pe.wait_ge(s_hT, k - 1)
                for t in range(NT):
                    mm = pe.transpose(tp[k % 2][:, t * P:(t + 1) * P], h[:, t, k * P:(k + 1) * P], c.ident[:, :])
                mm.then_inc(s_tp, 1)
            pe.wait_ge(wq_in, 16)
            pe.wait_ge(s_hT, DC)
            for g in range(G):
                if g >= 2:
                    pe.wait_ge(s_qT, g - 1)
                for k in range(DC):
                    mm = pe.matmul(qp[g % 2][:, :], w_raw["wq"][:, k, g * P:(g + 1) * P], hT[:, k, :],
                                   start=(k == 0), stop=(k == DC - 1))
                mm.then_inc(s_q, 1)
            pe.wait_ge(c.s_lo, 1 + PRIME_LO)
            pe.wait_ge(s_wlo, 1)
            for g in range(G):
                split_product(pe, c.proj[g][:, :],
                              [(c.wk_hi[:, k, g * P:(g + 1) * P], c.wk_lo[:, k, g * P:(g + 1) * P]) for k in range(DC)],
                              [(c.hi[0][:, k, :], c.lo[0][:, k, :]) for k in range(DC)]).then_inc(c.k_proj, 1)


def layer_norm(dve, x, h, stats, mv, std, rstd, s_stats, s_var, s_std, s_rstd, s_h):
    for t in range(NT):
        dve.bn_stats(stats[:, t, :], x[:, t, :]).then_inc(s_stats, 1)
    for t in range(NT):
        dve.wait_ge(s_stats, t + 1)
        dve.bn_aggr(mv[:, t, :], stats[:, t, :]).then_inc(s_stats, 1)
    dve.wait_ge(s_stats, 2 * NT)
    dve.tensor_scalar(std[:, :], mv[:, :, 1], EPS, None, ALU.add).then_inc(s_var, 1)
    dve.wait_ge(s_std, 1)
    dve.reciprocal(rstd[:, :], std[:, :]).then_inc(s_rstd, 1)
    dve.wait_ge(s_rstd, 1)
    for t in range(NT):
        dve.tensor_scalar(h[:, t, :], x[:, t, :], mv[:, t, 0:1], rstd[:, t:t + 1],
                          ALU.subtract, ALU.mult).then_inc(s_h, 1)


def project_context(nc, c):
    PRIME_V, PRIME_EV, PRIME_OUT, PRIME_ST, PRIME_CP, PRIME_R, PRIME_M = 8, 4, 16, 1, 1, 18, 2
    PAIRS = 2
    with ExitStack() as stack:
        sb, pb, sem = allocators(nc, stack, "ctx")
        raw, hi, lo, k_hi, k_lo, proj = c.raw, c.hi, c.lo, c.k_hi, c.k_lo, c.proj
        v = sb("v", [P, G, KT, P])
        run = sb("run", [P, H, 2 * CH], BF16)
        half = sb("half", [P, 2, 2 * CH], BF16)
        st = sb("st", [P, 2, H, 2])
        best = sb("best", [P, H, 2])
        sc = [pb(f"sc{i}", [P, 2 * CH]) for i in range(2)]
        ctx_in, s_hi, s_lo = c.ctx_in, c.s_hi, c.s_lo
        k_proj, k_hi_done, k_lo_done = c.k_proj, c.k_hi_done, c.k_lo_done
        v_proj, v_done, s_turn, s_stack = sem("v_proj"), sem("v_done"), sem("turn"), sem("stack")
        k_hi_out = [sem(f"k_hi_out{b}") for b in range(2)]
        k_lo_out, v_out = sem("k_lo_out"), sem("v_out")
        sc_ready = [sem(f"sc_ready{i}") for i in range(2)]
        s_st, s_copied, s_run, s_best = sem("st"), sem("copied"), sem("run"), sem("best")
        s_tree, s_neg, s_neg_hi = sem("tree"), sem("neg"), sem("neg_hi")
        block = stack.enter_context(nc.Block())

        @block.sync
        def _(sp):
            sp.sem_inc(k_hi_out[0], PRIME_OUT)
            sp.sem_inc(k_hi_out[1], PRIME_OUT)
            sp.sem_inc(k_lo_out, PRIME_OUT)
            sp.sem_inc(v_out, PRIME_OUT)

            def load(n):
                sp.wait_ge(s_lo, n + PRIME_LO)
                sp.dma_start(raw[:, :, :], c.dram["ctx"][n]).then_inc(ctx_in, 16)

            def store(n, b):
                sp.wait_ge(k_hi_done, G * n + G)
                sp.dma_start(c.k_dram[n, :, 0].rearrange("g p k -> p g k"), f32(k_hi[b][:, :, :])).then_inc(k_hi_out[b], 16)
                sp.wait_ge(k_lo_done, G * n + G)
                sp.dma_start(c.k_dram[n, :, 1].rearrange("g p k -> p g k"), f32(k_lo[:, :, :])).then_inc(k_lo_out, 16)
                sp.wait_ge(v_done, KT * n + KT + PRIME_EV)
                sp.dma_start(c.v_dram[n].rearrange("g p t d -> p g t d"), v[:, :, :, :]).then_inc(v_out, 16)

            with sp.Fori(0, NCH // 2 - 1) as i:
                for b in range(2):
                    load(2 * i + b + 1)
                    store(2 * i + b, b)
            load(NCH - 1)
            store(NCH - 2, 0)
            store(NCH - 1, 1)
            sp.wait_ge(k_hi_out[0], 16 * (NCH // 2) + PRIME_OUT)
            sp.wait_ge(k_hi_out[1], 16 * (NCH // 2) + PRIME_OUT)
            sp.wait_ge(k_lo_out, 16 * NCH + PRIME_OUT)
            sp.wait_ge(v_out, 16 * NCH + PRIME_OUT)
            for i in range(2):
                sp.wait_ge(sc_ready[i], H * NCH)
            for place, part in ((0, f32(c.q_hi[:, :, :])), (1, f32(c.q_hi[:, :, :])), (2, c.q_lo)):
                stack_copies(sp, c.stacks, part, place, s_stack)
            sp.wait_ge(s_stack, 16 * 3 * HG)

        @block.gpsimd
        def _(pool):
            def split(n, b):
                pool.wait_ge(ctx_in, 16 * n + 16)
                pool.wait_ge(v_proj, KT * (n - 1) + PRIME_V)
                pool.sem_inc(s_turn, 1)
                pool.tensor_copy(hi[b][:, :, :], raw[:, :, :]).then_inc(s_hi, 1)
                pool.wait_ge(s_hi, n + 1)
                pool.tensor_tensor(lo[b][:, :, :], raw[:, :, :], f32(hi[b][:, :, :]), ALU.subtract).then_inc(s_lo, 1)

            split(1, 1)
            with pool.Fori(1, NCH // 2) as i:
                for b in range(2):
                    split(2 * i + b, b)

        @block.tensor
        def _(pe):
            pe.sem_inc(v_proj, PRIME_V)

            def keys(n, b, g, part):
                if part == 0:
                    if g == 0:
                        pe.wait_ge(s_lo, n + 1 + PRIME_LO)
                    pe.wait_ge(v_done, KT * (n - 1) + g + 1 + PRIME_EV)
                ks = range(DC // 2 * part, DC // 2 * part + DC // 2)
                mm = split_product(pe, proj[g][:, :],
                                   [(c.wk_hi[:, k, g * P:(g + 1) * P], c.wk_lo[:, k, g * P:(g + 1) * P]) for k in ks],
                                   [(hi[b][:, k, :], lo[b][:, k, :]) for k in ks], first=(part == 0), last=(part == 1))
                if part == 1:
                    mm.then_inc(k_proj, 1)

            def values(n, b, t, part):
                if part == 0:
                    pe.wait_ge(k_lo_done, G * n + t + 1)
                ks = range(DC // 2 * part, DC // 2 * part + DC // 2)
                mm = split_product(pe, proj[t][:, :],
                                   [(hi[b][:, k, t * P:(t + 1) * P], lo[b][:, k, t * P:(t + 1) * P]) for k in ks],
                                   [(c.wv_hi[:, k, :], c.wv_lo[:, k, :]) for k in ks], first=(part == 0), last=(part == 1))
                if part == 1:
                    mm.then_inc(v_proj, 1)

            def scores(n, b, h):
                if h % HG == 0:
                    pe.wait_ge(k_hi_done, G * n + h // HG + 1)
                for s in range(PAIRS):
                    if s == 0:
                        pe.wait_ge(s_st, H * n + h - 1 + 1 + PRIME_ST)
                    else:
                        pe.wait_ge(s_copied, H * n + h - 1 + 1 + PRIME_CP)
                    for q in range(2):
                        at = (2 * s + q) * P
                        mm = pe.matmul(sc[s][:, q * CH:(q + 1) * CH], c.stacks[:, h, at:at + P],
                                       k_hi[b][:, h // HG, :], start=True, stop=True)
                    mm.then_inc(sc_ready[s], 1)

            def chunk(n, b, last=False):
                for h in range(H):
                    scores(n, b, h)
                    if h < 2 * KT:
                        values(n, b, h // 2, h % 2)
                    elif not last:
                        keys(n + 1, 1 - b, h // 2 - KT, h % 2)

            with pe.Fori(0, NCH // 2 - 1) as i:
                for b in range(2):
                    chunk(2 * i + b, b)
            chunk(NCH - 2, 0)
            chunk(NCH - 1, 1, last=True)

        @block.scalar
        def _(act):
            act.sem_inc(v_done, PRIME_EV)
            act.sem_inc(s_copied, PRIME_CP)

            def keys(n, b, g):
                if g == 0:
                    act.wait_ge(k_hi_out[b], 8 * (n - b) + PRIME_OUT)
                act.wait_ge(k_proj, G * n + g + 1)
                act.activation(k_hi[b][:, g, :], proj[g][:, :], ACT.Identity, bias=c.bk[:, g:g + 1]).then_inc(k_hi_done, 1)

            def values(n, t):
                if t == 0:
                    act.wait_ge(v_out, 16 * n + PRIME_OUT)
                act.wait_ge(v_proj, KT * n + t + 1 + PRIME_V)
                act.activation(v[:, :, t, :], proj[t][:, :].rearrange("p (g d) -> p g d", g=G), ACT.Copy).then_inc(v_done, 1)

            def copy(n, h):
                act.wait_ge(sc_ready[1], H * n + h + 1)
                act.wait_ge(s_run, H * n + h - 2 + 1 + PRIME_R)
                act.activation(half[:, h % 2, :], sc[1][:, :], ACT.Copy).then_inc(s_copied, 1)

            def chunk(n, b, last=False):
                for h in range(H):
                    copy(n, h)
                    if h % 2 and h < 2 * KT:
                        values(n, h // 2)
                    elif h % 2 and not last:
                        keys(n + 1, 1 - b, h // 2 - KT)

            with act.Fori(0, NCH // 2 - 1) as i:
                for b in range(2):
                    chunk(2 * i + b, b)
            chunk(NCH - 2, 0)
            chunk(NCH - 1, 1, last=True)

        @block.vector
        def _(dve):
            dve.memset(best[:, :, :], NEG).then_inc(s_best, PRIME_M)
            dve.sem_inc(s_run, PRIME_R)
            dve.memset(st[:, :, :, :], NEG).then_inc(s_st, PRIME_ST)

            def merge(n, h, first):
                dve.wait_ge(s_copied, H * n + h + 1 + PRIME_CP)
                if first:
                    dve.tensor_copy(run[:, h, :], half[:, h % 2, :]).then_inc(s_run, 1)
                    return
                dve.wait_ge(s_run, H * (n - 1) + h + 1 + PRIME_R)
                dve.tensor_tensor(run[:, h, :], run[:, h, :], half[:, h % 2, :], ALU.max).then_inc(s_run, 1)

            def keys(n, b, g):
                if g == 0:
                    dve.wait_ge(k_lo_out, 16 * n + PRIME_OUT)
                dve.wait_ge(k_hi_done, G * n + g + 1)
                dve.scalar_tensor_tensor(out=k_lo[:, g, :], in0=proj[g][:, :], scalar=c.bk[:, g:g + 1],
                                         in1=f32(k_hi[b][:, g, :]), op0=ALU.add, op1=ALU.subtract).then_inc(k_lo_done, 1)

            def update(n, b):
                dve.wait_ge(s_st, H * n + PRIME_ST)
                dve.wait_ge(s_best, n + PRIME_M)
                dve.tensor_tensor(best[:, :, :], best[:, :, :], st[:, b, :, :], ALU.max).then_inc(s_best, 1)

            def chunk(n, b, first=False, last=False):
                dve.wait_ge(s_best, n - 1 + PRIME_M)
                for h in range(H):
                    dve.wait_ge(sc_ready[0], H * n + h + 1)
                    dve.tensor_reduce(st[:, b, h, :], sc[0][:, :].rearrange("p (q k) -> p q k", q=2), AX.X, ALU.max).then_inc(s_st, 1)
                    if h >= 1:
                        merge(n, h - 1, first)
                    if h == 2:
                        update(n, 1 - b)
                    if h >= 2 * KT + 2 and h % 2 == 0 and not last:
                        keys(n + 1, 1 - b, h // 2 - KT - 1)
                merge(n, H - 1, first)
                if not last:
                    keys(n + 1, 1 - b, G - 1)

            chunk(0, 0, first=True)
            chunk(1, 1)
            with dve.Fori(1, NCH // 2 - 1) as i:
                for b in range(2):
                    chunk(2 * i + b, b)
            chunk(NCH - 2, 0)
            chunk(NCH - 1, 1, last=True)
            update(NCH, 1)

            dve.wait_ge(s_run, H * NCH + PRIME_R)
            view = run[:, :, :].rearrange("p h (q k) -> p (h q) k", q=2)
            width, steps = CH // 2, 0
            while width >= 32:
                if steps:
                    dve.wait_ge(s_tree, steps)
                dve.tensor_tensor(view[:, :, 0:width], view[:, :, 0:width], view[:, :, width:2 * width], ALU.max).then_inc(s_tree, 1)
                steps += 1
                width //= 2
            dve.wait_ge(s_tree, steps)
            dve.tensor_reduce(c.neg[:, :, 2:4], view[:, :, 0:2 * width].rearrange("p (h q) k -> p h q k", q=2), AX.X, ALU.max).then_inc(s_tree, 1)
            dve.wait_ge(s_best, NCH + 1 + PRIME_M)
            dve.tensor_copy(c.neg[:, :, 0:2], best[:, :, :]).then_inc(s_tree, 1)
            dve.wait_ge(s_tree, steps + 2)


def stack_copies(engine, stacks, part, place, s_copy):
    for j in range(HG):
        src, dst = part[HD * j:HD * j + HD, :, :], stacks[HD * place:HD * place + HD, j::HG, :]
        if engine.engine == mybir.EngineType.SP:
            engine.dma_start(f32(dst), src).then_inc(s_copy, 16)
        elif engine.engine == mybir.EngineType.Activation:
            engine.activation(dst, src, ACT.Copy).then_inc(s_copy, 1)
        else:
            engine.tensor_copy(dst, src).then_inc(s_copy, 1)


def maximum_rows(nc, block, c, sem, best, shift, shift_hi, rows, s_row):
    s_set, s_turned = sem("set"), sem("turned")

    @block.vector
    def _(dve):
        flat = best[:, :, :].rearrange("p h t -> p (h t)")
        parts = shift[:, MROW:].rearrange("p (i two) -> p i two", two=2)
        dve.memset(shift[:, 0:MROW], 0.0).then_inc(s_set, 1)
        dve.tensor_scalar(shift_hi[:, :], flat, -1.0, None, ALU.mult).then_inc(s_set, 1)
        dve.wait_ge(s_set, 2)
        dve.tensor_copy(parts[:, :, 0], f32(shift_hi[:, :])).then_inc(s_set, 1)
        dve.scalar_tensor_tensor(out=parts[:, :, 1], in0=flat, scalar=-1.0, in1=f32(shift_hi[:, :]),
                                 op0=ALU.mult, op1=ALU.subtract).then_inc(s_set, 1)
        for h in range(0, H, 2):
            dve.wait_ge(s_turned, h + 1)
            dve.tensor_copy(c.stacks[MROW:MROW + 2, h, :], rows[h % 4][MROW:MROW + 2, :]).then_inc(s_row[0], 1)

    @block.scalar
    def _(act):
        for h in range(1, H, 2):
            act.wait_ge(s_turned, h + 1)
            act.activation(c.stacks[MROW:MROW + 2, h, :], rows[h % 4][MROW:MROW + 2, :], ACT.Copy).then_inc(s_row[1], 1)

    @block.tensor
    def _(pe):
        pe.wait_ge(s_set, 4)
        for h in range(H):
            if h >= 4:
                pe.wait_ge(s_row[h % 2], h // 2 - 1)
            for t in range(NT):
                i = h * NT + t
                mm = pe.transpose(rows[h % 4][0:MROW + 2, t * P:(t + 1) * P], shift[:, 2 * i:2 * i + MROW + 2], c.ident[:, :])
            mm.then_inc(s_turned, 1)
        for half in range(2):
            pe.wait_ge(s_row[half], H // 2)


def attend_context(nc, c):
    CHUNKS = 3
    BODY = CHUNKS * KT
    TILES = NCH * KT
    LOOPS = NCH // CHUNKS
    REST = TILES - LOOPS * BODY
    RING = UNIT = BODY // 2
    PAIRS = 3
    UNITS = 2 * LOOPS + 1

    def added(u):
        return (UNIT - 1) * (u // UNIT) + max(u % UNIT, 1)

    ADDS = added(TILES - 1)
    with ExitStack() as stack:
        sb, pb, sem = allocators(nc, stack, "att")
        kst = [sb(f"kst{b}", [STK + 2, HG, CH], F32R) for b in range(CHUNKS)]
        val = [sb(f"val{b}", [P, KT, P]) for b in range(CHUNKS)]
        pr = sb("pr", [P, RING, HG, N])
        tot = [sb(f"tot{b}", [P, HG, N]) for b in range(2)]
        rs = sb("rs", [P, N])
        whole = sb("whole", [P, N])
        sc = [pb(f"sc{s}", [P, 2 * N]) for s in range(PAIRS)]
        o, den = pb("o", [P, N]), pb("den", [P, N])
        k_in = [sem(f"k_in{b}") for b in range(CHUNKS)]
        v_in = [sem(f"v_in{b}") for b in range(CHUNKS)]
        s_ones, s_sc, s_exp, s_pv, s_add, s_sum, s_whole = (
            sem(n) for n in ("ones", "sc", "exp", "pv", "add", "sum", "whole"))
        s_rs, s_norm, s_out = sem("rs"), sem("norm"), sem("out")
        s_row = [sem(f"row{half}") for half in range(2)]
        shift = sb("shift", [P, MROW + 2 * H * NT])
        shift_hi = sb("shift_hi", [P, H * NT], F32R)
        block = stack.enter_context(nc.Block())
        rows = [sc[i // 2][:, i % 2 * N:i % 2 * N + N] for i in range(4)]
        maximum_rows(nc, block, c, sem, c.neg, shift, shift_hi, rows, s_row)

        @block.gpsimd
        def _(pool):
            for b in range(CHUNKS):
                pool.memset(f32(kst[b][MROW:MROW + 2, :, :]), 1.0).then_inc(s_ones, 1)

        @block.sync
        def _(sp):
            def load(g, i, m):
                chunk = CHUNKS * i + m
                b = (NCH * g + m) % CHUNKS
                if NCH * g + m >= CHUNKS or not isinstance(i, int):
                    sp.wait_ge(s_sc, 2 * KT * (NCH * g + chunk - CHUNKS + 1))
                for row, part in ((0, 0), (1, 1), (2, 0)):
                    sp.dma_start(f32(kst[b][HD * row:HD * row + HD, :, :]),
                                 c.k_dram[chunk, g, part].rearrange("(j d) k -> d j k", j=HG)).then_inc(k_in[b], 16)
                if NCH * g + m >= CHUNKS or not isinstance(i, int):
                    sp.wait_ge(s_pv, KT * (NCH * g + chunk - CHUNKS + 1))
                sp.dma_start(val[b][:, :, :], c.v_dram[chunk, g]).then_inc(v_in[b], 16)

            for g in range(G):
                for m in range(CHUNKS):
                    load(g, 0, m)
                if g == 0:
                    sp.dma_start(c.woT[:, :, :], c.dram["WoT"].rearrange("(k p) o -> p k o", p=P)).then_inc(c.wo_in, 16)
                    load_self_weights(sp, c)
                with sp.Fori(1, LOOPS) as i:
                    for m in range(CHUNKS):
                        load(g, i, m)
                for m in range(CHUNKS * LOOPS, NCH):
                    load(g, 0, m)

        @block.tensor
        def _(pe):
            pe.wait_ge(s_ones, CHUNKS)

            def scores(g, i, pair):
                u, s = divmod(pair, 2)
                m = NCH * g + u // KT
                if u % KT == 0 and s == 0:
                    pe.wait_ge(k_in[m % CHUNKS], 48 * (m // CHUNKS + i + 1))
                place = 2 * TILES * g + pair
                if place >= PAIRS or not isinstance(i, int):
                    pe.wait_ge(s_exp, place + 2 * BODY * i - PAIRS + 1)
                for r in range(2):
                    j = 2 * s + r
                    at = u % KT * P
                    mm = pe.matmul(sc[place % PAIRS][:, r * N:(r + 1) * N], kst[m % CHUNKS][:, j, at:at + P],
                                   c.stacks[0:STK + 2, HG * (g + u // TILES) + j, :], start=True, stop=True)
                mm.then_inc(s_sc, 1)

            def weighted(g, i, u, first=False):
                m, T = NCH * g + u // KT, TILES * g + u
                if u % KT == 0:
                    pe.wait_ge(v_in[m % CHUNKS], 16 * (m // CHUNKS + i + 1))
                pe.wait_ge(s_exp, 2 * (T + BODY * i) + 2)
                for j in range(HG):
                    at = slice(HD * j, HD * j + HD)
                    mm = pe.matmul(o[at, :], val[m % CHUNKS][:, u % KT, at], pr[:, T % RING, j, :],
                                   start=first, stop=False, skip_group_check=True)
                mm.then_inc(s_pv, 1)

            def sums(g, i, k):
                pe.wait_ge(s_add, ADDS * g + added(UNIT * k + (REST if k == UNITS - 1 else UNIT) - 1)
                           + 2 * (UNIT - 1) * i)
                for j in range(HG):
                    mm = pe.matmul(den[HD * j:HD * j + HD, :], c.ones[:, :], tot[(UNITS * g + k) % 2][:, j, :],
                                   start=(k == 0 and isinstance(i, int)), stop=False, skip_group_check=True)
                mm.then_inc(s_sum, 1)

            def step(g, i, us, before):
                for u in us:
                    for s in range(2):
                        pair = 2 * u + PAIRS + s
                        if not (g == G - 1 and pair >= 2 * TILES):
                            scores(g, i, pair)
                    first = isinstance(i, int) and u == 0
                    if first and g:
                        pe.wait_ge(s_whole, g)
                    weighted(g, i, u, first)
                    if u % UNIT == 1 and (u > 1 or before):
                        if u > 1:
                            if isinstance(i, int) and u < BODY and g:
                                pe.wait_ge(s_rs, g)
                            sums(g, i, u // UNIT - 1)
                        else:
                            sums(*before)

            for pair in range(PAIRS):
                scores(0, 0, pair)
            for g in range(G):
                step(g, 0, range(BODY), before=(g - 1, 0, UNITS - 1) if g else None)
                with pe.Fori(1, LOOPS) as i:
                    step(g, i, range(BODY), before=(g, i, -1))
                step(g, 0, range(TILES - REST, TILES), before=None)
            sums(G - 1, 0, UNITS - 1)

        @block.scalar
        def _(act):
            def exponentials(g, i, u):
                T = TILES * g + u
                if not isinstance(i, int) or u >= RING:
                    act.wait_ge(s_pv, T + BODY * i - RING + 1)
                    act.wait_ge(s_add, ADDS * g + 2 * (UNIT - 1) * i + added(u) - (UNIT - 1))
                elif g:
                    act.wait_ge(s_pv, T - RING + 1)
                    act.wait_ge(s_add, ADDS * (g - 1) + added(TILES + u - RING))
                for s in range(2):
                    act.wait_ge(s_sc, 2 * (T + BODY * i) + s + 1)
                    act.activation(pr[:, T % RING, 2 * s:2 * s + 2, :],
                                   sc[(2 * T + s) % PAIRS][:, :].rearrange("p (j q) -> p j q", j=2), ACT.Exp,
                                   scale=SCALE).then_inc(s_exp, 1)

            for g in range(G):
                for u in range(BODY):
                    exponentials(g, 0, u)
                with act.Fori(1, LOOPS) as i:
                    for u in range(BODY):
                        exponentials(g, i, u)
                for u in range(TILES - REST, TILES):
                    exponentials(g, 0, u)

        @block.vector
        def _(dve):
            def add(g, i, u):
                v, unit = u % UNIT, UNITS * g + u // UNIT
                if v == 0:
                    return
                total = tot[unit % 2]
                dve.wait_ge(s_exp, 2 * (TILES * g + u + BODY * i) + 2)
                if v == 1:
                    if unit >= 2 or not isinstance(i, int):
                        dve.wait_ge(s_sum, unit + 2 * i - 1)
                    so_far = pr[:, (TILES * g + u - 1) % RING, :, :]
                else:
                    dve.wait_ge(s_add, ADDS * g + 2 * (UNIT - 1) * i + added(u) - 1)
                    so_far = total[:, :, :]
                dve.tensor_tensor(total[:, :, :], so_far, pr[:, (TILES * g + u) % RING, :, :], ALU.add).then_inc(s_add, 1)

            def normalise(g):
                dve.wait_ge(s_sum, UNITS * (g + 1))
                dve.reciprocal(rs[:, :], den[:, :]).then_inc(s_rs, 1)
                dve.wait_ge(s_rs, g + 1)
                dve.wait_ge(s_whole, g + 1)
                dve.tensor_tensor(c.aoT[:, g, :], whole[:, :], rs[:, :], ALU.mult).then_inc(s_norm, 1)
                dve.wait_ge(s_norm, g + 1)
                dve.tensor_scalar(c.aoT[:, g, :], c.aoT[:, g, :], c.bv[:, g:g + 1], None, ALU.add).then_inc(s_out, 1)

            for g in range(G):
                for u in range(BODY):
                    add(g, 0, u)
                    if u == UNIT // 2 and g:
                        normalise(g - 1)
                with dve.Fori(1, LOOPS) as i:
                    for u in range(BODY):
                        add(g, i, u)
                for u in range(TILES - REST, TILES):
                    add(g, 0, u)
                dve.wait_ge(s_pv, TILES * (g + 1))
                if g:
                    dve.wait_ge(s_norm, g)
                dve.tensor_copy(whole[:, :], o[:, :]).then_inc(s_whole, 1)
            normalise(G - 1)
            dve.wait_ge(s_out, G)


def add_and_normalise(nc, c, name, srcT, w, w_in, hT, bias=None):
    with ExitStack() as stack:
        sb, pb, sem = allocators(nc, stack, name)
        stats = sb("stats", [P, NT, 6])
        mv = sb("mv", [P, NT, 2])
        std = sb("std", [P, NT])
        rstd = sb("rstd", [P, NT])
        h = sb("h", [P, NT, D])
        acc = [pb(f"acc{t}", [P, D]) for t in range(NT)]
        tp = pb("tp", [P, DC, N])
        s_mm, s_x, s_stats, s_var, s_std, s_h, s_tp, s_hT = (
            sem(n) for n in ("mm", "x", "stats", "var", "std", "h", "tp", "hT"))
        block = stack.enter_context(nc.Block())

        @block.tensor
        def _(pe):
            pe.wait_ge(w_in, 16)
            for t in range(NT):
                if bias is not None:
                    pe.matmul(acc[t][:, :], c.one_row[:, :], bias, start=True, stop=False)
                for k in range(DC):
                    mm = pe.matmul(acc[t][:, :], srcT[:, k, t * P:(t + 1) * P], w[:, k, :],
                                   start=(bias is None and k == 0), stop=(k == DC - 1))
                mm.then_inc(s_mm, 1)
            for t in range(NT):
                pe.wait_ge(s_h, t + 1)
                for k in range(DC):
                    mm = pe.transpose(tp[:, k, t * P:(t + 1) * P], h[:, t, k * P:(k + 1) * P], c.ident[:, :])
            mm.then_inc(s_tp, 1)

        @block.vector
        def _(dve):
            for t in range(NT):
                dve.wait_ge(s_mm, t + 1)
                dve.tensor_tensor(c.x[:, t, :], acc[t][:, :], c.x[:, t, :], ALU.add).then_inc(s_x, 1)
                dve.wait_ge(s_x, t + 1)
                dve.bn_stats(stats[:, t, :], c.x[:, t, :]).then_inc(s_stats, 1)
                dve.wait_ge(s_stats, 2 * t + 1)
                dve.bn_aggr(mv[:, t, :], stats[:, t, :]).then_inc(s_stats, 1)
                dve.wait_ge(s_stats, 2 * t + 2)
                dve.tensor_scalar(std[:, t:t + 1], mv[:, t, 1:2], EPS, None, ALU.add).then_inc(s_var, 1)
            for t in range(NT):
                dve.wait_ge(s_std, t + 1)
                dve.reciprocal(rstd[:, t:t + 1], std[:, t:t + 1]).then_inc(s_stats, 1)
                dve.wait_ge(s_stats, 2 * NT + t + 1)
                dve.tensor_scalar(h[:, t, :], c.x[:, t, :], mv[:, t, 0:1], rstd[:, t:t + 1],
                                  ALU.subtract, ALU.mult).then_inc(s_h, 1)
            for k in range(DC // 2):
                dve.wait_ge(s_tp, 1)
                dve.tensor_copy(hT[:, k, :], tp[:, k, :]).then_inc(s_h, 1)
            dve.wait_ge(s_h, NT + DC // 2)

        @block.scalar
        def _(act):
            for t in range(NT):
                act.wait_ge(s_var, t + 1)
                act.activation(std[:, t:t + 1], std[:, t:t + 1], ACT.Sqrt).then_inc(s_std, 1)
            act.wait_ge(s_tp, 1)
            for k in range(DC // 2, DC):
                act.activation(hT[:, k, :], tp[:, k, :], ACT.Copy).then_inc(s_hT, 1)
            act.wait_ge(s_hT, DC // 2)


def load_self_weights(sp, c):
    for w, name, s_in in ((c.swqT, "sWqT", c.sq_in), (c.swkT, "sWkT", c.sk_in),
                          (c.swvT, "sWvT", c.sv_in), (c.swoT, "sWoT", c.so_in)):
        sp.dma_start(w[:, :, :], c.dram[name].rearrange("(k p) o -> p k o", p=P)).then_inc(s_in, 16)
    for j in range(HG):
        sp.dma_start(c.aff[HD * j:HD * j + HD, :], c.dram["affine"]).then_inc(c.aff_in, 16)


def self_projections(nc, c):
    with ExitStack() as stack:
        sb, pb, sem = allocators(nc, stack, "sp")
        total = sb("total", [P, NT * H])
        mean = sb("mean", [P, NT * H])
        spread = sb("spread", [P, NT * H])
        std = sb("std", [P, NT * H])
        rstd = sb("rstd", [P, NT * H])
        cen = sb("cen", [P, NT, D])
        nrm = sb("nrm", [P, NT, D])
        full = sb("full", [P, G, N])
        hi = sb("hi", [P, G, N], F32R)
        lo = sb("lo", [P, G, N], F32R)
        queries = pb("queries", [P, NT, D])
        keys = pb("keys", [P, NT, D])
        turned = queries[:, :, :]
        s_raw, s_cen, s_sq, s_var, s_std, s_nrm, s_tp, s_full, s_hi, s_lo, s_v, s_val, s_ones = (
            sem(n) for n in ("raw", "cen", "sq", "var", "std", "nrm", "tp", "full", "hi", "lo", "v", "val", "ones"))
        s_copy_act, s_copy_dve, s_copy_dma = sem("copy_act"), sem("copy_dve"), sem("copy_dma")
        s_step = sem("step")
        block = stack.enter_context(nc.Block())
        KINDS = ((c.stacks, 1, 2, 0), (c.skst, 2, 1, 2))

        def heads(ap):
            return ap.rearrange("p t (h d) -> p (t h) d", d=HD)

        def wide(ap):
            return ap[:, :].unsqueeze(2).broadcast_to([P, NT * H, HD])

        @block.sync
        def _(sp):
            for n, (stacks, second_hi, _, _) in enumerate(KINDS):
                sp.wait_ge(s_hi, G * (n + 1))
                stack_copies(sp, stacks, f32(hi[:, :, :]), second_hi, s_copy_dma)
            sp.wait_ge(s_copy_dma, 16 * 2 * HG)

        @block.tensor
        def _(pe):
            def project(out, w, t):
                for k in range(DC):
                    mm = pe.matmul(out[:, t, :], c.hT[:, k, t * P:(t + 1) * P], w[:, k, :],
                                   start=(k == 0), stop=(k == DC - 1))
                return mm

            def turn(n):
                pe.wait_ge(s_nrm, n + 1)
                if n:
                    pe.wait_ge(s_full, G)
                for g in range(G):
                    for t in range(NT):
                        mm = pe.transpose(turned[:, g, t * P:(t + 1) * P], nrm[:, t, g * P:(g + 1) * P], c.ident[:, :])
                    mm.then_inc(s_tp, 1)

            pe.wait_ge(c.sq_in, 16)
            for t in range(NT):
                mm = project(queries, c.swqT, t)
            mm.then_inc(s_raw, 1)
            pe.wait_ge(c.sk_in, 16)
            for t in range(NT):
                mm = project(keys, c.swkT, t)
            mm.then_inc(s_raw, 1)
            turn(0)
            pe.wait_ge(c.sv_in, 16)
            pe.wait_ge(s_cen, 2)
            for t in range(NT):
                if t == NT // 2:
                    turn(1)
                project(keys, c.swvT, t).then_inc(s_v, 1)

        @block.vector
        def _(dve):
            steps = 0

            def step(instruction):
                nonlocal steps
                steps += 1
                instruction.then_inc(s_step, 1)
                dve.wait_ge(s_step, steps)

            def centre(n, raw):
                dve.wait_ge(s_raw, n + 1)
                step(dve.tensor_reduce(total[:, :], heads(raw[:, :, :]), AX.X, ALU.add))
                step(dve.tensor_scalar(mean[:, :], total[:, :], 1.0 / HD, None, ALU.mult))
                if n:
                    dve.wait_ge(s_nrm, n)
                dve.tensor_tensor(heads(cen[:, :, :]), heads(raw[:, :, :]), wide(mean), ALU.subtract).then_inc(s_cen, 1)

            def normalise(n):
                dve.wait_ge(s_sq, n + 1)
                step(dve.tensor_reduce(spread[:, :], heads(nrm[:, :, :]), AX.X, ALU.add))
                dve.tensor_scalar(std[:, :], spread[:, :], 1.0 / HD, EPS, ALU.mult, ALU.add).then_inc(s_var, 1)
                dve.wait_ge(s_std, n + 1)
                step(dve.reciprocal(rstd[:, :], std[:, :]))
                dve.tensor_tensor(heads(nrm[:, :, :]), heads(cen[:, :, :]), wide(rstd), ALU.mult).then_inc(s_nrm, 1)

            def split(n):
                if n:
                    dve.wait_ge(s_copy_act, HG)
                    dve.wait_ge(s_copy_dve, HG)
                    dve.wait_ge(s_copy_dma, 16 * HG)
                for g in range(G):
                    dve.wait_ge(s_full, G * n + g + 1)
                    dve.tensor_copy(hi[:, g, :], full[:, g, :]).then_inc(s_hi, 1)
                    dve.wait_ge(s_hi, G * n + g + 1)
                    dve.tensor_tensor(lo[:, g, :], full[:, g, :], f32(hi[:, g, :]), ALU.subtract).then_inc(s_lo, 1)

            centre(0, queries)
            normalise(0)
            centre(1, keys)
            split(0)
            normalise(1)
            stack_copies(dve, KINDS[0][0], f32(hi[:, :, :]), 0, s_copy_dve)
            split(1)
            stack_copies(dve, KINDS[1][0], f32(hi[:, :, :]), 0, s_copy_dve)
            dve.wait_ge(s_copy_dve, 2 * HG)

        @block.scalar
        def _(act):
            def square(n):
                act.wait_ge(s_cen, n + 1)
                if n:
                    act.wait_ge(s_tp, G * n)
                act.activation(nrm[:, :, :], cen[:, :, :], ACT.Square).then_inc(s_sq, 1)

            def root(n):
                act.wait_ge(s_var, n + 1)
                act.activation(std[:, :], std[:, :], ACT.Sqrt).then_inc(s_std, 1)

            def affine(n):
                col = KINDS[n][3]
                if n:
                    act.wait_ge(s_lo, G * n)
                for g in range(G):
                    act.wait_ge(s_tp, G * n + g + 1)
                    act.activation(full[:, g, :], turned[:, g, :], ACT.Identity, scale=c.aff[:, col:col + 1],
                                   bias=c.aff[:, col + 1:col + 2]).then_inc(s_full, 1)

            def copy_lo(n):
                act.wait_ge(s_lo, G * (n + 1))
                stack_copies(act, KINDS[n][0], f32(lo[:, :, :]), KINDS[n][2], s_copy_act)

            def values(t):
                act.wait_ge(s_v, t + 1)
                act.activation(c.sval[:, t, :], keys[:, t, :], ACT.Copy).then_inc(s_val, 1)

            square(0)
            root(0)
            act.wait_ge(c.aff_in, 16 * HG)
            affine(0)
            square(1)
            root(1)
            copy_lo(0)
            affine(1)
            values(0)
            values(1)
            copy_lo(1)
            values(2)
            values(3)
            act.wait_ge(s_copy_act, 2 * HG)
            act.wait_ge(s_val, NT)

        @block.gpsimd
        def _(pool):
            pool.memset(f32(c.skst[MROW:MROW + 2, :, :]), 1.0).then_inc(s_ones, 1)
            pool.wait_ge(s_ones, 1)


def self_attend(nc, c):
    STEPS = HG * NT
    LEAD = STEPS + NT
    with ExitStack() as stack:
        sb, pb, sem = allocators(nc, stack, "sa")
        shift = sb("shift", [P, MROW + 2 * H * NT])
        shift_hi = sb("shift_hi", [P, H * NT], F32R)
        pr = sb("pr", [P, 2, HG, N])
        rs = sb("rs", [P, N])
        full = [pb(f"full{i}", [P, N]) for i in range(2)]
        rows = pb("rows", [P, N])
        sc = [pb(f"sc{i}", [P, N]) for i in range(3)]
        o = pb("o", [P, N])
        den = pb("den", [P, N])
        s_full, s_max, s_set, s_hi, s_parts, s_t, s_row, s_sc, s_exp, s_pv, s_rs, s_out = (
            sem(n) for n in ("full", "max", "set", "hi", "parts", "t", "row", "sc", "exp", "pv", "rs", "out"))
        block = stack.enter_context(nc.Block())

        @block.tensor
        def _(pe):
            def whole(i):
                if i >= 2:
                    pe.wait_ge(s_max, i - 1)
                h, t = divmod(i, NT)
                pe.matmul(full[i % 2][:, :], c.stacks[0:STK, h, t * P:(t + 1) * P], c.skst[0:STK, h, :],
                          start=True, stop=True).then_inc(s_full, 1)

            def turn(h):
                pe.wait_ge(s_parts, 2 * h + 2)
                if h >= 1:
                    pe.wait_ge(s_row, h)
                for t in range(NT):
                    i = h * NT + t
                    mm = pe.transpose(rows[0:MROW + 2, t * P:(t + 1) * P], shift[:, 2 * i:2 * i + MROW + 2], c.ident[:, :])
                mm.then_inc(s_t, 1)

            def scores(i):
                g, u, j = i // STEPS, i // HG % NT, i % HG
                if i >= 3:
                    pe.wait_ge(s_exp, i - 2)
                pe.matmul(sc[i % 3][:, :], c.skst[:, HG * g + j, u * P:(u + 1) * P],
                          c.stacks[0:STK + 2, HG * g + j, :], start=True, stop=True).then_inc(s_sc, 1)

            def weighted(T):
                g, u = divmod(T, NT)
                pe.wait_ge(s_exp, HG * T + HG)
                if u == 0 and g >= 1:
                    pe.wait_ge(s_out, g)
                for j in range(HG):
                    at = slice(HD * j, HD * j + HD)
                    pe.matmul(o[at, :], c.sval[:, u, P * g + HD * j:P * g + HD * j + HD], pr[:, T % 2, j, :],
                              start=(u == 0), stop=(u == NT - 1))
                for j in range(HG):
                    at = slice(HD * j, HD * j + HD)
                    mm = pe.matmul(den[at, :], c.ones[:, :], pr[:, T % 2, j, :], start=(u == 0), stop=(u == NT - 1))
                mm.then_inc(s_pv, 1)

            pe.wait_ge(s_set, 1)
            for i in range(LEAD):
                whole(i)
                if i % NT == NT - 1 and i > NT:
                    turn(i // NT - 1)
            for i in range(STEPS * G):
                if i + LEAD < STEPS * G:
                    whole(i + LEAD)
                if i % NT == NT - 1 and (i + LEAD) // NT <= H:
                    turn((i + LEAD) // NT - 1)
                if i % STEPS == 0:
                    pe.wait_ge(s_row, HG * (i // STEPS + 1))
                scores(i)
                if i % HG == HG - 1 and i >= 2 * HG - 1:
                    weighted(i // HG - 1)
            weighted(G * NT - 1)

        @block.scalar
        def _(act):
            def to_rows(h):
                act.wait_ge(s_t, h + 1)
                act.activation(c.stacks[MROW:MROW + 2, h, :], rows[MROW:MROW + 2, :], ACT.Copy).then_inc(s_row, 1)

            for h in range(HG):
                to_rows(h)
            for i in range(STEPS * G):
                T = i // HG
                if i % HG == 0 and T >= 2:
                    act.wait_ge(s_pv, T - 1)
                act.wait_ge(s_sc, i + 1)
                act.activation(pr[:, T % 2, i % HG, :], sc[i % 3][:, :], ACT.Exp, scale=SCALE).then_inc(s_exp, 1)
                if i % NT == NT - 1 and (i + LEAD) // NT <= H:
                    to_rows((i + LEAD) // NT - 1)

        @block.vector
        def _(dve):
            parts = shift[:, MROW:].rearrange("p (i two) -> p i two", two=2)
            dve.memset(shift[:, 0:MROW], 0.0).then_inc(s_set, 1)

            def normalise(g):
                dve.wait_ge(s_pv, NT * (g + 1))
                if g >= 1:
                    dve.wait_ge(s_out, g)
                dve.reciprocal(rs[:, :], den[:, :]).then_inc(s_rs, 1)
                dve.wait_ge(s_rs, g + 1)
                dve.tensor_tensor(c.aoT[:, g, :], o[:, :], rs[:, :], ALU.mult).then_inc(s_out, 1)

            for h in range(H):
                for i in range(NT * h, NT * h + NT):
                    dve.wait_ge(s_full, i + 1)
                    dve.tensor_reduce(c.neg[:, h, i % NT:i % NT + 1], full[i % 2][:, :], AX.X, ALU.max).then_inc(s_max, 1)
                at = slice(NT * h, NT * h + NT)
                best = c.neg[:, h, :]
                dve.wait_ge(s_max, NT * (h + 1))
                dve.tensor_scalar(shift_hi[:, at], best, -1.0, None, ALU.mult).then_inc(s_hi, 1)
                dve.wait_ge(s_hi, h + 1)
                dve.tensor_copy(parts[:, at, 0], f32(shift_hi[:, at])).then_inc(s_parts, 1)
                dve.scalar_tensor_tensor(out=parts[:, at, 1], in0=best, scalar=-1.0, in1=f32(shift_hi[:, at]),
                                         op0=ALU.mult, op1=ALU.subtract).then_inc(s_parts, 1)
                if h % HG == 2 and h // HG >= 2:
                    normalise(h // HG - 2)
            for g in (G - 2, G - 1):
                normalise(g)
            dve.wait_ge(s_out, G)


def sparse_mix(nc, c):
    with ExitStack() as stack:
        sb, pb, sem = allocators(nc, stack, "mix")
        wv = c.raw1[:, 0:H * TOPM // FF, :].rearrange("p k (h m) -> p (k h) m", m=TOPM)
        wo = c.raw2[:, 0:HD * TOPM // D, :].rearrange("p k (d m) -> p (k d) m", m=TOPM)
        vm = sb("vm", [P, H])
        om = sb("om", [P, HD])
        bv = sb("bv", [P, HG * H])
        bo = sb("bo", [P, HG, HD])
        flat = sb("flat", [P, G, N])
        z = sb("z", [P, 2, N])
        left = sb("left", [P, 2, N])
        top = sb("top", [P, 2, 8])
        zs = sb("zs", [P, 2, N])
        zp = [pb(f"zp{i}", [P, N]) for i in range(2)]
        yp = [pb(f"yp{g}", [P, N]) for g in range(G)]
        w_in, s_zero, s_vm, s_om, s_bv, s_bo, s_zp, s_z, s_zs, s_y, s_yT = (
            sem(n) for n in ("w_in", "zero", "vm", "om", "bv", "bo", "zp", "z", "zs", "y", "yT"))
        s_top, s_left, s_flat_act, s_flat_dve = sem("top"), sem("left"), sem("flat_act"), sem("flat_dve")
        block = stack.enter_context(nc.Block())

        def regroup(j, i):
            rows_per_block = N // H
            dst = flat[HD * i:HD * i + HD, :, :].rearrange("d b (t g j) -> d b t g j", g=G, j=HG)[:, :, :, :, j]
            src = c.aoT[HD * j:HD * j + HD, :, :].rearrange("d g (b i t) -> d b i t g", i=HG, t=rows_per_block)[:, :, i, :, :]
            return dst, src

        @block.sync
        def _(sp):
            for j in range(HG):
                sp.dma_start(wv[HD * j:HD * j + HD, :, :], c.dram["spVT"]).then_inc(w_in, 16)
            for j in range(2 * HG):
                sp.dma_start(wo[H * j:H * j + H, :, :], c.dram["spOT"]).then_inc(w_in, 16)
            sp.wait_ge(s_vm, 1)
            sp.wait_ge(s_om, 1)

        @block.gpsimd
        def _(pool):
            pool.memset(bv[:, :], 0.0).then_inc(s_zero, 1)
            pool.wait_ge(s_om, 2)
            for half in range(2):
                rows = slice(64 * half, 64 * half + 64)
                pool.tensor_copy(bo[rows, :, :], om[rows, :].unsqueeze(1).broadcast_to([64, HG, HD])).then_inc(s_bo, 1)
                pool.wait_ge(s_bo, 3 * half + 1)
                pool.affine_select(out=bo[rows, :, :], in_=bo[rows, :, :], compare_op=ALU.is_ge, fill=0.0, base=0,
                                   pattern=[[-H, HG], [0, HD]], channel_multiplier=1).then_inc(s_bo, 1)
                pool.wait_ge(s_bo, 3 * half + 2)
                pool.affine_select(out=bo[rows, :, :], in_=bo[rows, :, :], compare_op=ALU.is_ge, fill=0.0, base=H - 1,
                                   pattern=[[H, HG], [0, HD]], channel_multiplier=-1).then_inc(s_bo, 1)
            pool.wait_ge(s_bo, 6)

        @block.vector
        def _(dve):
            dve.wait_ge(w_in, 16 * 3 * HG)
            dve.tensor_reduce(vm[:, :], wv[:, :, :], AX.X, ALU.add).then_inc(s_vm, 1)
            dve.tensor_reduce(om[:, :], wo[:, :, :], AX.X, ALU.add).then_inc(s_om, 1)
            dve.wait_ge(s_om, 1)
            dve.tensor_scalar(om[:, :], om[:, :], 1.0 / TOPM, None, ALU.mult).then_inc(s_om, 1)
            dve.wait_ge(s_vm, 1)
            dve.wait_ge(s_zero, 1)
            for j in range(HG):
                rows = slice(HD * j, HD * j + HD)
                dve.tensor_scalar(bv[rows, H * j:H * j + H], vm[rows, :], 1.0 / TOPM, None, ALU.mult).then_inc(s_bv, 1)
            for j in range(HG // 2, HG):
                for i in range(HG):
                    dve.tensor_copy(*regroup(j, i)).then_inc(s_flat_dve, 1)
            for i in range(2):
                dve.wait_ge(s_zp, i + 1)
                dve.tensor_copy(z[:, i, :], zp[i][:, :]).then_inc(s_z, 1)
            for i in range(2):
                dve.wait_ge(s_z, i + 1)
            for r in range(KEEP // 8):
                for i in range(2):
                    rest = z if r == 0 else left
                    if r:
                        dve.wait_ge(s_left, 2 * (r - 1) + i + 1)
                    dve.max(out=top[:, i, :], in_=rest[:, i, :]).then_inc(s_top, 1)
                for i in range(2):
                    rest = z if r == 0 else left
                    dve.wait_ge(s_top, 2 * r + i + 1)
                    dve.match_replace(out=left[:, i, :], in_to_replace=top[:, i, :], in_values=rest[:, i, :],
                                      imm_value=NEG).then_inc(s_left, 1)
            for i in range(2):
                dve.wait_ge(s_left, 2 * (KEEP // 8 - 1) + i + 1)
                dve.scalar_tensor_tensor(out=zs[:, i, :], in0=left[:, i, :], scalar=NEG, in1=z[:, i, :],
                                         op0=ALU.is_equal, op1=ALU.mult).then_inc(s_zs, 1)

        @block.tensor
        def _(pe):
            pe.wait_ge(s_bv, HG)
            pe.wait_ge(s_flat_act, HG * HG // 2)
            pe.wait_ge(s_flat_dve, HG * HG // 2)
            for g in range(G):
                mm = pe.matmul(zp[g // 2][64 * (g % 2):64 * (g % 2) + 64, :], bv[:, :], flat[:, g, :], start=True, stop=True)
                if g % 2:
                    mm.then_inc(s_zp, 1)
            pe.wait_ge(s_bo, 6)
            for g in range(G):
                pe.wait_ge(s_zs, g // 2 + 1)
                rows = slice(64 * (g % 2), 64 * (g % 2) + 64)
                pe.matmul(yp[g][:, :], bo[rows, :, :].rearrange("p j d -> p (j d)"), zs[rows, g // 2, :],
                          start=True, stop=True).then_inc(s_y, 1)

        @block.scalar
        def _(act):
            for j in range(HG // 2):
                for i in range(HG):
                    dst, src = regroup(j, i)
                    act.activation(dst, src, ACT.Copy).then_inc(s_flat_act, 1)

        first_expert(nc, c, block)

        @block.scalar
        def _(act):
            for g in range(G):
                act.wait_ge(s_y, g + 1)
                act.activation(c.yT[:, g, :], yp[g][:, :], ACT.Copy).then_inc(s_yT, 1)
            act.wait_ge(s_yT, G)


def route(nc, c):
    with ExitStack() as stack:
        sb, pb, sem = allocators(nc, stack, "rt")
        wg = sb("wg", [P, DC, E])
        b2 = sb("b2", [E, D])
        iota = sb("iota", [P, E])
        big = sb("big", [P, NT])
        ex = sb("ex", [P, NT, E])
        su = sb("su", [P, NT])
        ri = sb("ri", [P, NT])
        prob = sb("prob", [P, NT, E])
        top = sb("top", [P, NT, 8])
        idx = sb("idx", [P, NT, 8], U32)
        idf = sb("idf", [P, NT, 8])
        m1 = sb("m1", [P, NT, E])
        m2 = sb("m2", [P, NT, E])
        two = sb("two", [P, NT])
        rt = sb("rt", [P, NT])
        scT = sb("scT", [E, N])
        lg = pb("lg", [P, NT, E])
        tp = pb("tp", [P, N])
        ac = [pb(f"ac{t}", [P, D]) for t in range(NT)]
        w_in, s_lg, s_step, s_exp, s_iota, s_score, s_tp, s_scT, s_ac, s_hi = (
            sem(n) for n in ("w_in", "lg", "step", "exp", "iota", "score", "tp", "scT", "ac", "hi"))
        s_sub = sem("sub")
        block = stack.enter_context(nc.Block())

        @block.sync
        def _(sp):
            sp.dma_start(wg[:, :, :], c.dram["Wg"].rearrange("(k p) e -> p k e", p=P)).then_inc(w_in, 16)
            sp.dma_start(b2[:, :], c.dram["b2"]).then_inc(w_in, 16)
            sp.dma_start(c.b1[:, :, :], c.dram["b1"]).then_inc(w_in, 16)
            sp.wait_ge(w_in, 48)

        @block.gpsimd
        def _(pool):
            pool.iota(iota[:, :], pattern=[[1, E]], base=0, channel_multiplier=0,
                      allow_small_or_imprecise_dtypes=True).then_inc(s_iota, 1)

        @block.tensor
        def _(pe):
            pe.wait_ge(w_in, 48)
            for t in range(NT):
                for k in range(DC):
                    mm = pe.matmul(lg[:, t, :], c.hT[:, k, t * P:(t + 1) * P], wg[:, k, :], start=(k == 0), stop=(k == DC - 1))
            mm.then_inc(s_lg, 1)
            pe.wait_ge(s_score, 1)
            for t in range(NT):
                mm = pe.transpose(tp[0:E, t * P:(t + 1) * P], c.score[:, t, :], c.ident[:, :])
            mm.then_inc(s_tp, 1)
            pe.wait_ge(s_scT, 1)
            for t in range(NT):
                pe.matmul(ac[t][:, :], scT[:, t * P:(t + 1) * P], b2[:, :], start=True, stop=True).then_inc(s_ac, 1)

        @block.scalar
        def _(act):
            act.activation(c.hT_hi[:, :, :], c.hT[:, :, :], ACT.Copy).then_inc(s_hi, 1)
            act.wait_ge(s_sub, 1)
            act.activation(ex[:, :, :], ex[:, :, :], ACT.Exp).then_inc(s_exp, 1)
            act.wait_ge(s_tp, 1)
            act.activation(scT[:, :], tp[0:E, :], ACT.Copy).then_inc(s_scT, 1)

        @block.vector
        def _(dve):
            steps = 0

            def step(instruction):
                nonlocal steps
                steps += 1
                instruction.then_inc(s_step, 1)
                dve.wait_ge(s_step, steps)

            def wide(ap, n=E):
                return ap.unsqueeze(2).broadcast_to([P, NT, n])

            dve.wait_ge(s_hi, 1)
            step(dve.tensor_tensor(c.hT_lo[:, :, :], c.hT[:, :, :], f32(c.hT_hi[:, :, :]), ALU.subtract))
            dve.wait_ge(s_lg, 1)
            step(dve.tensor_reduce(big[:, :], lg[:, :, :], AX.X, ALU.max))
            dve.tensor_tensor(ex[:, :, :], lg[:, :, :], wide(big[:, :]), ALU.subtract).then_inc(s_sub, 1)
            dve.wait_ge(s_exp, 1)
            step(dve.tensor_reduce(su[:, :], ex[:, :, :], AX.X, ALU.add))
            step(dve.reciprocal(ri[:, :], su[:, :]))
            step(dve.tensor_tensor(prob[:, :, :], ex[:, :, :], wide(ri[:, :]), ALU.mult))
            for t in range(NT):
                step(dve.max(out=top[:, t, :], in_=prob[:, t, :]))
                step(dve.max_index(out=idx[:, t, :], in_max=top[:, t, :], in_values=prob[:, t, :]))
            step(dve.tensor_copy(idf[:, :, :], idx[:, :, :]))
            dve.wait_ge(s_iota, 1)
            number = iota[:, :].unsqueeze(1).broadcast_to([P, NT, E])
            step(dve.tensor_tensor(m1[:, :, :], number, wide(idf[:, :, 0]), ALU.is_equal))
            step(dve.tensor_tensor(m2[:, :, :], number, wide(idf[:, :, 1]), ALU.is_equal))
            step(dve.tensor_tensor(m1[:, :, :], m1[:, :, :], m2[:, :, :], ALU.add))
            step(dve.tensor_tensor(two[:, :], top[:, :, 0], top[:, :, 1], ALU.add))
            step(dve.reciprocal(rt[:, :], two[:, :]))
            step(dve.tensor_tensor(m2[:, :, :], prob[:, :, :], m1[:, :, :], ALU.mult))
            dve.tensor_tensor(c.score[:, :, :], m2[:, :, :], wide(rt[:, :]), ALU.mult).then_inc(s_score, 1)
            for t in range(NT):
                dve.wait_ge(s_ac, t + 1)
                step(dve.tensor_tensor(c.x[:, t, :], ac[t][:, :], c.x[:, t, :], ALU.add))


def first_expert(nc, c, block):
    @block.sync
    def _(sp):
        sp.dma_start(c.raw1[:, :, :], c.dram["W1"][0].rearrange("(k p) f -> p k f", p=P)).then_inc(c.in1, 16)
        sp.dma_start(c.raw2[:, :, :], c.dram["W2"][0].rearrange("(k p) d -> p k d", p=P)).then_inc(c.in2, 16)

    @block.scalar
    def _(act):
        act.wait_ge(c.in1, 16)
        act.activation(c.w1_hi[:, :, :], c.raw1[:, :, :], ACT.Copy).then_inc(c.s_hi1, 1)
        act.wait_ge(c.in2, 16)
        act.activation(c.w2_hi[:, :, :], c.raw2[:, :, :], ACT.Copy).then_inc(c.s_hi2, 1)

    @block.gpsimd
    def _(pool):
        pool.wait_ge(c.s_hi1, 1)
        pool.tensor_tensor(c.w1_lo[:, :, :], c.raw1[:, :, :], f32(c.w1_hi[:, :, :]), ALU.subtract).then_inc(c.s_lo1, 1)
        pool.wait_ge(c.s_hi2, 1)
        pool.tensor_tensor(c.w2_lo[:, :, :], c.raw2[:, :, :], f32(c.w2_hi[:, :, :]), ALU.subtract).then_inc(c.s_lo2, 1)


def experts(nc, c):
    PRIME = 8
    HALF = 4
    with ExitStack() as stack:
        sb, pb, sem = allocators(nc, stack, "ex")
        raw1, raw2, w1_hi, w1_lo, w2_hi, w2_lo = c.raw1, c.raw2, c.w1_hi, c.w1_lo, c.w2_hi, c.w2_lo
        in1, in2, s_hi1, s_lo1, s_hi2, s_lo2 = c.in1, c.in2, c.s_hi1, c.s_lo1, c.s_hi2, c.s_lo2
        hid = sb("hid", [P, 2, N])
        hid_hi, hid_lo = c.stacks[:, 0:FC, :], c.stacks[:, FC:2 * FC, :]
        hp = [pb(f"hp{i}", [P, N]) for i in range(HALF)]
        yp = [pb(f"yp{t}", [P, D]) for t in range(NT)]
        s_hp, s_hid, s_hh, s_hl, s_yp, s_acc = (sem(n) for n in ("hp", "hid", "hh", "hl", "yp", "acc"))
        s_done = sem("done")
        block = stack.enter_context(nc.Block())

        @block.sync
        def _(sp):
            with sp.Fori(1, E) as e:
                sp.wait_ge(s_lo1, e)
                sp.dma_start(raw1[:, :, :], c.dram["W1"][e].rearrange("(k p) f -> p k f", p=P)).then_inc(in1, 16)
                sp.wait_ge(s_lo2, e)
                sp.dma_start(raw2[:, :, :], c.dram["W2"][e].rearrange("(k p) d -> p k d", p=P)).then_inc(in2, 16)
            sp.wait_ge(s_acc, NT * E + PRIME)
            sp.dma_start(c.dram["out"].rearrange("(t p) d -> p t d", p=P), c.x[:, :, :]).then_inc(s_done, 16)
            sp.wait_ge(s_done, 16)

        @block.gpsimd
        def _(pool):
            with pool.Fori(1, E) as e:
                pool.wait_ge(s_hi1, e + 1)
                pool.tensor_tensor(w1_lo[:, :, :], raw1[:, :, :], f32(w1_hi[:, :, :]), ALU.subtract).then_inc(s_lo1, 1)
                pool.wait_ge(s_hi2, e + 1)
                pool.tensor_tensor(w2_lo[:, :, :], raw2[:, :, :], f32(w2_hi[:, :, :]), ALU.subtract).then_inc(s_lo2, 1)

        @block.tensor
        def _(pe):
            pe.sem_inc(s_hp, PRIME)
            pe.sem_inc(s_yp, PRIME)
            with pe.Fori(0, E) as e:
                pe.wait_ge(s_lo1, e + 1)
                for f in range(FC):
                    pe.wait_ge(s_hid, FC * e + f - HALF + 1 + PRIME)
                    split_product(pe, hp[f % HALF][:, :],
                                  [(w1_hi[:, k, f * P:(f + 1) * P], w1_lo[:, k, f * P:(f + 1) * P]) for k in range(DC)],
                                  [(c.hT_hi[:, k, :], c.hT_lo[:, k, :]) for k in range(DC)]).then_inc(s_hp, 1)
                pe.wait_ge(s_lo2, e + 1)
                pe.wait_ge(s_hl, FC * e + FC + PRIME)
                for t in range(NT):
                    pe.wait_ge(s_acc, NT * (e - 1) + t + 1 + PRIME)
                    split_product(pe, yp[t][:, :],
                                  [(hid_hi[:, f, t * P:(t + 1) * P], hid_lo[:, f, t * P:(t + 1) * P]) for f in range(FC)],
                                  [(w2_hi[:, f, :], w2_lo[:, f, :]) for f in range(FC)]).then_inc(s_yp, 1)

        @block.scalar
        def _(act):
            act.sem_inc(s_hid, PRIME)

            def hidden(e, b1):
                for f in range(FC):
                    act.wait_ge(s_hp, FC * e + f + 1 + PRIME)
                    act.wait_ge(s_hl, FC * e + f - 2 + 1 + PRIME)
                    act.activation(hid[:, f % 2, :], hp[f % HALF][:, :], ACT.Relu, bias=b1[:, f, :]).then_inc(s_hid, 1)

            hidden(0, c.b1[:, :, 0:1])
            with act.Fori(1, E) as e:
                act.wait_ge(in1, 16 * e + 16)
                act.wait_ge(s_hp, FC * e + PRIME)
                act.activation(w1_hi[:, :, :], raw1[:, :, :], ACT.Copy).then_inc(s_hi1, 1)
                act.wait_ge(in2, 16 * e + 16)
                act.wait_ge(s_yp, NT * e + PRIME)
                act.activation(w2_hi[:, :, :], raw2[:, :, :], ACT.Copy).then_inc(s_hi2, 1)
                hidden(e, c.b1[:, :, bass.ds(e, 1)])

        @block.vector
        def _(dve):
            dve.sem_inc(s_hl, PRIME)
            dve.sem_inc(s_acc, PRIME)
            with dve.Fori(0, E) as e:
                dve.wait_ge(s_yp, NT * e + PRIME)
                for f in range(FC):
                    dve.wait_ge(s_hid, FC * e + f + 1 + PRIME)
                    dve.tensor_copy(hid_hi[:, f, :], hid[:, f % 2, :]).then_inc(s_hh, 1)
                    dve.wait_ge(s_hh, FC * e + f + 1)
                    dve.tensor_tensor(hid_lo[:, f, :], hid[:, f % 2, :], f32(hid_hi[:, f, :]), ALU.subtract).then_inc(s_hl, 1)
                for t in range(NT):
                    dve.wait_ge(s_yp, NT * e + t + 1 + PRIME)
                    dve.wait_ge(s_acc, NT * (e - 1) + t + 1 + PRIME)
                    dve.scalar_tensor_tensor(out=c.x[:, t, :], in0=yp[t][:, :], scalar=c.score[:, t, bass.ds(e, 1)],
                                             in1=c.x[:, t, :], op0=ALU.mult, op1=ALU.add).then_inc(s_acc, 1)


def perceiver_layer(nc, dram):
    c = Ctx()
    c.dram = dram
    c.k_dram = nc.dram_tensor("keys_scratch", [NCH, G, 2, P, CH], F32).ap()
    c.v_dram = nc.dram_tensor("values_scratch", [NCH, G, P, KT, P], F32).ap()
    with ExitStack() as whole:
        sb, pb, sem = allocators(nc, whole, "g")
        c.ident = sb("ident", [P, P])
        c.ones = sb("ones", [P, HD])
        c.one_row = sb("one_row", [1, P])
        c.x = sb("x", [P, NT, D])
        c.hT = sb("hT", [P, DC, N])
        c.bq, c.bk, c.bv = sb("bq", [P, DC]), sb("bk", [P, DC]), sb("bv", [P, DC])
        c.bo = sb("bo", [1, D])
        c.neg = sb("neg", [P, H, NT])
        c.stacks = sb("stacks", [P, H, N], F32R)
        with ExitStack() as first:
            sb, pb, sem = allocators(nc, first, "f")
            c.q_hi, c.q_lo = sb("q_hi", [P, G, N], F32R), c.hT
            c.wk_hi, c.wk_lo = sb("wk_hi", [P, DC, D], F32R), sb("wk_lo", [P, DC, D], F32R)
            c.wv_hi, c.wv_lo = sb("wv_hi", [P, DC, D], F32R), sb("wv_lo", [P, DC, D], F32R)
            c.raw = sb("raw", [P, DC, CH])
            c.hi = [sb(f"hi{b}", [P, DC, CH], F32R) for b in range(2)]
            c.lo = [sb(f"lo{b}", [P, DC, CH], F32R) for b in range(2)]
            c.k_hi = [sb(f"k_hi{b}", [P, G, CH], F32R) for b in range(2)]
            c.k_lo = sb("k_lo", [P, G, CH], F32R)
            c.proj = [pb(f"proj{i}", [P, CH]) for i in range(KT)]
            c.ctx_in, c.s_hi, c.s_lo, c.k_proj, c.k_hi_done, c.k_lo_done = (
                sem(n) for n in ("ctx_in", "hi", "lo", "k_proj", "k_hi_done", "k_lo_done"))
            prepare(nc, c)
            project_context(nc, c)
        with ExitStack() as own:
            sb, pb, sem = allocators(nc, own, "o")
            c.swoT = sb("swoT", [P, DC, D])
            c.aoT = sb("aoT", [P, G, N])
            c.yT = sb("yT", [P, G, N])
            c.wo_in, c.sq_in, c.sk_in, c.sv_in, c.so_in, c.aff_in = (
                sem(n) for n in ("wo_in", "sq_in", "sk_in", "sv_in", "so_in", "aff_in"))
            with ExitStack() as attention:
                sb, pb, sem = allocators(nc, attention, "a")
                c.swqT, c.swkT, c.swvT = (sb(n, [P, DC, D]) for n in ("swqT", "swkT", "swvT"))
                c.aff = sb("aff", [P, 4])
                c.woT = sb("woT", [P, DC, D])
                attend_context(nc, c)
                add_and_normalise(nc, c, "xo", c.aoT, c.woT, c.wo_in, c.hT, bias=c.bo[:, :])
                c.skst = sb("skst", [STK + 2, H, N], F32R)
                c.sval = sb("sval", [P, NT, D])
                self_projections(nc, c)
                self_attend(nc, c)
            with ExitStack() as ffn:
                sb, pb, sem = allocators(nc, ffn, "m")
                c.raw1, c.raw2 = sb("raw1", [P, DC, FF]), sb("raw2", [P, FC, D])
                c.w1_hi, c.w1_lo = sb("w1_hi", [P, DC, FF], F32R), sb("w1_lo", [P, DC, FF], F32R)
                c.w2_hi, c.w2_lo = sb("w2_hi", [P, FC, D], F32R), sb("w2_lo", [P, FC, D], F32R)
                c.in1, c.in2, c.s_hi1, c.s_lo1, c.s_hi2, c.s_lo2 = (
                    sem(n) for n in ("in1", "in2", "hi1", "lo1", "hi2", "lo2"))
                sparse_mix(nc, c)
                add_and_normalise(nc, c, "so", c.yT, c.swoT, c.so_in, c.hT)
                c.hT_hi, c.hT_lo = sb("hT_hi", [P, DC, N], F32R), sb("hT_lo", [P, DC, N], F32R)
                c.score = sb("score", [P, NT, E])
                c.b1 = sb("b1", [P, FC, E])
                route(nc, c)
                experts(nc, c)


def kernel(**inputs):
    import numpy as _np
    import concourse.bacc as _bacc
    from concourse import mybir as _mybir
    from concourse.bass_utils import run_bass_kernel_spmd as _run

    a = {k: _np.asarray(v) for k, v in inputs.items()}
    keep = _np.ascontiguousarray
    column = lambda b: keep(b.reshape(DC, P).T)
    arrays = {
        "x": keep(a["x"][0]),
        "ctx": keep(a["ctx_1024"][0].reshape(NCH, CH, DC, P).transpose(0, 3, 2, 1)),
        "WqT": keep(a["L0_xattn_Wq"].T), "WkT": keep(a["L0_xattn_Wk"].T),
        "WvT": keep(a["L0_xattn_Wv"].T), "WoT": keep(a["L0_xattn_Wo"].T),
        "bq": column(a["L0_xattn_bq"]), "bk": column(a["L0_xattn_bk"]), "bv": column(a["L0_xattn_bv"]),
        "bo": keep(a["L0_xattn_bo"].reshape(1, D)),
        "sWqT": keep(a["L0_attn_W_Q"].T), "sWkT": keep(a["L0_attn_W_K"].T),
        "sWvT": keep(a["L0_attn_W_V"].T), "sWoT": keep(a["L0_attn_W_O"].T),
        "affine": keep(_np.stack([a["L0_attn_q_ln_w"], a["L0_attn_q_ln_b"], a["L0_attn_k_ln_w"], a["L0_attn_k_ln_b"]], 1)),
        "spVT": keep(a["L0_attn_sparse_W_V"].transpose(1, 0, 2)),
        "spOT": keep(a["L0_attn_sparse_W_O"].transpose(0, 2, 1)),
        "Wg": keep(a["L0_ffn_Wg"]), "W1": keep(a["L0_ffn_W1"]), "W2": keep(a["L0_ffn_W2"]),
        "b1": keep(a["L0_ffn_b1"].reshape(E, FC, P).transpose(2, 1, 0)), "b2": keep(a["L0_ffn_b2"]),
    }
    nc = _bacc.Bacc("TRN2", target_bir_lowering=False, num_devices=1)
    dram = {n: nc.dram_tensor(f"in_{n}", v.shape, _mybir.dt.from_np(v.dtype), kind="ExternalInput").ap()
            for n, v in arrays.items()}
    dram["out"] = nc.dram_tensor("out_0", (N, D), F32, kind="ExternalOutput").ap()
    perceiver_layer(nc, dram)
    r = _run(nc, [{f"in_{n}": v for n, v in arrays.items()}], core_ids=[0])
    return r.results[0]["out_0"].reshape(1, N, D)
```
